# Optimizing a Trainium2 kernel written in Bass

```python
import numpy as np
import jax
import jax.numpy as jnp

def _softmax(x, axis=-1):
    return jax.nn.softmax(x, axis=axis)

def _gelu(x):
    return jax.nn.gelu(x, approximate=True)

def _silu(x):
    return jax.nn.silu(x)

def _sigmoid(x):
    return jax.nn.sigmoid(x)

def _layernorm(x, axis=-1, eps=1e-05):
    m = jnp.mean(x, axis=axis, keepdims=True)
    v = jnp.var(x, axis=axis, keepdims=True)
    return (x - m) / jnp.sqrt(v + eps)

def _scatter_add(tgt, idx, src, axis=0):
    return tgt.at[idx].add(src)

def _segment_sum(src, seg, n):
    return jax.ops.segment_sum(src, seg, n)
kernel_name = 'mk_adj_ffn_d4_adj_r2_1c8ece'

def setup_inputs(seed: int=0):
    np.random.seed(seed)
    _w = jnp.asarray

    def _rec_inputs():
        import jax
        import jax.numpy as jnp
        _gk = jax.random.key(seed)
        x = -0.0005146 + 1 * jax.random.normal(jax.random.fold_in(_gk, 1), (8, 1024, 128), jnp.float32)
        _w = (1.0 + jnp.arange(1024, dtype=jnp.float32)) ** (-0.5)
        _w = _w / _w.mean()
        _pij = jnp.clip(0.0078125 * _w[:, None] * _w[None, :], 0.0, 1.0)
        _a = jax.random.uniform(jax.random.fold_in(_gk, 2), (8, 1024, 1024)) < _pij
        adj = _a.astype(jnp.int32)
        return (x, adj)
    x, adj = _rec_inputs()

    def _L0_gnn_setup():
        import jax, jax.numpy as jnp
        import numpy as np
        B, N, C, OUT, S = (4, 1024, 128, 128, 25)
        DENSITY = 0.008
        key = jax.random.key(seed)
        kA, kX, kW = jax.random.split(key, 3)
        A = jax.random.bernoulli(kA, DENSITY, (B, N, N)).astype(jnp.int32)
        X = jax.random.normal(kX, (B, N, C), dtype=jnp.float32)
        W = jax.random.normal(kW, (2 * C, OUT), dtype=jnp.float32) * np.float32(1.0 / np.sqrt(2 * C))
        b = jnp.zeros((OUT,), dtype=jnp.float32)
        return {'A': A, 'X': X, 'W': W, 'b': b}
    _L0_gnn_all = _L0_gnn_setup()
    _L0_gnn_in = {k: v for k, v in _L0_gnn_all.items() if k in ('W', 'b')}
    del _L0_gnn_all

    def _L0_ffn_setup():
        import jax, jax.numpy as jnp
        import numpy as np
        B, A = (2048, 8)
        IN, OUT = (128, 128)
        SH1, SH2 = (128, 128)
        EH1, EH2 = (128, 64)
        E, TOPK = (4, 2)

        def _shared_mlp(x, W1, b1, W2, b2, W3, b3):
            h = jax.nn.relu(x @ W1 + b1)
            h = jax.nn.relu(h @ W2 + b2)
            return h @ W3 + b3

        def _experts_mlp(x, eW1, eb1, eW2, eb2, eW3, eb3):
            h = jax.nn.relu(jnp.einsum('baf,efh->ebah', x, eW1) + eb1[:, None, None, :])
            h = jax.nn.relu(jnp.einsum('ebah,ehg->ebag', h, eW2) + eb2[:, None, None, :])
            o = jnp.einsum('ebag,ego->ebao', h, eW3) + eb3[:, None, None, :]
            return jnp.moveaxis(o, 0, -1)
        key = jax.random.key(seed)
        ks = jax.random.split(key, 16)
        s = 0.05
        return {'x': jax.random.normal(ks[0], (B, A, IN), jnp.float32), 'sW1': jax.random.normal(ks[1], (IN, SH1), jnp.float32) * s, 'sb1': jnp.zeros((SH1,), jnp.float32), 'sW2': jax.random.normal(ks[2], (SH1, SH2), jnp.float32) * s, 'sb2': jnp.zeros((SH2,), jnp.float32), 'sW3': jax.random.normal(ks[3], (SH2, OUT), jnp.float32) * s, 'sb3': jnp.zeros((OUT,), jnp.float32), 'eW1': jax.random.normal(ks[4], (E, IN, EH1), jnp.float32) * s, 'eb1': jnp.zeros((E, EH1), jnp.float32), 'eW2': jax.random.normal(ks[5], (E, EH1, EH2), jnp.float32) * s, 'eb2': jnp.zeros((E, EH2), jnp.float32), 'eW3': jax.random.normal(ks[6], (E, EH2, OUT), jnp.float32) * s, 'eb3': jnp.zeros((E, OUT), jnp.float32), 'gW': jax.random.normal(ks[7], (IN, E), jnp.float32) * s, 'gb': jnp.zeros((E,), jnp.float32)}
    _L0_ffn_all = _L0_ffn_setup()
    _L0_ffn_in = {k: v for k, v in _L0_ffn_all.items() if k in ('sW1', 'sb1', 'sW2', 'sb2', 'sW3', 'sb3', 'eW1', 'eb1', 'eW2', 'eb2', 'eW3', 'eb3', 'gW', 'gb')}
    del _L0_ffn_all

    def _L1_gnn_setup():
        import jax, jax.numpy as jnp
        import numpy as np
        key = jax.random.key(seed)
        k1, k2, k3, k4 = jax.random.split(key, 4)
        B, N, F, U = (8, 1024, 128, 128)
        x = jax.random.normal(k1, (B, N, F), dtype=jnp.float32)
        adj = jax.random.randint(k2, (B, N, N), 0, 2, dtype=jnp.int32)
        W_msg = jax.random.normal(k3, (F, U), dtype=jnp.float32) / np.sqrt(F)
        W_upd = jax.random.normal(k4, (F, U), dtype=jnp.float32) / np.sqrt(F)
        bias = jnp.zeros((U,), dtype=jnp.float32)
        return {'x': x, 'adj': adj, 'W_msg': W_msg, 'W_upd': W_upd, 'bias': bias}
    _L1_gnn_all = _L1_gnn_setup()
    _L1_gnn_in = {k: v for k, v in _L1_gnn_all.items() if k in ('W_msg', 'W_upd', 'bias')}
    del _L1_gnn_all

    def _L1_ffn_setup():
        import jax, jax.numpy as jnp
        import numpy as np
        D_MODEL = 128
        D_STATE = 64
        D_CONV = 4
        EXPAND = 2
        HEADDIM = 64
        D_INNER = EXPAND * D_MODEL
        NHEADS = D_INNER // HEADDIM
        CONV_DIM = D_INNER + 2 * D_STATE
        D_IN_PROJ = 2 * D_INNER + 2 * D_STATE + NHEADS
        CHUNK = 128
        EPS = 1e-05

        def segsum(a):
            T = a.shape[-1]
            cs = jnp.cumsum(a, axis=-1)
            ss = cs[..., :, None] - cs[..., None, :]
            mask = jnp.tril(jnp.ones((T, T), dtype=bool))
            return jnp.where(mask, ss, -jnp.inf)

        def mamba2_block(x, W_in, conv_w, conv_b, dt_bias, A_log, D, norm_w, W_out, W_lin, b_lin):
            Bsz, L, _ = x.shape
            zxbcdt = x @ W_in
            z, xBC, dt = jnp.split(zxbcdt, [D_INNER, D_INNER + CONV_DIM], axis=-1)
            xp = jnp.pad(xBC, ((0, 0), (D_CONV - 1, 0), (0, 0)))
            conv = conv_b + sum((xp[:, k:k + L, :] * conv_w[:, k] for k in range(D_CONV)))
            xBC = jax.nn.silu(conv)
            xh, Bmat, Cmat = jnp.split(xBC, [D_INNER, D_INNER + D_STATE], axis=-1)
            dt = jax.nn.softplus(dt + dt_bias)
            A = -jnp.exp(A_log)
            nc = L // CHUNK
            xh = xh.reshape(Bsz, nc, CHUNK, NHEADS, HEADDIM)
            Bc = Bmat.reshape(Bsz, nc, CHUNK, D_STATE)
            Cc = Cmat.reshape(Bsz, nc, CHUNK, D_STATE)
            dtc = dt.reshape(Bsz, nc, CHUNK, NHEADS)
            dA = jnp.einsum('bclh,h->bhcl', dtc, A)
            A_cum = jnp.cumsum(dA, axis=-1)
            Lmat = jnp.exp(segsum(dA))
            xdt = xh * dtc[..., None]
            Y_diag = jnp.einsum('bcln,bcsn,bhcls,bcshp->bclhp', Cc, Bc, Lmat, xdt)
            decay_states = jnp.exp(A_cum[..., -1:] - A_cum)
            states = jnp.einsum('bcln,bhcl,bclhp->bchpn', Bc, decay_states, xdt)
            chunk_decay = jnp.exp(A_cum[..., -1])

            def step(h, inp):
                s, d = inp
                return (h * d[..., None, None] + s, h)
            _, prevs = jax.lax.scan(step, jnp.zeros_like(states[:, 0]), (jnp.moveaxis(states, 1, 0), jnp.moveaxis(chunk_decay, 2, 0)))
            prevs = jnp.moveaxis(prevs, 0, 1)
            Y_off = jnp.einsum('bcln,bchpn,bhcl->bclhp', Cc, prevs, jnp.exp(A_cum))
            Y = (Y_diag + Y_off + xh * D[:, None]).reshape(Bsz, L, D_INNER)
            Y = Y * jax.nn.silu(z)
            Y = Y * jax.lax.rsqrt(jnp.mean(Y * Y, axis=-1, keepdims=True) + EPS) * norm_w
            out = Y @ W_out
            return out @ W_lin + b_lin
        key = jax.random.key(seed)
        ks = jax.random.split(key, 12)
        B, L = (8, 2048)

        def gauss(k, shape, scale):
            return jax.random.normal(k, shape, dtype=jnp.float32) * scale
        return {'x': gauss(ks[0], (B, L, D_MODEL), 1.0), 'W_in': gauss(ks[1], (D_MODEL, D_IN_PROJ), D_MODEL ** (-0.5)), 'conv_w': gauss(ks[2], (CONV_DIM, D_CONV), 0.3), 'conv_b': gauss(ks[3], (CONV_DIM,), 0.1), 'dt_bias': jax.random.uniform(ks[4], (NHEADS,), minval=-4.0, maxval=-1.0), 'A_log': jnp.log(jax.random.uniform(ks[5], (NHEADS,), minval=1.0, maxval=16.0)), 'D': jnp.ones((NHEADS,), jnp.float32), 'norm_w': jnp.ones((D_INNER,), jnp.float32), 'W_out': gauss(ks[6], (D_INNER, D_MODEL), D_INNER ** (-0.5)), 'W_lin': gauss(ks[7], (D_MODEL, D_MODEL), D_MODEL ** (-0.5)), 'b_lin': jnp.zeros((D_MODEL,), jnp.float32)}
    _L1_ffn_all = _L1_ffn_setup()
    _L1_ffn_in = {k: v for k, v in _L1_ffn_all.items() if k in ('W_in', 'conv_w', 'conv_b', 'dt_bias', 'A_log', 'D', 'norm_w', 'W_out', 'W_lin', 'b_lin')}
    del _L1_ffn_all

    def _L2_gnn_setup():
        import jax, jax.numpy as jnp
        import numpy as np
        DIM = 128
        HEADS = 4
        B, N = (2, 2048)
        NEG = -1000000000.0
        EPS = 1e-05
        key = jax.random.key(seed)
        ks = jax.random.split(key, 12)
        s = 0.02
        inp = {'x': jax.random.normal(ks[0], (B, N, DIM), dtype=jnp.float32), 'adj': jax.random.randint(ks[1], (B, N, N), 0, 2, dtype=jnp.int32), 'Wq': jax.random.normal(ks[2], (DIM, DIM), dtype=jnp.float32) * s, 'bq': jnp.zeros((DIM,), jnp.float32), 'Wk': jax.random.normal(ks[3], (DIM, DIM), dtype=jnp.float32) * s, 'bk': jnp.zeros((DIM,), jnp.float32), 'Wv': jax.random.normal(ks[4], (DIM, DIM), dtype=jnp.float32) * s, 'bv': jnp.zeros((DIM,), jnp.float32), 'Wo': jax.random.normal(ks[5], (DIM, DIM), dtype=jnp.float32) * s, 'bo': jnp.zeros((DIM,), jnp.float32), 'gamma': jnp.ones((DIM,), jnp.float32), 'beta': jnp.zeros((DIM,), jnp.float32)}
        return inp
    _L2_gnn_all = _L2_gnn_setup()
    _L2_gnn_in = {k: v for k, v in _L2_gnn_all.items() if k in ('Wq', 'bq', 'Wk', 'bk', 'Wv', 'bv', 'Wo', 'bo', 'gamma', 'beta')}
    del _L2_gnn_all

    def _L2_ffn_setup():
        import jax, jax.numpy as jnp
        import numpy as np
        B, T, C = (64, 192, 128)
        NH, NKV = (4, 2)
        HD = C // NH
        NREP = NH // NKV
        NE, TOPK = (8, 2)
        HID = int(8 / 3 * C)
        EPS_RMS = 1e-06

        def _rope_tables(t_len):
            inv_freq = 1.0 / 10000.0 ** (np.arange(0, HD, 2, dtype=np.float32) / HD)
            t = np.arange(t_len, dtype=np.float32)
            freqs = np.outer(t, inv_freq)
            emb = np.concatenate([freqs, freqs], axis=-1)
            return (jnp.asarray(np.cos(emb)), jnp.asarray(np.sin(emb)))

        def _rotate_half(x):
            h = x.shape[-1] // 2
            return jnp.concatenate([-x[..., h:], x[..., :h]], axis=-1)

        def _rmsnorm(v, w):
            return v * jax.lax.rsqrt(jnp.mean(v * v, axis=-1, keepdims=True) + EPS_RMS) * w
        key = jax.random.key(seed)
        ks = jax.random.split(key, 10)
        s = lambda k, shape: jax.random.normal(k, shape, jnp.float32) * 0.02
        return {'x': jax.random.normal(ks[0], (B, T, C), jnp.float32), 'ln1_w': jnp.ones((C,), jnp.float32), 'ln2_w': jnp.ones((C,), jnp.float32), 'wq': s(ks[1], (NH * HD, C)), 'wk': s(ks[2], (NKV * HD, C)), 'wv': s(ks[3], (NKV * HD, C)), 'wo': s(ks[4], (C, C)), 'router_w': s(ks[5], (NE, C)), 'w1': s(ks[6], (NE, HID, C)), 'w2': s(ks[7], (NE, C, HID)), 'w3': s(ks[8], (NE, HID, C))}
    _L2_ffn_all = _L2_ffn_setup()
    _L2_ffn_in = {k: v for k, v in _L2_ffn_all.items() if k in ('ln1_w', 'ln2_w', 'wq', 'wk', 'wv', 'wo', 'router_w', 'w1', 'w2', 'w3')}
    del _L2_ffn_all

    def _L3_gnn_setup():
        import jax, jax.numpy as jnp
        import numpy as np
        B, N, C_IN, H, C_OUT = (8, 512, 128, 4, 128)
        C = C_OUT // H
        ALPHA = 0.2
        NEG_INF = -9000000000000000.0
        key = jax.random.key(seed)
        k1, k2, k3, k4, k5 = jax.random.split(key, 5)
        node_feats = jax.random.normal(k1, (B, N, C_IN), dtype=jnp.float32)
        adj_matrix = jax.random.randint(k2, (B, N, N), 0, 2, dtype=jnp.int32)
        eye = jnp.eye(N, dtype=jnp.int32)[None]
        adj_matrix = jnp.maximum(adj_matrix, eye)

        def xavier(k, shape, fan_in, fan_out, gain=1.414):
            lim = gain * np.sqrt(6.0 / (fan_in + fan_out))
            return jax.random.uniform(k, shape, jnp.float32, -lim, lim)
        W = xavier(k3, (C_OUT, C_IN), C_IN, C_OUT)
        b = jnp.zeros((C_OUT,), dtype=jnp.float32)
        a = xavier(k4, (H, 2 * C), 2 * C, H)
        return {'node_feats': node_feats, 'adj_matrix': adj_matrix, 'W': W, 'b': b, 'a': a}
    _L3_gnn_all = _L3_gnn_setup()
    _L3_gnn_in = {k: v for k, v in _L3_gnn_all.items() if k in ('W', 'b', 'a')}
    del _L3_gnn_all

    def _L3_ffn_setup():
        import jax, jax.numpy as jnp
        import numpy as np
        TOP_K = 2
        LN_EPS = 1e-05
        key = jax.random.key(seed)
        ks = jax.random.split(key, 8)
        B, S, D, E, H = (16, 512, 128, 8, 512)
        x = jax.random.normal(ks[0], (B, S, D), dtype=jnp.float32)
        Wr = jax.random.normal(ks[1], (D, E), dtype=jnp.float32) * 0.1
        br = jnp.zeros((E,), dtype=jnp.float32)
        ln_g = jnp.ones((E, D), dtype=jnp.float32)
        ln_b = jnp.zeros((E, D), dtype=jnp.float32)
        W1 = jax.random.normal(ks[2], (E, D, H), dtype=jnp.float32) * (1.0 / np.sqrt(D))
        b1 = jnp.zeros((E, H), dtype=jnp.float32)
        W2 = jax.random.normal(ks[3], (E, H, D), dtype=jnp.float32) * (1.0 / np.sqrt(H))
        b2 = jnp.zeros((E, D), dtype=jnp.float32)
        return {'x': x, 'Wr': Wr, 'br': br, 'ln_g': ln_g, 'ln_b': ln_b, 'W1': W1, 'b1': b1, 'W2': W2, 'b2': b2}
    _L3_ffn_all = _L3_ffn_setup()
    _L3_ffn_in = {k: v for k, v in _L3_ffn_all.items() if k in ('Wr', 'br', 'ln_g', 'ln_b', 'W1', 'b1', 'W2', 'b2')}
    del _L3_ffn_all
    return {'x': x, 'adj': adj, 'L0_gnn_W': _L0_gnn_in['W'], 'L0_gnn_b': _L0_gnn_in['b'], 'L0_ffn_sW1': _L0_ffn_in['sW1'], 'L0_ffn_sb1': _L0_ffn_in['sb1'], 'L0_ffn_sW2': _L0_ffn_in['sW2'], 'L0_ffn_sb2': _L0_ffn_in['sb2'], 'L0_ffn_sW3': _L0_ffn_in['sW3'], 'L0_ffn_sb3': _L0_ffn_in['sb3'], 'L0_ffn_eW1': _L0_ffn_in['eW1'], 'L0_ffn_eb1': _L0_ffn_in['eb1'], 'L0_ffn_eW2': _L0_ffn_in['eW2'], 'L0_ffn_eb2': _L0_ffn_in['eb2'], 'L0_ffn_eW3': _L0_ffn_in['eW3'], 'L0_ffn_eb3': _L0_ffn_in['eb3'], 'L0_ffn_gW': _L0_ffn_in['gW'], 'L0_ffn_gb': _L0_ffn_in['gb'], 'L1_gnn_W_msg': _L1_gnn_in['W_msg'], 'L1_gnn_W_upd': _L1_gnn_in['W_upd'], 'L1_gnn_bias': _L1_gnn_in['bias'], 'L1_ffn_W_in': _L1_ffn_in['W_in'], 'L1_ffn_conv_w': _L1_ffn_in['conv_w'], 'L1_ffn_conv_b': _L1_ffn_in['conv_b'], 'L1_ffn_dt_bias': _L1_ffn_in['dt_bias'], 'L1_ffn_A_log': _L1_ffn_in['A_log'], 'L1_ffn_D': _L1_ffn_in['D'], 'L1_ffn_norm_w': _L1_ffn_in['norm_w'], 'L1_ffn_W_out': _L1_ffn_in['W_out'], 'L1_ffn_W_lin': _L1_ffn_in['W_lin'], 'L1_ffn_b_lin': _L1_ffn_in['b_lin'], 'L2_gnn_Wq': _L2_gnn_in['Wq'], 'L2_gnn_bq': _L2_gnn_in['bq'], 'L2_gnn_Wk': _L2_gnn_in['Wk'], 'L2_gnn_bk': _L2_gnn_in['bk'], 'L2_gnn_Wv': _L2_gnn_in['Wv'], 'L2_gnn_bv': _L2_gnn_in['bv'], 'L2_gnn_Wo': _L2_gnn_in['Wo'], 'L2_gnn_bo': _L2_gnn_in['bo'], 'L2_gnn_gamma': _L2_gnn_in['gamma'], 'L2_gnn_beta': _L2_gnn_in['beta'], 'L2_ffn_ln1_w': _L2_ffn_in['ln1_w'], 'L2_ffn_ln2_w': _L2_ffn_in['ln2_w'], 'L2_ffn_wq': _L2_ffn_in['wq'], 'L2_ffn_wk': _L2_ffn_in['wk'], 'L2_ffn_wv': _L2_ffn_in['wv'], 'L2_ffn_wo': _L2_ffn_in['wo'], 'L2_ffn_router_w': _L2_ffn_in['router_w'], 'L2_ffn_w1': _L2_ffn_in['w1'], 'L2_ffn_w2': _L2_ffn_in['w2'], 'L2_ffn_w3': _L2_ffn_in['w3'], 'L3_gnn_W': _L3_gnn_in['W'], 'L3_gnn_b': _L3_gnn_in['b'], 'L3_gnn_a': _L3_gnn_in['a'], 'L3_ffn_Wr': _L3_ffn_in['Wr'], 'L3_ffn_br': _L3_ffn_in['br'], 'L3_ffn_ln_g': _L3_ffn_in['ln_g'], 'L3_ffn_ln_b': _L3_ffn_in['ln_b'], 'L3_ffn_W1': _L3_ffn_in['W1'], 'L3_ffn_b1': _L3_ffn_in['b1'], 'L3_ffn_W2': _L3_ffn_in['W2'], 'L3_ffn_b2': _L3_ffn_in['b2']}

def reference(x, adj, L0_gnn_W, L0_gnn_b, L0_ffn_sW1, L0_ffn_sb1, L0_ffn_sW2, L0_ffn_sb2, L0_ffn_sW3, L0_ffn_sb3, L0_ffn_eW1, L0_ffn_eb1, L0_ffn_eW2, L0_ffn_eb2, L0_ffn_eW3, L0_ffn_eb3, L0_ffn_gW, L0_ffn_gb, L1_gnn_W_msg, L1_gnn_W_upd, L1_gnn_bias, L1_ffn_W_in, L1_ffn_conv_w, L1_ffn_conv_b, L1_ffn_dt_bias, L1_ffn_A_log, L1_ffn_D, L1_ffn_norm_w, L1_ffn_W_out, L1_ffn_W_lin, L1_ffn_b_lin, L2_gnn_Wq, L2_gnn_bq, L2_gnn_Wk, L2_gnn_bk, L2_gnn_Wv, L2_gnn_bv, L2_gnn_Wo, L2_gnn_bo, L2_gnn_gamma, L2_gnn_beta, L2_ffn_ln1_w, L2_ffn_ln2_w, L2_ffn_wq, L2_ffn_wk, L2_ffn_wv, L2_ffn_wo, L2_ffn_router_w, L2_ffn_w1, L2_ffn_w2, L2_ffn_w3, L3_gnn_W, L3_gnn_b, L3_gnn_a, L3_ffn_Wr, L3_ffn_br, L3_ffn_ln_g, L3_ffn_ln_b, L3_ffn_W1, L3_ffn_b1, L3_ffn_W2, L3_ffn_b2):
    import jax
    import jax.numpy as jnp

    def _L0_gnn_ref(A, X, W, b):
        import jax, jax.numpy as jnp
        import numpy as np
        B, N, C, OUT, S = (4, 1024, 128, 128, 25)
        DENSITY = 0.008
        mask = A != 0
        neg_inf = jnp.float32(-jnp.inf)
        pri = -jnp.arange(N, dtype=jnp.float32)
        scores = jnp.where(mask, pri, neg_inf)
        vals, idx = jax.lax.top_k(scores, S)
        valid = vals > neg_inf
        feats = jax.vmap(lambda x, i: x[i])(X, idx)
        feats = jnp.where(valid[..., None], feats, neg_inf)
        agg = feats.max(axis=2)
        degree = mask.sum(axis=-1)
        agg = jnp.where((degree <= S)[..., None], jnp.maximum(agg, 0.0), agg)
        h = jnp.concatenate([X, agg], axis=-1)
        out = jax.nn.relu(jnp.einsum('bnf,fo->bno', h, W) + b)
        return out

    def _L0_ffn_ref(x, sW1, sb1, sW2, sb2, sW3, sb3, eW1, eb1, eW2, eb2, eW3, eb3, gW, gb):
        import jax, jax.numpy as jnp
        import numpy as np
        B, A = (2048, 8)
        IN, OUT = (128, 128)
        SH1, SH2 = (128, 128)
        EH1, EH2 = (128, 64)
        E, TOPK = (4, 2)

        def _shared_mlp(x, W1, b1, W2, b2, W3, b3):
            h = jax.nn.relu(x @ W1 + b1)
            h = jax.nn.relu(h @ W2 + b2)
            return h @ W3 + b3

        def _experts_mlp(x, eW1, eb1, eW2, eb2, eW3, eb3):
            h = jax.nn.relu(jnp.einsum('baf,efh->ebah', x, eW1) + eb1[:, None, None, :])
            h = jax.nn.relu(jnp.einsum('ebah,ehg->ebag', h, eW2) + eb2[:, None, None, :])
            o = jnp.einsum('ebag,ego->ebao', h, eW3) + eb3[:, None, None, :]
            return jnp.moveaxis(o, 0, -1)
        all_out = _experts_mlp(x, eW1, eb1, eW2, eb2, eW3, eb3)
        shared = _shared_mlp(x, sW1, sb1, sW2, sb2, sW3, sb3)
        gates = jax.nn.softmax(x @ gW + gb, axis=-1)
        topv, topi = jax.lax.top_k(gates, TOPK)
        topw = jax.nn.softmax(topv, axis=-1)
        sel = jnp.take_along_axis(all_out, topi[:, :, None, :], axis=-1)
        gated = jnp.sum(sel * topw[:, :, None, :], axis=-1)
        return shared + gated

    def _L1_gnn_ref(x, adj, W_msg, W_upd, bias):
        import jax, jax.numpy as jnp
        import numpy as np
        a = adj.astype(x.dtype)
        h = jnp.einsum('bnf,fu->bnu', x, W_msg)
        msg_sum = jnp.einsum('bij,biu->bju', a, h)
        deg = jnp.sum(a, axis=1)
        messages = jnp.where(deg[..., None] > 0, msg_sum / jnp.maximum(deg, 1.0)[..., None], 0.0)
        out = jnp.einsum('bnf,fu->bnu', x, W_upd) + messages + bias
        return jax.nn.relu(out)

    def _L1_ffn_ref(x, W_in, conv_w, conv_b, dt_bias, A_log, D, norm_w, W_out, W_lin, b_lin):
        import jax, jax.numpy as jnp
        import numpy as np
        D_MODEL = 128
        D_STATE = 64
        D_CONV = 4
        EXPAND = 2
        HEADDIM = 64
        D_INNER = EXPAND * D_MODEL
        NHEADS = D_INNER // HEADDIM
        CONV_DIM = D_INNER + 2 * D_STATE
        D_IN_PROJ = 2 * D_INNER + 2 * D_STATE + NHEADS
        CHUNK = 128
        EPS = 1e-05

        def segsum(a):
            T = a.shape[-1]
            cs = jnp.cumsum(a, axis=-1)
            ss = cs[..., :, None] - cs[..., None, :]
            mask = jnp.tril(jnp.ones((T, T), dtype=bool))
            return jnp.where(mask, ss, -jnp.inf)

        def mamba2_block(x, W_in, conv_w, conv_b, dt_bias, A_log, D, norm_w, W_out, W_lin, b_lin):
            Bsz, L, _ = x.shape
            zxbcdt = x @ W_in
            z, xBC, dt = jnp.split(zxbcdt, [D_INNER, D_INNER + CONV_DIM], axis=-1)
            xp = jnp.pad(xBC, ((0, 0), (D_CONV - 1, 0), (0, 0)))
            conv = conv_b + sum((xp[:, k:k + L, :] * conv_w[:, k] for k in range(D_CONV)))
            xBC = jax.nn.silu(conv)
            xh, Bmat, Cmat = jnp.split(xBC, [D_INNER, D_INNER + D_STATE], axis=-1)
            dt = jax.nn.softplus(dt + dt_bias)
            A = -jnp.exp(A_log)
            nc = L // CHUNK
            xh = xh.reshape(Bsz, nc, CHUNK, NHEADS, HEADDIM)
            Bc = Bmat.reshape(Bsz, nc, CHUNK, D_STATE)
            Cc = Cmat.reshape(Bsz, nc, CHUNK, D_STATE)
            dtc = dt.reshape(Bsz, nc, CHUNK, NHEADS)
            dA = jnp.einsum('bclh,h->bhcl', dtc, A)
            A_cum = jnp.cumsum(dA, axis=-1)
            Lmat = jnp.exp(segsum(dA))
            xdt = xh * dtc[..., None]
            Y_diag = jnp.einsum('bcln,bcsn,bhcls,bcshp->bclhp', Cc, Bc, Lmat, xdt)
            decay_states = jnp.exp(A_cum[..., -1:] - A_cum)
            states = jnp.einsum('bcln,bhcl,bclhp->bchpn', Bc, decay_states, xdt)
            chunk_decay = jnp.exp(A_cum[..., -1])

            def step(h, inp):
                s, d = inp
                return (h * d[..., None, None] + s, h)
            _, prevs = jax.lax.scan(step, jnp.zeros_like(states[:, 0]), (jnp.moveaxis(states, 1, 0), jnp.moveaxis(chunk_decay, 2, 0)))
            prevs = jnp.moveaxis(prevs, 0, 1)
            Y_off = jnp.einsum('bcln,bchpn,bhcl->bclhp', Cc, prevs, jnp.exp(A_cum))
            Y = (Y_diag + Y_off + xh * D[:, None]).reshape(Bsz, L, D_INNER)
            Y = Y * jax.nn.silu(z)
            Y = Y * jax.lax.rsqrt(jnp.mean(Y * Y, axis=-1, keepdims=True) + EPS) * norm_w
            out = Y @ W_out
            return out @ W_lin + b_lin
        return mamba2_block(x, W_in, conv_w, conv_b, dt_bias, A_log, D, norm_w, W_out, W_lin, b_lin)

    def _L2_gnn_ref(x, adj, Wq, bq, Wk, bk, Wv, bv, Wo, bo, gamma, beta):
        import jax, jax.numpy as jnp
        import numpy as np
        DIM = 128
        HEADS = 4
        B, N = (2, 2048)
        NEG = -1000000000.0
        EPS = 1e-05
        Bx, Nx, C = x.shape
        H = HEADS
        D = C // H
        scale = D ** (-0.5)

        def proj(W, b):
            return (x @ W.T + b).reshape(Bx, Nx, H, D).transpose(0, 2, 1, 3)
        q = proj(Wq, bq)
        k = proj(Wk, bk)
        v = proj(Wv, bv)
        attn = jnp.einsum('bhnd,bhmd->bhnm', q, k) * scale
        attn = jnp.where(adj[:, None, :, :] == 0, NEG, attn)
        attn = jax.nn.softmax(attn, axis=-1)
        out = jnp.einsum('bhnm,bhmd->bhnd', attn, v)
        out = out.transpose(0, 2, 1, 3).reshape(Bx, Nx, C)
        out = out @ Wo.T + bo
        mu = jnp.mean(out, axis=-1, keepdims=True)
        var = jnp.var(out, axis=-1, keepdims=True)
        return (out - mu) * jax.lax.rsqrt(var + EPS) * gamma + beta

    def _L2_ffn_ref(x, ln1_w, ln2_w, wq, wk, wv, wo, router_w, w1, w2, w3):
        import jax, jax.numpy as jnp
        import numpy as np
        B, T, C = (64, 192, 128)
        NH, NKV = (4, 2)
        HD = C // NH
        NREP = NH // NKV
        NE, TOPK = (8, 2)
        HID = int(8 / 3 * C)
        EPS_RMS = 1e-06

        def _rope_tables(t_len):
            inv_freq = 1.0 / 10000.0 ** (np.arange(0, HD, 2, dtype=np.float32) / HD)
            t = np.arange(t_len, dtype=np.float32)
            freqs = np.outer(t, inv_freq)
            emb = np.concatenate([freqs, freqs], axis=-1)
            return (jnp.asarray(np.cos(emb)), jnp.asarray(np.sin(emb)))

        def _rotate_half(x):
            h = x.shape[-1] // 2
            return jnp.concatenate([-x[..., h:], x[..., :h]], axis=-1)

        def _rmsnorm(v, w):
            return v * jax.lax.rsqrt(jnp.mean(v * v, axis=-1, keepdims=True) + EPS_RMS) * w
        Bx, Tx, Cx = x.shape
        h = _rmsnorm(x, ln1_w)
        q = (h @ wq.T).reshape(Bx, Tx, NH, HD).transpose(0, 2, 1, 3)
        k = (h @ wk.T).reshape(Bx, Tx, NKV, HD).transpose(0, 2, 1, 3)
        v = (h @ wv.T).reshape(Bx, Tx, NKV, HD).transpose(0, 2, 1, 3)
        cos, sin = _rope_tables(Tx)
        cos, sin = (cos[None, None], sin[None, None])
        q = q * cos + _rotate_half(q) * sin
        k = k * cos + _rotate_half(k) * sin
        k = jnp.repeat(k, NREP, axis=1)
        v = jnp.repeat(v, NREP, axis=1)
        scores = jnp.einsum('bhtd,bhsd->bhts', q, k) / jnp.sqrt(jnp.float32(HD))
        causal = jnp.tril(jnp.ones((Tx, Tx), dtype=bool))
        scores = jnp.where(causal[None, None], scores, jnp.float32(-1e+30))
        att = jax.nn.softmax(scores, axis=-1)
        y = jnp.einsum('bhts,bhsd->bhtd', att, v).transpose(0, 2, 1, 3).reshape(Bx, Tx, Cx)
        x = x + y @ wo.T
        flat = _rmsnorm(x, ln2_w).reshape(-1, Cx)
        probs = jax.nn.softmax(flat @ router_w.T, axis=-1)
        tp, ti = jax.lax.top_k(probs, TOPK)
        tp = tp / (jnp.sum(tp, axis=-1, keepdims=True) + 1e-09)
        weights = jnp.sum(tp[..., None] * jax.nn.one_hot(ti, NE, dtype=flat.dtype), axis=1)
        out = jnp.zeros_like(flat)
        for e in range(NE):
            hh = jax.nn.silu(flat @ w1[e].T) * (flat @ w3[e].T)
            out = out + weights[:, e:e + 1] * (hh @ w2[e].T)
        return x + out.reshape(Bx, Tx, Cx)

    def _L3_gnn_ref(node_feats, adj_matrix, W, b, a):
        import jax, jax.numpy as jnp
        import numpy as np
        B, N, C_IN, H, C_OUT = (8, 512, 128, 4, 128)
        C = C_OUT // H
        ALPHA = 0.2
        NEG_INF = -9000000000000000.0
        Bb, Nn, _ = node_feats.shape
        Hh, twoC = a.shape
        Cc = twoC // 2
        h = (node_feats @ W.T + b).reshape(Bb, Nn, Hh, Cc)
        a_src, a_dst = (a[:, :Cc], a[:, Cc:])
        l_src = jnp.einsum('bihc,hc->bih', h, a_src)
        l_dst = jnp.einsum('bjhc,hc->bjh', h, a_dst)
        logits = jax.nn.leaky_relu(l_src[:, :, None, :] + l_dst[:, None, :, :], ALPHA)
        logits = jnp.where(adj_matrix[..., None] == 1, logits, NEG_INF)
        probs = jax.nn.softmax(logits, axis=2)
        out = jnp.einsum('bijh,bjhc->bihc', probs, h)
        return out.reshape(Bb, Nn, Hh * Cc)

    def _L3_ffn_ref(x, Wr, br, ln_g, ln_b, W1, b1, W2, b2):
        import jax, jax.numpy as jnp
        import numpy as np
        TOP_K = 2
        LN_EPS = 1e-05
        B, S, D = x.shape
        N = B * S
        xt = x.reshape(N, D)
        logits = xt @ Wr + br
        probs = jax.nn.softmax(logits, axis=-1)
        top_p, top_idx = jax.lax.top_k(probs, TOP_K)
        weights = top_p / top_p.sum(axis=-1, keepdims=True)
        mu = xt.mean(axis=-1, keepdims=True)
        var = ((xt - mu) ** 2).mean(axis=-1, keepdims=True)
        xn = (xt - mu) * jax.lax.rsqrt(var + LN_EPS)
        xe = xn[None, :, :] * ln_g[:, None, :] + ln_b[:, None, :]
        h = jax.nn.gelu(jnp.einsum('end,edh->enh', xe, W1) + b1[:, None, :], approximate=False)
        y = jnp.einsum('enh,ehd->end', h, W2) + b2[:, None, :]
        y_tok = jnp.transpose(y, (1, 0, 2))
        sel = jnp.take_along_axis(y_tok, top_idx[:, :, None], axis=1)
        out = (weights[:, :, None] * sel).sum(axis=1)
        return out.reshape(B, S, D)
    x = x + _L0_gnn_ref(adj, _layernorm(x, axis=-1), L0_gnn_W, L0_gnn_b)
    x = x + _L0_ffn_ref(_layernorm(x, axis=-1), L0_ffn_sW1, L0_ffn_sb1, L0_ffn_sW2, L0_ffn_sb2, L0_ffn_sW3, L0_ffn_sb3, L0_ffn_eW1, L0_ffn_eb1, L0_ffn_eW2, L0_ffn_eb2, L0_ffn_eW3, L0_ffn_eb3, L0_ffn_gW, L0_ffn_gb)
    x = x + _L1_gnn_ref(_layernorm(x, axis=-1), adj, L1_gnn_W_msg, L1_gnn_W_upd, L1_gnn_bias)
    x = x + _L1_ffn_ref(_layernorm(x, axis=-1), L1_ffn_W_in, L1_ffn_conv_w, L1_ffn_conv_b, L1_ffn_dt_bias, L1_ffn_A_log, L1_ffn_D, L1_ffn_norm_w, L1_ffn_W_out, L1_ffn_W_lin, L1_ffn_b_lin)
    x = x + _L2_gnn_ref(_layernorm(x, axis=-1), adj, L2_gnn_Wq, L2_gnn_bq, L2_gnn_Wk, L2_gnn_bk, L2_gnn_Wv, L2_gnn_bv, L2_gnn_Wo, L2_gnn_bo, L2_gnn_gamma, L2_gnn_beta)
    x = x + _L2_ffn_ref(_layernorm(x, axis=-1), L2_ffn_ln1_w, L2_ffn_ln2_w, L2_ffn_wq, L2_ffn_wk, L2_ffn_wv, L2_ffn_wo, L2_ffn_router_w, L2_ffn_w1, L2_ffn_w2, L2_ffn_w3)
    x = x + _L3_gnn_ref(_layernorm(x, axis=-1), adj, L3_gnn_W, L3_gnn_b, L3_gnn_a)
    x = x + _L3_ffn_ref(_layernorm(x, axis=-1), L3_ffn_Wr, L3_ffn_br, L3_ffn_ln_g, L3_ffn_ln_b, L3_ffn_W1, L3_ffn_b1, L3_ffn_W2, L3_ffn_b2)
    return x

_drawn_inputs = setup_inputs


def setup_inputs(seed=0):
    import zlib

    import numpy as np

    out = dict(_drawn_inputs(seed))
    spreads = {'L0_gnn_b': (0.0, 0.1),
     'L0_ffn_sb1': (0.0, 0.399),
     'L0_ffn_sb2': (0.0, 0.1),
     'L0_ffn_sb3': (0.0, 0.1),
     'L0_ffn_eb1': (0.0, 0.659),
     'L0_ffn_eb2': (0.0, 0.37),
     'L0_ffn_eb3': (0.0, 0.1),
     'L0_ffn_gb': (0.0, 0.399),
     'L1_gnn_bias': (0.0, 0.1),
     'L1_ffn_D': (1.0, 0.2),
     'L1_ffn_norm_w': (1.0, 0.2),
     'L1_ffn_b_lin': (0.0, 0.1),
     'L2_gnn_bq': (0.0, 0.8),
     'L2_gnn_bk': (0.0, 2.0),
     'L2_gnn_bv': (0.0, 0.1),
     'L2_gnn_bo': (0.0, 0.1),
     'L2_gnn_gamma': (1.0, 0.2),
     'L2_gnn_beta': (0.0, 0.1),
     'L2_ffn_ln1_w': (1.0, 0.6),
     'L2_ffn_ln2_w': (1.0, 0.6),
     'L3_gnn_b': (0.0, 0.8),
     'L3_ffn_br': (0.0, 0.566),
     'L3_ffn_ln_g': (1.0, 0.6),
     'L3_ffn_ln_b': (0.0, 1.697),
     'L3_ffn_b1': (0.0, 1.675),
     'L3_ffn_b2': (0.0, 1.206)}
    factors = {'L1_ffn_dt_bias': 11.55,
     'L1_ffn_A_log': 7.336,
     'L2_gnn_Wq': 6.841,
     'L2_gnn_Wk': 6.741,
     'L2_ffn_wq': 8.0,
     'L2_ffn_wk': 8.0,
     'L2_ffn_wv': 3.995,
     'L2_ffn_wo': 4.099,
     'L2_ffn_router_w': 8.0,
     'L2_ffn_w1': 8.0,
     'L2_ffn_w2': 8.0,
     'L2_ffn_w3': 8.0}
    for name, (base, spread) in spreads.items():
        noise = np.random.default_rng([zlib.crc32(name.encode()), seed]).standard_normal(out[name].shape)
        drawn = base * np.exp(spread * noise) if base else spread * noise
        out[name] = jnp.asarray(drawn.astype(out[name].dtype))
    for name, factor in factors.items():
        out[name] = (out[name] * factor).astype(out[name].dtype)
    return out
```

```python
from collections import namedtuple
from contextlib import ExitStack, contextmanager

import numpy as np

import concourse.bass as bass
from concourse import mybir

F32 = mybir.dt.float32
BF16 = mybir.dt.bfloat16
I32 = mybir.dt.int32
U32 = mybir.dt.uint32
ALU = mybir.AluOpType
ACT = mybir.ActivationFunctionType
AX_X = mybir.AxisListType.X

P = 128
GRAPHS, NODES, CH = 8, 1024, 128
TILES = NODES // P
HALVES, HALF = 2, 512
NEIGH = 25
SLOTS = 32
HEADS, HD = 4, 32
MASKED = -(2.0 ** 100)
LN_EPS, RMS_EPS = 1e-5, 1e-6

L0_E, L2_E, L3_E = 4, 8, 8
EH2 = 64
HID = 341
HID_CHUNKS = [(0, 128), (128, 128), (256, HID - 256)]
L3_HID = 512
M_HEADS, M_HD, M_STATE, M_CONV = 4, 64, 64, 4
M_INNER = M_HEADS * M_HD

WEIGHTS = [
    ("l0_top", 128), ("l0_bot", 128), ("sW1", 128), ("sW2", 128), ("sW3", 128), ("eW1", L0_E * 128),
    ("eW2", L0_E * EH2), ("eW3", L0_E * 128), ("gW", L0_E), ("msg", 128), ("upd", 128),
    ("W_z", M_INNER), ("W_xh", M_INNER), ("W_B", M_STATE), ("W_C", M_STATE), ("W_dt", M_HEADS),
    ("W_out", 2 * 128), ("W_lin", 128), ("Wq", 128), ("Wk", 128), ("Wv", 128), ("Wo", 128),
    ("wq", 128), ("wq_rot", 128), ("wk", 128), ("wk_rot", 128), ("wv", 64), ("wo", 128), ("router", L2_E),
    ("gatW", 128), ("Wr", L3_E),
]
COLS = [
    ("sb1", 1), ("sb2", 1), ("sb3", 1), ("eb1", L0_E), ("eb2", L0_E), ("eb3", L0_E), ("gnn_bias", 1),
    ("conv_xh", 2 * M_CONV), ("conv_B", M_CONV), ("conv_C", M_CONV), ("convb_xh", 2), ("convb_B", 1),
    ("convb_C", 1), ("norm_w", 2), ("bq", 1), ("bk", 1), ("ln1", 1), ("ln2", 1), ("gat_b", 1),
    ("a_src", HEADS), ("a_dst", HEADS), ("ln_g", L3_E), ("ln_b", L3_E), ("b1", L3_E * 4), ("b2", L3_E),
]
ROWS = [
    ("l0_b", 128), ("gb", L0_E), ("dt_bias", M_HEADS), ("A_log", M_HEADS), ("D", M_INNER), ("b_lin", 128),
    ("bv", 128), ("bo", 128), ("gamma", 128), ("beta", 128), ("gat_brow", 128), ("br", L3_E),
    ("iota8", 8), ("rank", NODES),
]
CONSTS = [("ident", 128), ("le", 128), ("gt", 128), ("onehot", 8 * 128)]
EXP2 = 2 * HID + 3 * 128
EXP3 = 2 * L3_HID


class Memory:
    pass


def named_sems(sem, layer, names):
    return namedtuple("Semaphores", names)(*[sem(f"{layer}_{n}") for n in names])


def offsets(table):
    at, out = 0, {}
    for name, n in table:
        out[name] = (at, n)
        at += n
    return out, at


def sizes(table):
    return offsets(table)[1]


@contextmanager
def semaphores(nc, gathers=False):
    with ExitStack() as c:
        used = []

        def sem(name):
            used.append(c.enter_context(nc.semaphore(name)))
            return used[-1]

        yield sem
        numbers = sorted(s.num for s in used)
        starts = [n for n in numbers if n - 1 not in numbers]
        ends = [n + 1 for n in numbers if n + 1 not in numbers]
        runs = [range(first, end) for first, end in zip(starts, ends)]
        if gathers:
            for run in runs:
                nc.gpsimd.dma_reset(run)
        for run in runs:
            nc.gpsimd.sem_clear(run)
        nc.all_engine_barrier()




def linker(engine, semaphore):
    count = [0]

    def link(instruction):
        count[0] += 1
        instruction.then_inc(semaphore, 1)
        engine.wait_ge(semaphore, count[0])

    return link


def norm_vector(v, K, N, src, dst, eps, rms=False):
    link = linker(v, N.chain)
    for t in range(TILES):
        last = v.bn_stats(K.stats[:, t, :], src[:, t, :])
    link(last)
    for t in range(TILES):
        last = v.bn_aggr(K.mv[:, t, :], K.stats[:, t, :])
    link(last)
    spread = K.mv[:, :, 1]
    if rms:
        link(v.tensor_tensor(K.nsq[:, :], K.mv[:, :, 0], K.mv[:, :, 0], ALU.mult))
        link(v.tensor_tensor(K.nsq[:, :], K.nsq[:, :], K.mv[:, :, 1], ALU.add))
        spread = K.nsq[:, :]
    v.tensor_scalar(K.veps[:, :], spread, eps, None, ALU.add).then_inc(N.var, 1)
    v.wait_ge(N.std, 1)
    link(v.reciprocal(K.rstd[:, :], K.std[:, :]))
    for t in range(TILES):
        if rms:
            v.tensor_scalar(dst[:, t, :], src[:, t, :], K.rstd[:, t:t + 1], None, ALU.mult).then_inc(N.xn, 1)
        else:
            v.tensor_scalar(dst[:, t, :], src[:, t, :], K.mv[:, t, 0:1], K.rstd[:, t:t + 1],
                            ALU.subtract, ALU.mult).then_inc(N.xn, 1)


def norm_scalar(act, K, N):
    act.wait_ge(N.var, 1)
    act.activation(K.std[:, :], K.veps[:, :], ACT.Sqrt).then_inc(N.std, 1)


def turn_tensor(pe, K, src, banks, ready, done):
    for t in range(TILES):
        if ready is not None:
            pe.wait_ge(ready, t + 1)
        last = pe.transpose(K.ps[:, banks[t // 4], (t % 4) * P:(t % 4 + 1) * P], src[:, t, :], K.ident)
        if t % 4 == 3:
            last.then_inc(done, 1)


def turn_scalar(act, K, dst, banks, turned, done, scale=None):
    for h in range(HALVES):
        act.wait_ge(turned, h + 1)
        out = dst[:, h * HALF:(h + 1) * HALF]
        if scale is None:
            act.activation(out, K.ps[:, banks[h], :], ACT.Copy).then_inc(done, 1)
        else:
            act.activation(out, K.ps[:, banks[h], :], ACT.Copy, scale=scale).then_inc(done, 1)


def turn_back_tensor(pe, K, accT, banks, ready, need, done):
    for h in range(HALVES):
        pe.wait_ge(ready, need[h])
        for q in range(4):
            t = 4 * h + q
            last = pe.transpose(K.ps[:, banks[h], q * P:(q + 1) * P], accT[:, t * P:(t + 1) * P], K.ident)
        last.then_inc(done, 1)


def turn_back_vector(v, K, banks, done):
    for h in range(HALVES):
        v.wait_ge(done, h + 1)
        xh = K.x[:, 4 * h:4 * h + 4, :]
        v.tensor_tensor(xh, xh, K.ps[:, banks[h], :].rearrange("p (t c) -> p t c", t=4), ALU.add)


def router_tensor(pe, K, R, w, experts):
    for t in range(TILES):
        last = pe.matmul(K.ps[:, 6, t * 8:t * 8 + experts], K.xnT[:, t * P:(t + 1) * P], w, start=True, stop=True)
    last.then_inc(R.logits, 1)


def router_vector(v, K, R, experts, bias, mode):
    link = linker(v, R.chain)

    def over(ap):
        return ap.unsqueeze(2).to_broadcast((P, TILES, experts))

    link(v.memset(K.prob[:, :, :], -1.0))
    lg = K.logit[:, :, 0:experts]
    v.wait_ge(R.logits, 1)
    got = K.ps[:, 6, 0:8 * TILES].rearrange("p (t e) -> p t e", e=8)[:, :, 0:experts]
    if bias is None:
        link(v.tensor_copy(lg, got))
    else:
        link(v.tensor_tensor(lg, got, bias.unsqueeze(1).to_broadcast((P, TILES, experts)), ALU.add))
    link(v.tensor_reduce(K.r1[:, :], lg, AX_X, ALU.max))
    v.tensor_tensor(lg, lg, over(K.r1[:, :]), ALU.subtract).then_inc(R.shifted, 1)
    v.wait_ge(R.exps, 1)
    link(v.tensor_reduce(K.r1[:, :], lg, AX_X, ALU.add))
    link(v.reciprocal(K.r2[:, :], K.r1[:, :]))
    link(v.tensor_tensor(K.prob[:, :, 0:experts], lg, over(K.r2[:, :]), ALU.mult))
    for t in range(TILES):
        last = v.max(K.top[:, t, :], K.prob[:, t, :])
    link(last)
    for t in range(TILES):
        last = v.max_index(K.topi[:, t, :], K.top[:, t, :], K.prob[:, t, :])
    link(last)
    link(v.tensor_copy(K.topf[:, :, :], K.topi[:, :, 0:2]))
    first, second = K.top[:, :, 0], K.top[:, :, 1]
    if mode == "softmax":
        v.tensor_tensor(K.r1[:, :], second, first, ALU.subtract).then_inc(R.shifted, 1)
        v.wait_ge(R.exps, 2)
        link(v.tensor_scalar(K.r2[:, :], K.r1[:, :], 1.0, None, ALU.add))
        link(v.reciprocal(K.w1[:, :], K.r2[:, :]))
        link(v.tensor_tensor(K.w2[:, :], K.r1[:, :], K.w1[:, :], ALU.mult))
    else:
        link(v.tensor_tensor(K.r1[:, :], first, second, ALU.add))
        if mode == "floor":
            link(v.tensor_scalar(K.r1[:, :], K.r1[:, :], 1e-9, None, ALU.add))
        link(v.reciprocal(K.r2[:, :], K.r1[:, :]))
        link(v.tensor_tensor(K.w1[:, :], first, K.r2[:, :], ALU.mult))
        link(v.tensor_tensor(K.w2[:, :], second, K.r2[:, :], ALU.mult))
    iota = K.row("iota8").unsqueeze(1).to_broadcast((P, TILES, 8))

    def all8(ap):
        return ap.unsqueeze(2).to_broadcast((P, TILES, 8))

    link(v.tensor_tensor(K.gate[:, :, :], iota, all8(K.topf[:, :, 0]), ALU.is_equal))
    link(v.tensor_tensor(K.gate2[:, :, :], iota, all8(K.topf[:, :, 1]), ALU.is_equal))
    link(v.tensor_tensor(K.gate[:, :, :], K.gate[:, :, :], all8(K.w1[:, :]), ALU.mult))
    link(v.tensor_tensor(K.gate2[:, :, :], K.gate2[:, :, :], all8(K.w2[:, :]), ALU.mult))
    v.tensor_tensor(K.gate[:, :, :], K.gate[:, :, :], K.gate2[:, :, :], ALU.add).then_inc(R.gate, 1)


def router_scalar(act, K, R, experts, mode):
    act.wait_ge(R.shifted, 1)
    lg = K.logit[:, :, 0:experts]
    act.activation(lg, lg, ACT.Exp).then_inc(R.exps, 1)
    if mode == "softmax":
        act.wait_ge(R.shifted, 2)
        act.activation(K.r1[:, :], K.r1[:, :], ACT.Exp).then_inc(R.exps, 1)


def gates_tensor(pe, K, R):
    pe.wait_ge(R.gate, 1)
    for t in range(TILES):
        last = pe.transpose(K.ps[0:8, 6 + t // 4, (t % 4) * P:(t % 4 + 1) * P], K.gate[:, t, :], K.ident)
    last.then_inc(R.turned, 1)


def gates_scalar(act, K, R):
    act.wait_ge(R.turned, 1)
    for h in range(HALVES):
        act.activation(K.gateT[:, h * HALF:(h + 1) * HALF], K.ps[0:8, 6 + h, :], ACT.Copy).then_inc(R.gateT, 1)


def spread_gate_tensor(pe, K, R, n, e, h):
    pe.wait_ge(R.gateT, 2)
    if n >= 1:
        pe.wait_ge(R.spread_out, n)
    pe.matmul(K.ps[:, 7, :], K.onehot[:, e * P:(e + 1) * P], K.gateT[:, h * HALF:(h + 1) * HALF],
              start=True, stop=True).then_inc(R.spread, 1)


def spread_gate_scalar(act, K, R, n):
    act.wait_ge(R.spread, n + 1)
    if n >= 2:
        act.wait_ge(R.used, n - 1)
    act.activation(K.wb[:, n % 2, :], K.ps[:, 7, :], ACT.Copy).then_inc(R.spread_out, 1)


def norm_sems(sem, layer):
    return named_sems(sem, f"{layer}_norm", ("chain", "var", "std", "xn", "turned", "xT"))


def router_sems(sem, layer):
    names = ("chain", "logits", "shifted", "exps", "gate", "turned", "gateT", "spread", "spread_out", "used")
    return named_sems(sem, f"{layer}_route", names)




def next_rows_vector(v, K, G):
    v.wait_ge(G.x_in, 16)
    link = linker(v, G.norm_chain)
    for t in range(TILES):
        last = v.bn_stats(K.g_stats[:, t, :], K.xg[:, t, :])
    link(last)
    for t in range(TILES):
        last = v.bn_aggr(K.g_mv[:, t, :], K.g_stats[:, t, :])
    link(last)
    v.tensor_scalar(K.g_veps[:, :], K.g_mv[:, :, 1], LN_EPS, None, ALU.add).then_inc(G.var, 1)
    v.wait_ge(G.std, 1)
    link(v.reciprocal(K.g_rstd[:, :], K.g_std[:, :]))
    for t in range(TILES):
        v.tensor_scalar(K.xg[:, t, :], K.xg[:, t, :], K.g_mv[:, t, 0:1], K.g_rstd[:, t:t + 1],
                        ALU.subtract, ALU.mult).then_inc(G.xn, 1)


def next_rows_scalar(act, K, G):
    act.wait_ge(G.var, 1)
    act.activation(K.g_std[:, :], K.g_veps[:, :], ACT.Sqrt).then_inc(G.std, 1)


def next_rows_sync(sp, K, G, g):
    sp.dma_start(K.xg[:, :, :], K.d_x[g, :, :].rearrange("(t p) c -> p t c", p=P)).then_inc(G.x_in, 16)
    sp.wait_ge(G.xn, TILES)
    sp.dma_start(K.d_rows[0:NODES, :].rearrange("(t p) c -> p t c", p=P), K.xg[:, :, :]).then_inc(G.rows, 16)
    sp.dma_start(K.d_rows[NODES:NODES + 1, :], K.zero_row[:, :]).then_inc(G.rows, 16)
    sp.wait_ge(G.rows, 32)


def next_adj_sync(sp, K, G, g, t):
    if t >= 1:
        sp.wait_ge(G.ranked, t)
    sp.dma_start(K.adj_next[:, :], K.d_adj[g, t * P:(t + 1) * P, :]).then_inc(G.adj_in, 16)


def next_index_vector(v, K, G, t, link):
    v.wait_ge(G.adj_in, 16 * (t + 1))
    v.tensor_tensor(K.ranks[:, :], K.adj_next[:, :], K.row("rank"), ALU.mult).then_inc(G.ranked, 1)
    v.wait_ge(G.ranked, t + 1)
    for q in range(SLOTS // 8):
        link(v.max(K.first[:, 8 * q:8 * q + 8], K.ranks[:, :]))
        if q < SLOTS // 8 - 1:
            link(v.match_replace(K.ranks[:, :], K.first[:, 8 * q:8 * q + 8], K.ranks[:, :], 0.0))
    link(v.tensor_scalar(K.idx[:, t, :], K.first[:, :], -1.0, float(NODES), ALU.mult, ALU.add))
    link(v.tensor_scalar(K.floor[:, t:t + 1], K.first[:, NEIGH:NEIGH + 1], 0.0, -3.0e38, ALU.is_gt, ALU.mult))


def gather_pool(pool, K, G, t):
    if t >= 2:
        pool.wait_ge(G.pooled, t - 1)
    for s in range(NEIGH):
        pool.indirect_dma_start(out=K.neigh[:, t % 2, s, :], out_offset=None, in_=K.d_rows,
                                in_offset=bass.IndirectOffsetOnAxis(ap=K.idx[:, t, s:s + 1], axis=0)
                                ).then_inc(G.gathered[t % 2], 16)


def pool_max_vector(v, K, G, t, link):
    v.wait_ge(G.gathered[t % 2], 16 * NEIGH * (t // 2 + 1))
    v.tensor_reduce(K.aggraw[:, :], K.neigh[:, t % 2, :, :].rearrange("p s c -> p c s"), AX_X, ALU.max
                    ).then_inc(G.pooled, 1)
    v.wait_ge(G.pooled, t + 1)
    link(v.tensor_scalar(K.agg[:, t, :], K.aggraw[:, :], K.floor[:, t:t + 1], None, ALU.max))




def layer0_gnn(nc, K, sem, g):
    N = norm_sems(sem, "pool")
    x_in, agg_turned, aggT_ready = sem("x_in"), sem("agg_turned"), sem("aggT_ready")
    mixed, chain = sem("pool_mixed"), sem("pool_chain")
    with ExitStack() as c:
        aggT = c.enter_context(nc.sbuf_tensor("aggT", [P, NODES], F32))
        tmp = c.enter_context(nc.sbuf_tensor("pool_tmp", [P, HALVES, HALF], F32))
        with nc.Block() as block:
            @block.sync
            def _(sp):
                sp.dma_start(K.x[:, :, :], K.d_x[g, :, :].rearrange("(t p) c -> p t c", p=P)).then_inc(x_in, 16)

            @block.vector
            def _(v):
                v.wait_ge(x_in, 16)
                norm_vector(v, K, N, K.x, K.xn, LN_EPS)
                link = linker(v, chain)
                for h in range(HALVES):
                    v.wait_ge(mixed, h + 1)
                    th = tmp[:, h, :].rearrange("p (t c) -> p t c", t=4)
                    xh = K.x[:, 4 * h:4 * h + 4, :]
                    link(v.tensor_tensor(th, K.ps[:, 4 + h, :].rearrange("p (t c) -> p t c", t=4),
                                         K.row("l0_b").unsqueeze(1).to_broadcast((P, 4, CH)), ALU.add))
                    v.scalar_tensor_tensor(out=xh, in0=th, scalar=0.0, in1=xh, op0=ALU.max, op1=ALU.add)

            @block.scalar
            def _(act):
                norm_scalar(act, K, N)
                turn_scalar(act, K, aggT, (2, 3), agg_turned, aggT_ready)
                turn_scalar(act, K, K.xnT, (0, 1), N.turned, N.xT)

            @block.tensor
            def _(pe):
                turn_tensor(pe, K, K.agg, (2, 3), None, agg_turned)
                turn_tensor(pe, K, K.xn, (0, 1), N.xn, N.turned)
                for h in range(HALVES):
                    pe.wait_ge(aggT_ready, h + 1)
                    pe.wait_ge(N.xT, h + 1)
                    for q in range(4):
                        t = 4 * h + q
                        out = K.ps[:, 4 + h, q * P:(q + 1) * P]
                        pe.matmul(out, K.xnT[:, t * P:(t + 1) * P], K.w("l0_top"), start=True, stop=False)
                        last = pe.matmul(out, aggT[:, t * P:(t + 1) * P], K.w("l0_bot"), start=False, stop=True)
                    last.then_inc(mixed, 1)




def layer0_ffn(nc, K, sem, g):
    N, R = norm_sems(sem, "mlp"), router_sems(sem, "mlp")
    l1, l2, l3 = sem("mlp_l1"), sem("mlp_l2"), sem("mlp_l3")
    h1_ready, h2_ready, y_used = sem("mlp_h1"), sem("mlp_h2"), sem("mlp_y_used")
    chain, turned_back = sem("mlp_chain"), sem("mlp_turned_back")
    adj_in, adj_done, adj_chain = [sem("adj_in0"), sem("adj_in1")], sem("adj_done"), sem("adj_chain")
    jobs = [(m, h) for m in range(1 + L0_E) for h in range(HALVES)]
    J = len(jobs)
    with ExitStack() as c:
        h1 = c.enter_context(nc.sbuf_tensor("h1", [P, 2, HALF], F32))
        h2 = c.enter_context(nc.sbuf_tensor("h2", [P, 2, HALF], F32))
        accT = c.enter_context(nc.sbuf_tensor("accT", [P, NODES], F32))
        tmp = c.enter_context(nc.sbuf_tensor("mlp_tmp", [P, HALF], F32))
        raw = c.enter_context(nc.sbuf_tensor("adj_raw", [P, 2, NODES], I32))
        with nc.Block() as block:
            @block.sync
            def _(sp):
                for t in range(TILES):
                    if t >= 2:
                        sp.wait_ge(adj_done, t - 1)
                    sp.dma_start(raw[:, t % 2, :], K.d_adj[g, t * P:(t + 1) * P, :]).then_inc(adj_in[t % 2], 16)

            @block.gpsimd
            def _(pool):
                for t in range(TILES):
                    pool.wait_ge(adj_in[t % 2], 16 * (t // 2 + 1))
                    pool.tensor_copy(K.adj[:, t, :], raw[:, t % 2, :]).then_inc(adj_done, 1)
                    pool.wait_ge(adj_done, t + 1)
                    pool.tensor_scalar(K.masked[:, t, :], K.adj[:, t, :], -MASKED, MASKED, ALU.mult, ALU.add
                                       ).then_inc(adj_chain, 1)

            @block.tensor
            def _(pe):
                turn_tensor(pe, K, K.xn, (4, 5), N.xn, N.turned)
                pe.wait_ge(N.xT, HALVES)
                router_tensor(pe, K, R, K.w("gW"), L0_E)
                for k in range(J + 2):
                    if k < J:
                        m, h = jobs[k]
                        w = K.w("sW1") if m == 0 else K.w("eW1")[:, (m - 1) * P:m * P]
                        if k >= 2:
                            pe.wait_ge(h1_ready, k - 1)
                        pe.matmul(K.ps[:, k % 2, :], w, K.xnT[:, h * HALF:(h + 1) * HALF], start=True, stop=True
                                  ).then_inc(l1, 1)
                    if 1 <= k <= J:
                        m, h = jobs[k - 1]
                        wide = P if m == 0 else EH2
                        w = K.w("sW2") if m == 0 else K.w("eW2")[:, (m - 1) * EH2:m * EH2]
                        pe.wait_ge(h1_ready, k)
                        if k - 1 >= 2:
                            pe.wait_ge(h2_ready, k - 2)
                        pe.matmul(K.ps[0:wide, 2 + (k - 1) % 2, :], w, h1[:, (k - 1) % 2, :], start=True, stop=True
                                  ).then_inc(l2, 1)
                    if k == 3:
                        gates_tensor(pe, K, R)
                    if k >= 2:
                        n = k - 2
                        m, h = jobs[n]
                        if m >= 1:
                            spread_gate_tensor(pe, K, R, n - HALVES, m - 1, h)
                        wide = P if m == 0 else EH2
                        w = K.w("sW3") if m == 0 else K.w("eW3")[0:EH2, (m - 1) * P:m * P]
                        pe.wait_ge(h2_ready, n + 1)
                        if n >= 2 * HALVES:
                            pe.wait_ge(R.used, n - 1 - HALVES)
                        elif n >= 2:
                            pe.wait_ge(y_used, n - 1)
                        pe.matmul(K.ps[:, 4 + n % 2, :], w, h2[0:wide, n % 2, :], start=True, stop=True
                                  ).then_inc(l3, 1)
                turn_back_tensor(pe, K, accT, (0, 1), chain, (J - HALVES - 1, J - HALVES), turned_back)

            @block.scalar
            def _(act):
                norm_scalar(act, K, N)
                turn_scalar(act, K, K.xnT, (4, 5), N.turned, N.xT)
                router_scalar(act, K, R, L0_E, "softmax")
                for k in range(J + 2):
                    if k == 3:
                        gates_scalar(act, K, R)
                    if k < J:
                        m = jobs[k][0]
                        act.wait_ge(l1, k + 1)
                        if k >= 2:
                            act.wait_ge(l2, k - 1)
                        bias = K.col("sb1") if m == 0 else K.col("eb1")[:, m - 1:m]
                        act.activation(h1[:, k % 2, :], K.ps[:, k % 2, :], ACT.Relu, bias=bias).then_inc(h1_ready, 1)
                    if 1 <= k <= J:
                        n = k - 1
                        m = jobs[n][0]
                        wide = P if m == 0 else EH2
                        act.wait_ge(l2, n + 1)
                        if n >= 2:
                            act.wait_ge(l3, n - 1)
                        bias = K.col("sb2") if m == 0 else K.col("eb2")[0:EH2, m - 1:m]
                        act.activation(h2[0:wide, n % 2, :], K.ps[0:wide, 2 + n % 2, :], ACT.Relu, bias=bias
                                       ).then_inc(h2_ready, 1)
                    if k >= 2 and jobs[k - 2][0] >= 1:
                        spread_gate_scalar(act, K, R, k - 2 - HALVES)

            @block.vector
            def _(v):
                norm_vector(v, K, N, K.x, K.xn, LN_EPS)
                router_vector(v, K, R, L0_E, K.row("gb"), "softmax")
                link = linker(v, chain)
                for n, (m, h) in enumerate(jobs):
                    v.wait_ge(l3, n + 1)
                    acc = accT[:, h * HALF:(h + 1) * HALF]
                    if m == 0:
                        v.tensor_scalar(acc, K.ps[:, 4 + n % 2, :], K.col("sb3"), None, ALU.add).then_inc(y_used, 1)
                        v.wait_ge(y_used, n + 1)
                        continue
                    v.wait_ge(R.spread_out, n - HALVES + 1)
                    v.scalar_tensor_tensor(out=tmp[:, :], in0=K.ps[:, 4 + n % 2, :],
                                           scalar=K.col("eb3")[:, m - 1:m], in1=K.wb[:, (n - HALVES) % 2, :],
                                           op0=ALU.add, op1=ALU.mult).then_inc(R.used, 1)
                    v.wait_ge(R.used, n - HALVES + 1)
                    link(v.tensor_tensor(acc, acc, tmp[:, :], ALU.add))
                turn_back_vector(v, K, (0, 1), turned_back)




def layer1_gnn(nc, K, sem, g):
    N = norm_sems(sem, "mean")
    h_ps, split, split_done, msg_ps, upd_ps = (sem(n) for n in ("mean_h", "mean_split", "mean_split_done",
                                                              "mean_msg", "mean_upd"))
    chain, summed, act_done, turned_back = (sem(n) for n in ("mean_chain", "mean_summed", "mean_act",
                                                             "mean_turned_back"))
    with ExitStack() as c:
        parts = [c.enter_context(nc.sbuf_tensor(f"mean_part{i}", [P, TILES * CH], BF16)) for i in range(3)]
        rest = c.enter_context(nc.sbuf_tensor("mean_rest", [P, NODES], F32))
        rdeg = c.enter_context(nc.sbuf_tensor("mean_rdeg", [P, NODES], F32))
        accT = c.enter_context(nc.sbuf_tensor("mean_accT", [P, NODES], F32))
        with nc.Block() as block:
            @block.tensor
            def _(pe):
                turn_tensor(pe, K, K.xn, (0, 1), N.xn, N.turned)
                for h in range(HALVES):
                    for t in range(TILES):
                        last = pe.matmul(K.ps[:, 2 + h, :], K.ones_bf[:, :], K.adj[:, t, h * HALF:(h + 1) * HALF],
                                         start=(t == 0), stop=(t == TILES - 1))
                    last.then_inc(upd_ps, 1)
                pe.wait_ge(N.xT, HALVES)
                for t in range(TILES):
                    last = pe.matmul(K.ps[:, 4 + t // 4, (t % 4) * P:(t % 4 + 1) * P], K.xnT[:, t * P:(t + 1) * P],
                                     K.w("msg"), start=True, stop=True)
                    if t % 4 == 3:
                        last.then_inc(h_ps, 1)
                for h in range(HALVES):
                    last = pe.matmul(K.ps[:, 0 + h, :], K.w("upd"), K.xnT[:, h * HALF:(h + 1) * HALF],
                                     start=True, stop=True)
                    last.then_inc(upd_ps, 1)
                pe.wait_ge(split_done, 3)
                for h in range(HALVES):
                    for i in range(3):
                        for t in range(TILES):
                            last = pe.matmul(K.ps[:, 6 + h, :], parts[i][:, t * CH:(t + 1) * CH],
                                             K.adj[:, t, h * HALF:(h + 1) * HALF],
                                             start=(i == 0 and t == 0), stop=(i == 2 and t == TILES - 1))
                    last.then_inc(msg_ps, 1)
                turn_back_tensor(pe, K, accT, (2, 3), act_done, (1, 2), turned_back)

            @block.scalar
            def _(act):
                norm_scalar(act, K, N)
                turn_scalar(act, K, K.xnT, (0, 1), N.turned, N.xT)
                for h in range(HALVES):
                    act.wait_ge(summed, h + 1)
                    out = accT[:, h * HALF:(h + 1) * HALF]
                    act.activation(out, out, ACT.Relu, bias=K.col("gnn_bias")).then_inc(act_done, 1)

            @block.vector
            def _(v):
                norm_vector(v, K, N, K.x, K.xn, LN_EPS)
                link = linker(v, chain)
                v.wait_ge(upd_ps, HALVES)
                for h in range(HALVES):
                    last = v.tensor_scalar(rdeg[:, h * HALF:(h + 1) * HALF], K.ps[:, 2 + h, :], 1.0, None, ALU.max)
                link(last)
                v.reciprocal(rdeg[:, :], rdeg[:, :])
                v.wait_ge(h_ps, HALVES)
                both = K.ps[:, 4:6, :].rearrange("p b n -> p (b n)")
                v.tensor_copy(parts[0][:, :], both).then_inc(split_done, 1)
                v.wait_ge(split_done, 1)
                link(v.tensor_tensor(rest[:, :], both, parts[0][:, :], ALU.subtract))
                v.tensor_copy(parts[1][:, :], rest[:, :]).then_inc(split_done, 1)
                v.wait_ge(split_done, 2)
                link(v.tensor_tensor(rest[:, :], rest[:, :], parts[1][:, :], ALU.subtract))
                v.tensor_copy(parts[2][:, :], rest[:, :]).then_inc(split_done, 1)
                v.wait_ge(upd_ps, 2 * HALVES)
                for h in range(HALVES):
                    v.wait_ge(msg_ps, h + 1)
                    out = accT[:, h * HALF:(h + 1) * HALF]
                    link(v.tensor_tensor(out, K.ps[:, 6 + h, :], rdeg[:, h * HALF:(h + 1) * HALF], ALU.mult))
                    v.tensor_tensor(out, out, K.ps[:, 0 + h, :], ALU.add).then_inc(summed, 1)
                turn_back_vector(v, K, (2, 3), turned_back)




def layer1_ffn(nc, K, sem, g):
    N = norm_sems(sem, "ssm")
    names = ("conv_ps", "conv_in", "conv_chain", "conv_done", "silu", "dt_ps", "dt_chain", "dt_exp", "dA", "sums_ps",
             "decays", "z_ps", "z_done", "seg_w", "tok_ps", "tok", "seg_ps", "seg", "cb_ps", "cbm", "mix", "xdd",
             "y_ps", "state_ps", "state", "y_chain", "y", "off", "xD", "ss_std_in", "ss_std", "yn", "yT_ps", "yT",
             "out_ps", "outT", "lin_ps", "padded", "decayed", "xdt")
    S = named_sems(sem, "ssm", names)
    CONVS = [("xh", 0, 128), ("xh", 1, 128), ("B", 0, M_STATE), ("C", 0, M_STATE)]
    with ExitStack() as c:
        def sb(name, shape, dt=F32):
            return c.enter_context(nc.sbuf_tensor("ssm_" + name, shape, dt))

        pre = [sb(f"pre{i}", [P, NODES + M_CONV - 1]) for i in range(2)]
        cv = [sb(f"cv{i}", [P, NODES]) for i in range(4)]
        sz = sb("sz", [P, TILES, M_INNER])
        yall = sb("y", [P, TILES, M_INNER])
        dt = sb("dt", [P, TILES * M_HEADS])
        dA = sb("dA", [P, TILES * M_HEADS])
        sp_t = [sb(f"sp{i}", [P, TILES * M_HEADS]) for i in range(4)]
        A = sb("A", [P, M_HEADS])
        decays = sb("decays", [P, 3, TILES * M_HEADS])
        segw = sb("segw", [P, 2, M_HEADS, P])
        L = sb("L", [P, M_HEADS, P])
        cbm = sb("cbm", [P, P])
        mix = sb("mix", [P, 2, M_HEADS, P])
        xtok = sb("xtok", [P, 2, M_INNER])
        xdt = sb("xdt", [P, 2, M_INNER])
        xdd = sb("xdd", [P, 2, M_INNER])
        xD = sb("xD", [P, 2, M_INNER])
        btok = sb("btok", [P, 2, M_STATE])
        state = sb("state", [M_STATE, 2, M_INNER])
        ya = sb("ya", [P, M_INNER])
        ysq = sb("ysq", [P, M_INNER])
        ss = sb("ss", [P, TILES])
        std = sb("std", [P, TILES])
        rstd = sb("rstd", [P, TILES])
        outT = sb("outT", [P, NODES])

        def heads(ap, d):
            return ap.rearrange("p (h d) -> p h d", d=d)

        def per_head(ap, d, n=P):
            return ap.unsqueeze(2).to_broadcast((n, M_HEADS, d))

        with nc.Block() as block:
            @block.tensor
            def _(pe):
                turn_tensor(pe, K, K.xn, (0, 1), N.xn, N.turned)
                pe.wait_ge(N.xT, HALVES)
                for t in range(TILES):
                    last = pe.matmul(K.ps[:, 6, t * M_HEADS:(t + 1) * M_HEADS], K.xnT[:, t * P:(t + 1) * P],
                                     K.w("W_dt"), start=True, stop=True)
                last.then_inc(S.dt_ps, 1)
                for i, (name, part, rows) in enumerate(CONVS):
                    for h in range(HALVES):
                        n = HALVES * i + h
                        if n >= 4:
                            pe.wait_ge(S.conv_in, n - 3)
                        pe.matmul(K.ps[0:rows, 2 + n % 4, :], K.w("W_" + name)[:, part * 128:part * 128 + rows],
                                  K.xnT[:, h * HALF:(h + 1) * HALF], start=True, stop=True).then_inc(S.conv_ps, 1)
                for q in range(4):
                    if q >= 2:
                        pe.wait_ge(S.z_done, q - 1)
                    for t in (2 * q, 2 * q + 1):
                        last = pe.matmul(K.ps[:, q % 2, (t % 2) * M_INNER:(t % 2 + 1) * M_INNER],
                                         K.xnT[:, t * P:(t + 1) * P], K.w("W_z"), start=True, stop=True)
                    last.then_inc(S.z_ps, 1)
                pe.wait_ge(S.dA, 1)
                for i, tri in enumerate((K.le, K.gt, K.ones)):
                    last = pe.matmul(K.ps[:, 7, 32 * i:32 * i + 32], tri, dA[:, :], start=True, stop=True)
                last.then_inc(S.sums_ps, 1)
                pe.wait_ge(S.z_done, 4)
                pe.wait_ge(S.silu, 4)
                pe.wait_ge(S.decays, 1)
                for t in range(TILES):
                    cols = slice(t * P, (t + 1) * P)
                    b = t % 2
                    if t >= 1:
                        pe.wait_ge(S.tok, 2 * t)
                        pe.wait_ge(S.cbm, t)
                    for i in range(2):
                        pe.transpose(K.ps[:, 2, i * P:(i + 1) * P], cv[i][:, cols], K.ident)
                    pe.transpose(K.ps[:, 3, 0:M_STATE], cv[2][0:M_STATE, cols], K.ident[0:M_STATE, 0:M_STATE]
                                 ).then_inc(S.tok_ps, 1)
                    pe.matmul(K.ps[:, 0, 0:P], cv[2][0:M_STATE, cols], cv[3][0:M_STATE, cols],
                              start=True, stop=True).then_inc(S.cb_ps, 1)
                    pe.wait_ge(S.seg_w, t + 1)
                    if t >= 1:
                        pe.wait_ge(S.seg, t)
                    for h in range(M_HEADS):
                        last = pe.matmul(K.ps[:, 4, h * P:(h + 1) * P], segw[:, b, h, :], K.le, start=True, stop=True)
                    last.then_inc(S.seg_ps, 1)
                    pe.wait_ge(S.xdd, t + 1)
                    if t >= 1:
                        pe.wait_ge(S.state, t)
                    pe.matmul(K.ps[0:M_STATE, 5, 0:M_INNER], btok[:, b, :], xdd[:, b, :], start=True, stop=True
                              ).then_inc(S.state_ps, 1)
                    if t >= 1:
                        pe.wait_ge(S.off, t)
                        pe.wait_ge(S.y, t)
                        pe.matmul(K.ps[:, 6, 0:M_INNER], cv[3][0:M_STATE, cols], state[:, (t - 1) % 2, :],
                                  start=True, stop=True)
                    pe.wait_ge(S.mix, t + 1)
                    for h in range(M_HEADS):
                        last = pe.matmul(K.ps[:, 7, h * M_HD:(h + 1) * M_HD], mix[:, b, h, :],
                                         xdt[:, b, h * M_HD:(h + 1) * M_HD], start=True, stop=True)
                    last.then_inc(S.y_ps, 1)
                for i in range(2):
                    for h in range(HALVES):
                        for q in range(4):
                            t = 4 * h + q
                            pe.wait_ge(S.yn, t + 1)
                            last = pe.transpose(K.ps[:, 2 * i + h, q * P:(q + 1) * P],
                                                yall[:, t, i * P:(i + 1) * P], K.ident)
                        last.then_inc(S.yT_ps, 1)
                for h in range(HALVES):
                    pe.wait_ge(S.yT, 4)
                    for i in range(2):
                        last = pe.matmul(K.ps[:, 4 + h, :], K.w("W_out")[:, i * P:(i + 1) * P],
                                         cv[i][:, h * HALF:(h + 1) * HALF], start=(i == 0), stop=(i == 1))
                    last.then_inc(S.out_ps, 1)
                for h in range(HALVES):
                    pe.wait_ge(S.outT, h + 1)
                    for q in range(4):
                        t = 4 * h + q
                        last = pe.matmul(K.ps[:, h, q * P:(q + 1) * P], outT[:, t * P:(t + 1) * P], K.w("W_lin"),
                                         start=True, stop=True)
                    last.then_inc(S.lin_ps, 1)

            @block.scalar
            def _(act):
                norm_scalar(act, K, N)
                act.activation(A[:, :], K.row("A_log"), ACT.Exp).then_inc(S.dt_exp, 1)
                turn_scalar(act, K, K.xnT, (0, 1), N.turned, N.xT)
                act.wait_ge(S.dt_chain, 2)
                act.activation(sp_t[1][:, :], sp_t[1][:, :], ACT.Exp, scale=-1.0).then_inc(S.dt_exp, 1)
                for i, (name, part, rows) in enumerate(CONVS):
                    if i >= 2:
                        act.wait_ge(S.conv_done, i - 1)
                    for h in range(HALVES):
                        n = HALVES * i + h
                        act.wait_ge(S.conv_ps, n + 1)
                        at = M_CONV - 1 + h * HALF
                        if n == 0:
                            act.wait_ge(S.padded, 1)
                        act.activation(pre[i % 2][0:rows, at:at + HALF], K.ps[0:rows, 2 + n % 4, :], ACT.Copy
                                       ).then_inc(S.conv_in, 1)
                for q in range(4):
                    act.wait_ge(S.z_ps, q + 1)
                    act.activation(sz[:, 2 * q:2 * q + 2, :].rearrange("p t n -> p (t n)"), K.ps[:, q % 2, :],
                                   ACT.Silu).then_inc(S.z_done, 1)
                for i, (name, part, rows) in enumerate(CONVS):
                    act.wait_ge(S.conv_done, i + 1)
                    act.activation(cv[i][0:rows, :], cv[i][0:rows, :], ACT.Silu).then_inc(S.silu, 1)
                act.wait_ge(S.sums_ps, 1)
                act.activation(decays[:, :, :], K.ps[:, 7, 0:96].rearrange("p (i n) -> p i n", i=3), ACT.Exp
                               ).then_inc(S.decays, 1)
                for t in range(TILES):
                    b = t % 2
                    act.wait_ge(S.tok_ps, t + 1)
                    if t >= 2:
                        act.wait_ge(S.xD, t - 1)
                        act.wait_ge(S.xdt, t - 1)
                        act.wait_ge(S.state_ps, t - 1)
                    act.activation(xtok[:, b, :], K.ps[:, 2, 0:M_INNER], ACT.Copy).then_inc(S.tok, 1)
                    act.activation(btok[:, b, :], K.ps[:, 3, 0:M_STATE], ACT.Copy).then_inc(S.tok, 1)
                    act.wait_ge(S.seg_ps, t + 1)
                    if t >= 1:
                        act.wait_ge(S.mix, t)
                    act.activation(L[:, :, :], K.ps[:, 4, :].rearrange("p (h n) -> p h n", h=M_HEADS), ACT.Exp
                                   ).then_inc(S.seg, 1)
                act.wait_ge(S.ss_std_in, 1)
                act.activation(std[:, :], ss[:, :], ACT.Sqrt).then_inc(S.ss_std, 1)
                for i in range(2):
                    for h in range(HALVES):
                        act.wait_ge(S.yT_ps, 2 * i + h + 1)
                        act.activation(cv[i][:, h * HALF:(h + 1) * HALF], K.ps[:, 2 * i + h, :], ACT.Copy,
                                       scale=K.col("norm_w")[:, i:i + 1]).then_inc(S.yT, 1)
                for h in range(HALVES):
                    act.wait_ge(S.out_ps, h + 1)
                    act.activation(outT[:, h * HALF:(h + 1) * HALF], K.ps[:, 4 + h, :], ACT.Copy
                                   ).then_inc(S.outT, 1)

            @block.gpsimd
            def _(pool):
                for i in range(2):
                    last = pool.memset(pre[i][:, 0:M_CONV - 1], 0.0)
                last.then_inc(S.padded, 1)
                pool.wait_ge(S.dA, 1)
                pool.wait_ge(S.decays, 1)
                for t in range(TILES):
                    b = t % 2
                    hs = slice(t * M_HEADS, (t + 1) * M_HEADS)
                    if t >= 2:
                        pool.wait_ge(S.seg_ps, t - 1)
                    pool.tensor_tensor(segw[:, b, :, :], K.gt.unsqueeze(1).to_broadcast((P, M_HEADS, P)),
                                       per_head(dA[:, hs], P), ALU.mult).then_inc(S.seg_w, 1)
                    pool.wait_ge(S.xdt, t + 1)
                    if t >= 2:
                        pool.wait_ge(S.state_ps, t - 1)
                    pool.tensor_tensor(heads(xdd[:, b, :], M_HD), heads(xdt[:, b, :], M_HD),
                                       per_head(decays[:, 1, hs], M_HD), ALU.mult).then_inc(S.xdd, 1)
                    if t >= 2:
                        pool.wait_ge(S.y, t - 1)
                    pool.tensor_tensor(xD[:, b, :], xtok[:, b, :], K.row("D"), ALU.mult).then_inc(S.xD, 1)

            @block.vector
            def _(v):
                norm_vector(v, K, N, K.x, K.xn, LN_EPS)
                dlink = linker(v, S.dt_chain)
                a, u, s, w = (sp_t[i][:, :] for i in range(4))
                v.wait_ge(S.dt_ps, 1)
                dlink(v.tensor_tensor(heads(a, M_HEADS), heads(K.ps[:, 6, 0:32], M_HEADS),
                                      K.row("dt_bias").unsqueeze(1).to_broadcast((P, TILES, M_HEADS)), ALU.add))
                v.scalar_tensor_tensor(out=u, in0=a, scalar=-1.0, in1=a, op0=ALU.mult, op1=ALU.max
                                       ).then_inc(S.dt_chain, 1)
                v.wait_ge(S.dt_exp, 2)
                dlink2 = linker(v, S.y_chain)
                dlink2(v.tensor_scalar(s, u, 2.0, None, ALU.add))
                dlink2(v.reciprocal(w, s))
                dlink2(v.tensor_tensor(s, u, w, ALU.mult))
                dlink2(v.tensor_tensor(w, s, s, ALU.mult))
                dlink2(v.tensor_scalar(u, w, 1.0 / 17.0, None, ALU.mult))
                for odd in (15, 13, 11, 9, 7, 5, 3):
                    dlink2(v.scalar_tensor_tensor(out=u, in0=u, scalar=1.0 / odd, in1=w, op0=ALU.add, op1=ALU.mult))
                dlink2(v.scalar_tensor_tensor(out=u, in0=u, scalar=1.0, in1=s, op0=ALU.add, op1=ALU.mult))
                dlink2(v.tensor_scalar(u, u, 2.0, None, ALU.mult))
                dlink2(v.scalar_tensor_tensor(out=dt[:, :], in0=a, scalar=0.0, in1=u, op0=ALU.max, op1=ALU.add))
                v.scalar_tensor_tensor(out=heads(dA[:, :], M_HEADS), in0=heads(dt[:, :], M_HEADS), scalar=-1.0,
                                       in1=A[:, :].unsqueeze(1).to_broadcast((P, TILES, M_HEADS)),
                                       op0=ALU.mult, op1=ALU.mult).then_inc(S.dA, 1)
                clink = linker(v, S.conv_chain)
                for i, (name, part, rows) in enumerate(CONVS):
                    taps = K.col("conv_" + name)[0:rows, part * M_CONV:(part + 1) * M_CONV]
                    out = cv[i][0:rows, :]
                    v.wait_ge(S.conv_in, HALVES * (i + 1))
                    clink(v.tensor_scalar(out, pre[i % 2][0:rows, 0:NODES], taps[:, 0:1],
                                          K.col("convb_" + name)[0:rows, part:part + 1], ALU.mult, ALU.add))
                    for k in range(1, M_CONV):
                        last = v.scalar_tensor_tensor(out=out, in0=pre[i % 2][0:rows, k:k + NODES],
                                                      scalar=taps[:, k:k + 1], in1=out, op0=ALU.mult, op1=ALU.add)
                        if k < M_CONV - 1:
                            clink(last)
                    last.then_inc(S.conv_done, 1)
                ylink = linker(v, S.off)
                for t in range(TILES):
                    b = t % 2
                    hs = slice(t * M_HEADS, (t + 1) * M_HEADS)
                    v.wait_ge(S.tok, 2 * t + 2)
                    if t >= 2:
                        v.wait_ge(S.y_ps, t - 1)
                        v.wait_ge(S.xdd, t - 1)
                    v.tensor_tensor(heads(xdt[:, b, :], M_HD), heads(xtok[:, b, :], M_HD),
                                    per_head(dt[:, hs], M_HD), ALU.mult).then_inc(S.xdt, 1)
                    v.wait_ge(S.cb_ps, t + 1)
                    v.tensor_tensor(cbm[:, :], K.ps[:, 0, 0:P], K.le, ALU.mult).then_inc(S.cbm, 1)
                    v.wait_ge(S.cbm, t + 1)
                    v.wait_ge(S.seg, t + 1)
                    if t >= 2:
                        v.wait_ge(S.y_ps, t - 1)
                    v.tensor_tensor(mix[:, b, :, :], L[:, :, :], cbm[:, :].unsqueeze(1).to_broadcast((P, M_HEADS, P)),
                                    ALU.mult).then_inc(S.mix, 1)
                    v.wait_ge(S.state_ps, t + 1)
                    if t == 0:
                        v.tensor_copy(state[:, 0, :], K.ps[0:M_STATE, 5, 0:M_INNER]).then_inc(S.state, 1)
                    elif t >= 1:
                        v.wait_ge(S.state, t)
                        now = heads(state[:, b, :], M_HD)
                        v.wait_ge(S.y_ps, t)
                        v.tensor_tensor(now, heads(state[:, 1 - b, :], M_HD),
                                        per_head(decays[0:M_STATE, 2, hs], M_HD, M_STATE), ALU.mult
                                        ).then_inc(S.decayed, 1)
                        v.wait_ge(S.decayed, t)
                        v.tensor_tensor(state[:, b, :], state[:, b, :], K.ps[0:M_STATE, 5, 0:M_INNER], ALU.add
                                        ).then_inc(S.state, 1)
                    v.wait_ge(S.y_ps, t + 1)
                    v.wait_ge(S.xD, t + 1)
                    if t >= 1:
                        ylink(v.tensor_tensor(heads(ya[:, :], M_HD), heads(K.ps[:, 6, 0:M_INNER], M_HD),
                                              per_head(decays[:, 0, hs], M_HD), ALU.mult))
                        dlink2(v.tensor_tensor(ya[:, :], ya[:, :], K.ps[:, 7, 0:M_INNER], ALU.add))
                    else:
                        ylink(v.tensor_copy(ya[:, :], K.ps[:, 7, 0:M_INNER]))
                    dlink2(v.tensor_tensor(ya[:, :], ya[:, :], xD[:, b, :], ALU.add))
                    v.tensor_tensor(yall[:, t, :], ya[:, :], sz[:, t, :], ALU.mult).then_inc(S.y, 1)
                    v.wait_ge(S.y, t + 1)
                    dlink2(v.tensor_tensor(ysq[:, :], yall[:, t, :], yall[:, t, :], ALU.mult))
                    dlink2(v.tensor_reduce(ss[:, t:t + 1], ysq[:, :], AX_X, ALU.add))
                v.tensor_scalar(ss[:, :], ss[:, :], 1.0 / M_INNER, LN_EPS, ALU.mult, ALU.add).then_inc(S.ss_std_in, 1)
                v.wait_ge(S.ss_std, 1)
                dlink2(v.reciprocal(rstd[:, :], std[:, :]))
                for t in range(TILES):
                    v.tensor_scalar(yall[:, t, :], yall[:, t, :], rstd[:, t:t + 1], None, ALU.mult
                                    ).then_inc(S.yn, 1)
                for h in range(HALVES):
                    v.wait_ge(S.lin_ps, h + 1)
                    xh = K.x[:, 4 * h:4 * h + 4, :]
                    dlink2(v.tensor_tensor(xh, xh, K.ps[:, h, :].rearrange("p (t c) -> p t c", t=4), ALU.add))
                    dlink2(v.tensor_tensor(xh, xh, K.row("b_lin").unsqueeze(1).to_broadcast((P, 4, CH)), ALU.add))




def attend_sems(sem, layer):
    names = ("scores", "shifted", "top", "probs", "turned", "copied0", "copied1", "out", "outT", "back", "normed", "chain")
    return named_sems(sem, f"{layer}_att", names)



RING = 8


def attend_scores_tensor(pe, K, A, n, qT, kT, width):
    t, h = n // HEADS, n % HEADS
    if n >= 2:
        pe.wait_ge(A.shifted, n - 1)
    for at in range(0, width, HALF):
        n_cols = min(HALF, width - at)
        last = pe.matmul(K.ps[:, 2 * (n % 2) + at // HALF, 0:n_cols], qT[:, h, t * P:(t + 1) * P],
                         kT[:, at:at + n_cols], start=True, stop=True)
    last.then_inc(A.scores, 1)


def attend_turn_tensor(pe, K, A, n, probs, width):
    pe.wait_ge(A.probs, n + 1)
    if n >= 1:
        pe.wait_ge(A.copied0, n)
        pe.wait_ge(A.copied1, n)
    for at in range(0, width, HALF):
        for j in range(at // P, min(at + HALF, width) // P):
            last = pe.transpose(K.ps[:, 4 + at // HALF, (j % 4) * P:(j % 4 + 1) * P],
                                probs[:, n % 2, j * P:(j + 1) * P], K.ident)
        last.then_inc(A.turned, 1)


def attend_values_tensor(pe, K, A, t, probsT, values, width):
    pe.wait_ge(A.copied0, HEADS * (t + 1))
    pe.wait_ge(A.copied1, HEADS * (t + 1))
    if t >= 1:
        pe.wait_ge(A.outT, t)
    blocks = width // P
    for j in range(blocks):
        for h in range(HEADS):
            last = pe.matmul(K.ps[h * HD:(h + 1) * HD, 6, 0:P], values(j, h),
                             probsT[:, (HEADS * t + h) % RING, j * P:(j + 1) * P],
                             start=(j == 0), stop=(j == blocks - 1))
    last.then_inc(A.out, 1)


def attend_out_scalar(act, K, A, t, oT):
    act.wait_ge(A.out, t + 1)
    if t >= 2:
        act.wait_ge(A.back, t - 1)
    act.activation(oT[:, t % 2, :], K.ps[:, 6, 0:P], ACT.Copy).then_inc(A.outT, 1)


def attend_back_tensor(pe, K, A, t, oT):
    pe.wait_ge(A.outT, t + 1)
    if t >= 1:
        pe.wait_ge(A.normed, t)
    pe.transpose(K.ps[:, 7, 0:P], oT[:, t % 2, :], K.ident).then_inc(A.back, 1)


def attend_tensor(pe, K, A, n, probs, probsT, oT, values, widths):
    units = HEADS * TILES
    if 2 <= n < units + 2:
        attend_turn_tensor(pe, K, A, n - 2, probs, widths[(n - 2) // HEADS])
    if n >= 6 and (n - 6) % HEADS == 0:
        t = (n - 6) // HEADS
        attend_values_tensor(pe, K, A, t, probsT, values, widths[t])
    if n >= 8 and (n - 8) % HEADS == 0:
        attend_back_tensor(pe, K, A, (n - 8) // HEADS, oT)


def attend_scale_vector(v, K, A, t, total, rtotal, out, link):
    v.wait_ge(A.back, t + 1)
    cols = slice(HEADS * t, HEADS * (t + 1))
    link(v.reciprocal(rtotal[:, cols], total[:, cols]))
    v.tensor_tensor(out.rearrange("p (h d) -> p h d", d=HD), K.ps[:, 7, 0:CH].rearrange("p (h d) -> p h d", d=HD),
                    rtotal[:, cols].unsqueeze(2).to_broadcast((P, HEADS, HD)), ALU.mult).then_inc(A.normed, 1)


def turned_count(widths, n, half):
    each = [min(HALVES, -(-widths[m // HEADS] // HALF)) for m in range(n + 1)]
    return sum(each[:n]) + min(half + 1, each[n])


def attend_copy(engine, copy, K, A, n, half, probsT, width, widths):
    engine.wait_ge(A.turned, turned_count(widths, n, half))
    if n >= RING:
        engine.wait_ge(A.out, n // HEADS - 1)
    cols = min(HALF, width - half * HALF)
    copy(probsT[:, n % RING, half * HALF:half * HALF + cols], K.ps[:, 4 + half, 0:cols]).then_inc((A.copied0, A.copied1)[half], 1)




def layer2_gnn(nc, K, sem, g):
    N, A, N2 = norm_sems(sem, "att"), attend_sems(sem, "att"), norm_sems(sem, "att_out")
    qkv_ps, qk_ready, v_ready = sem("att_qkv_ps"), sem("att_qk"), sem("att_v")
    zeroed = sem("att_zeroed")
    o_turned, oT_ready, mixed, chain = sem("att_o_turned"), sem("att_oT"), sem("att_mixed"), sem("att_chain2")
    UNITS = TILES * HEADS
    widths = [NODES] * TILES
    scale = float(np.float32(HD) ** np.float32(-0.5))
    with ExitStack() as c:
        def sb(name, shape, dt=F32):
            return c.enter_context(nc.sbuf_tensor("att_" + name, shape, dt))

        qT, kT = sb("qT", [P, HEADS, NODES]), sb("kT", [P, NODES])
        val = sb("v", [P, TILES, CH])
        shifted = sb("shifted", [P, 2, NODES])
        probs = sb("probs", [P, 2, NODES])
        probsT = sb("probsT", [P, RING, NODES])
        oT = sb("oT", [P, 2, P])
        top, ntop, total = sb("top", [P, UNITS]), sb("ntop", [P, UNITS]), sb("total", [P, UNITS])
        rtotal = sb("rtotal", [P, UNITS])
        out = sb("out", [P, TILES, CH])
        outT = sb("outT", [P, NODES])
        with nc.Block() as block:
            @block.gpsimd
            def _(pool):
                pool.memset(qT[:, :, :], 0.0).then_inc(zeroed, 1)

            @block.tensor
            def _(pe):
                turn_tensor(pe, K, K.xn, (0, 1), N.xn, N.turned)
                pe.wait_ge(N.xT, HALVES)
                for i, name in enumerate(("Wq", "Wk")):
                    for h in range(HALVES):
                        pe.matmul(K.ps[:, 2 + 2 * i + h, :], K.w(name), K.xnT[:, h * HALF:(h + 1) * HALF],
                                  start=True, stop=True).then_inc(qkv_ps, 1)
                for t in range(TILES):
                    last = pe.matmul(K.ps[:, 6 + t // 4, (t % 4) * P:(t % 4 + 1) * P], K.xnT[:, t * P:(t + 1) * P],
                                     K.w("Wv"), start=True, stop=True)
                last.then_inc(qkv_ps, 1)
                pe.wait_ge(qk_ready, 2 * HALVES)
                pe.wait_ge(v_ready, 1)
                for n in range(UNITS + 5):
                    if n < UNITS:
                        attend_scores_tensor(pe, K, A, n, qT, kT, NODES)
                    attend_tensor(pe, K, A, n, probs, probsT, oT, lambda j, h: val[:, j, h * HD:(h + 1) * HD],
                                  widths)
                turn_tensor(pe, K, out, (0, 1), A.normed, o_turned)
                for h in range(HALVES):
                    pe.wait_ge(oT_ready, h + 1)
                    for q in range(4):
                        t = 4 * h + q
                        last = pe.matmul(K.ps[:, 2 + h, q * P:(q + 1) * P], outT[:, t * P:(t + 1) * P], K.w("Wo"),
                                         start=True, stop=True)
                    last.then_inc(mixed, 1)

            @block.scalar
            def _(act):
                norm_scalar(act, K, N)
                turn_scalar(act, K, K.xnT, (0, 1), N.turned, N.xT)
                act.wait_ge(zeroed, 1)
                for h in range(HALVES):
                    act.wait_ge(qkv_ps, h + 1)
                    for head in range(HEADS):
                        rows = slice(head * HD, (head + 1) * HD)
                        last = act.activation(qT[rows, head, h * HALF:(h + 1) * HALF], K.ps[rows, 2 + h, :],
                                              ACT.Identity, bias=K.col("bq")[rows, :])
                    last.then_inc(qk_ready, 1)
                for h in range(HALVES):
                    act.wait_ge(qkv_ps, 2 + h + 1)
                    act.activation(kT[:, h * HALF:(h + 1) * HALF], K.ps[:, 4 + h, :], ACT.Identity,
                                   bias=K.col("bk")).then_inc(qk_ready, 1)
                for n in range(UNITS + 2):
                    if n < UNITS:
                        act.wait_ge(A.top, n + 1)
                        if n >= 2:
                            act.wait_ge(A.turned, HALVES * (n - 1))
                        act.activation(probs[:, n % 2, :], shifted[:, n % 2, :], ACT.Exp, bias=ntop[:, n:n + 1],
                                       scale=scale, accum_out=total[:, n:n + 1]).then_inc(A.probs, 1)
                    if 1 <= n <= UNITS:
                        attend_copy(act, lambda o, i: act.activation(o, i, ACT.Copy), K, A, n - 1, 0, probsT,
                                    NODES, widths)
                    if n >= 5 and (n - 5) % HEADS == 0:
                        attend_out_scalar(act, K, A, (n - 5) // HEADS, oT)
                turn_scalar(act, K, outT, (0, 1), o_turned, oT_ready)
                norm_scalar(act, K, N2)

            @block.vector
            def _(v):
                norm_vector(v, K, N, K.x, K.xn, LN_EPS)
                v.wait_ge(qkv_ps, 5)
                v.tensor_tensor(val[:, :, :], K.ps[:, 6:8, :].rearrange("p b (t c) -> p (b t) c", c=CH),
                                K.row("bv").unsqueeze(1).to_broadcast((P, TILES, CH)), ALU.add).then_inc(v_ready, 1)
                link = linker(v, A.chain)

                for n in range(UNITS + 5):
                    if n < UNITS:
                        t, h = n // HEADS, n % HEADS
                        v.wait_ge(A.scores, n + 1)
                        if n >= 2:
                            v.wait_ge(A.probs, n - 1)
                        b = 2 * (n % 2)
                        v.tensor_tensor_reduce(shifted[:, n % 2, :], K.ps[:, b:b + 2, :].rearrange("p b n -> p (b n)"),
                                               K.masked[:, t, :], 1.0, MASKED * 4, ALU.add, ALU.max,
                                               top[:, n:n + 1]).then_inc(A.shifted, 1)
                        v.wait_ge(A.shifted, n + 1)
                        v.tensor_scalar(ntop[:, n:n + 1], top[:, n:n + 1], -scale, None, ALU.mult).then_inc(A.top, 1)
                    if 2 <= n < UNITS + 2:
                        attend_copy(v, v.tensor_copy, K, A, n - 2, 1, probsT, NODES, widths)
                    if n >= 8 and (n - 8) % HEADS == 0:
                        t = (n - 8) // HEADS
                        attend_scale_vector(v, K, A, t, total, rtotal, out[:, t, :], link)
                link2 = linker(v, chain)
                for h in range(HALVES):
                    v.wait_ge(mixed, h + 1)
                    link2(v.tensor_tensor(K.xn[:, 4 * h:4 * h + 4, :],
                                          K.ps[:, 2 + h, :].rearrange("p (t c) -> p t c", t=4),
                                          K.row("bo").unsqueeze(1).to_broadcast((P, 4, CH)), ALU.add))
                norm_vector(v, K, N2, K.xn, out, LN_EPS)
                v.wait_ge(N2.xn, TILES)
                every = (P, TILES, CH)
                link2(v.tensor_tensor(out[:, :, :], out[:, :, :], K.row("gamma").unsqueeze(1).to_broadcast(every),
                                      ALU.mult))
                link2(v.tensor_tensor(out[:, :, :], out[:, :, :], K.row("beta").unsqueeze(1).to_broadcast(every),
                                      ALU.add))
                v.tensor_tensor(K.x[:, :, :], K.x[:, :, :], out[:, :, :], ALU.add)




def layer2_att(nc, K, sem, g):
    N, A, N2 = norm_sems(sem, "rot"), attend_sems(sem, "rot"), norm_sems(sem, "rot_rms")
    qkv_ps, rotated, v_ready, trig_in = sem("rot_qkv_ps"), sem("rot_qk"), sem("rot_v"), sem("rot_trig")
    zeroed = sem("rot_zeroed")
    o_turned, oT_ready, mixed, chain = sem("rot_o_turned"), sem("rot_oT"), sem("rot_mixed"), sem("rot_chain2")
    rope_chain = sem("rot_rope")
    UNITS = TILES * HEADS
    widths = [(t + 1) * P for t in range(TILES)]
    scale = float(1.0 / np.sqrt(np.float32(HD)))
    with ExitStack() as c:
        def sb(name, shape, dt=F32):
            return c.enter_context(nc.sbuf_tensor("rot_" + name, shape, dt))

        qT, kT, hT = sb("qT", [P, HEADS, NODES]), sb("kT", [P, NODES]), sb("hT", [P, NODES])
        trig = sb("trig", [P, 2, NODES])
        tmp = sb("tmp", [P, 2, HALF])
        val = sb("v", [P, TILES, 64])
        shifted = sb("shifted", [P, 2, NODES])
        probs = sb("probs", [P, 2, NODES])
        probsT = sb("probsT", [P, RING, NODES])
        oT = sb("oT", [P, 2, P])
        top, ntop, total = sb("top", [P, UNITS]), sb("ntop", [P, UNITS]), sb("total", [P, UNITS])
        rtotal = sb("rtotal", [P, UNITS])
        out = sb("out", [P, TILES, CH])
        outT = sb("outT", [P, NODES])
        with nc.Block() as block:
            @block.sync
            def _(sp):
                sp.dma_start(trig[:, :, :], K.d_trig.rearrange("p (i n) -> p i n", i=2)).then_inc(trig_in, 16)

            @block.gpsimd
            def _(pool):
                pool.memset(qT[:, :, :], 0.0).then_inc(zeroed, 1)

            @block.tensor
            def _(pe):
                turn_tensor(pe, K, out, (0, 1), N2.xn, N2.turned)
                pe.wait_ge(N2.xT, HALVES)
                for h in range(HALVES):
                    for i, name in enumerate(("wq", "wq_rot", "wk", "wk_rot")):
                        if h == 1:
                            pe.wait_ge(rotated, 1 + i // 2)
                        pe.matmul(K.ps[:, 2 + i, :], K.w(name), hT[:, h * HALF:(h + 1) * HALF],
                                  start=True, stop=True).then_inc(qkv_ps, 1)
                for t in range(TILES):
                    last = pe.matmul(K.ps[:, 6, t * 64:(t + 1) * 64], hT[:, t * P:(t + 1) * P], K.w("wv"),
                                     start=True, stop=True)
                last.then_inc(qkv_ps, 1)
                pe.wait_ge(rotated, 2 * HALVES)
                pe.wait_ge(v_ready, 1)
                for n in range(UNITS + 5):
                    if n < UNITS:
                        attend_scores_tensor(pe, K, A, n, qT, kT, widths[n // HEADS])
                    attend_tensor(pe, K, A, n, probs, probsT, oT,
                                  lambda j, h: val[:, j, (h // 2) * HD:(h // 2 + 1) * HD], widths)
                turn_tensor(pe, K, out, (0, 1), A.normed, o_turned)
                for h in range(HALVES):
                    pe.wait_ge(oT_ready, h + 1)
                    for q in range(4):
                        t = 4 * h + q
                        last = pe.matmul(K.ps[:, 2 + h, q * P:(q + 1) * P], outT[:, t * P:(t + 1) * P], K.w("wo"),
                                         start=True, stop=True)
                    last.then_inc(mixed, 1)

            @block.scalar
            def _(act):
                norm_scalar(act, K, N)
                norm_scalar(act, K, N2)
                turn_scalar(act, K, hT, (0, 1), N2.turned, N2.xT, scale=K.col("ln1"))
                act.wait_ge(qkv_ps, 4 * HALVES + 1)
                act.activation(val[:, :, :], K.ps[:, 6, :].rearrange("p (t c) -> p t c", c=64), ACT.Copy
                               ).then_inc(v_ready, 1)
                for n in range(UNITS + 2):
                    if n < UNITS:
                        width = widths[n // HEADS]
                        act.wait_ge(A.top, n + 1)
                        if n >= 2:
                            act.wait_ge(A.turned, turned_count(widths, n - 2, 1))
                        act.activation(probs[:, n % 2, 0:width], shifted[:, n % 2, 0:width], ACT.Exp,
                                       bias=ntop[:, n:n + 1], scale=scale, accum_out=total[:, n:n + 1]
                                       ).then_inc(A.probs, 1)
                    if 1 <= n <= UNITS:
                        attend_copy(act, lambda o, i: act.activation(o, i, ACT.Copy), K, A, n - 1, 0, probsT,
                                    widths[(n - 1) // HEADS], widths)
                    if n >= 5 and (n - 5) % HEADS == 0:
                        attend_out_scalar(act, K, A, (n - 5) // HEADS, oT)
                turn_scalar(act, K, outT, (0, 1), o_turned, oT_ready)

            @block.vector
            def _(v):
                norm_vector(v, K, N, K.x, K.xn, LN_EPS)
                v.wait_ge(N.xn, TILES)
                norm_vector(v, K, N2, K.xn, out, RMS_EPS, rms=True)
                v.wait_ge(trig_in, 16)
                rlink = linker(v, rope_chain)
                for h in range(HALVES):
                    cols = slice(h * HALF, (h + 1) * HALF)
                    for i in range(2):
                        v.wait_ge(qkv_ps, 4 * h + 2 * i + 2)
                        v.tensor_tensor(tmp[:, 0, :], K.ps[:, 3 + 2 * i, :], trig[:, 1, cols], ALU.mult)
                        rlink(v.tensor_tensor(tmp[:, 1, :], K.ps[:, 2 + 2 * i, :], trig[:, 0, cols], ALU.mult))
                        if i == 1:
                            last = v.tensor_tensor(kT[:, cols], tmp[:, 0, :], tmp[:, 1, :], ALU.add)
                        else:
                            v.wait_ge(zeroed, 1)
                            for head in range(HEADS):
                                rows = slice(head * HD, (head + 1) * HD)
                                last = v.tensor_tensor(qT[rows, head, cols], tmp[rows, 0, :], tmp[rows, 1, :], ALU.add)
                        last.then_inc(rotated, 1)
                        v.wait_ge(rotated, 2 * h + i + 1)
                link = linker(v, A.chain)

                for n in range(UNITS + 5):
                    if n < UNITS:
                        t, h = n // HEADS, n % HEADS
                        width = widths[t]
                        v.wait_ge(A.scores, n + 1)
                        if n >= 2:
                            v.wait_ge(A.probs, n - 1)
                        b = 2 * (n % 2)
                        v.tensor_tensor_reduce(shifted[:, n % 2, 0:width],
                                               K.ps[:, b:b + 2, :].rearrange("p b n -> p (b n)")[:, 0:width],
                                               K.causal[:, NODES - width:NODES], 1.0, MASKED * 4, ALU.add, ALU.max,
                                               top[:, n:n + 1]).then_inc(A.shifted, 1)
                        v.wait_ge(A.shifted, n + 1)
                        v.tensor_scalar(ntop[:, n:n + 1], top[:, n:n + 1], -scale, None, ALU.mult).then_inc(A.top, 1)
                    if 2 <= n < UNITS + 2:
                        m = n - 2
                        if widths[m // HEADS] > HALF:
                            attend_copy(v, v.tensor_copy, K, A, m, 1, probsT, widths[m // HEADS], widths)
                        else:
                            v.engine_nop().then_inc(A.copied1, 1)
                    if n >= 8 and (n - 8) % HEADS == 0:
                        t = (n - 8) // HEADS
                        attend_scale_vector(v, K, A, t, total, rtotal, out[:, t, :], link)
                link2 = linker(v, chain)
                for h in range(HALVES):
                    v.wait_ge(mixed, h + 1)
                    xh = K.xn[:, 4 * h:4 * h + 4, :]
                    link2(v.tensor_tensor(xh, xh, K.ps[:, 2 + h, :].rearrange("p (t c) -> p t c", t=4), ALU.add))
                v.tensor_tensor(K.x[:, :, :], K.x[:, :, :], K.xn[:, :, :], ALU.add)




def layer2_moe(nc, K, sem, g, g_next, G):
    N, R = norm_sems(sem, "glu"), router_sems(sem, "glu")
    w_in, a_ps, b_ps, silu, hid, y_ps = (sem(f"glu_{n}") for n in ("w_in", "a_ps", "b_ps", "silu", "hid", "y_ps"))
    chain, index_chain, turned_back = sem("glu_chain"), sem("glu_index"), sem("glu_turned_back")
    jobs = [(e, h) for e in range(L2_E) for h in range(HALVES)]
    J, C = len(jobs), len(HID_CHUNKS)
    with ExitStack() as c:
        w = c.enter_context(nc.sbuf_tensor("glu_w", [P, 2, EXP2], F32))
        a = c.enter_context(nc.sbuf_tensor("glu_a", [P, 2, HALF], F32))
        hidden = c.enter_context(nc.sbuf_tensor("glu_hid", [P, 2, C, HALF], F32))
        rms = c.enter_context(nc.sbuf_tensor("glu_rms", [P, TILES, CH], F32))
        accT = c.enter_context(nc.sbuf_tensor("glu_accT", [P, NODES], F32))
        tmp = c.enter_context(nc.sbuf_tensor("glu_tmp", [P, HALF], F32))
        with nc.Block() as block:
            @block.sync
            def _(sp):
                for e in range(2):
                    sp.dma_start(w[:, e, :], K.d_exp2[e, :, :]).then_inc(w_in, 16)
                    sp.wait_ge(w_in, 16 * (e + 1))
                next_rows_sync(sp, K, G, g_next)
                for t in range(TILES):
                    next_adj_sync(sp, K, G, g_next, t)
                    e = t + 2
                    if e < L2_E:
                        sp.wait_ge(y_ps, HALVES * (e - 1))
                        sp.dma_start(w[:, e % 2, :], K.d_exp2[e, :, :]).then_inc(w_in, 16)

            @block.tensor
            def _(pe):
                turn_tensor(pe, K, rms, (4, 5), N.xn, N.turned)
                pe.wait_ge(N.xT, HALVES)
                router_tensor(pe, K, R, K.w("router"), L2_E)

                def up(n, m):
                    e, h = jobs[n]
                    at, wide = HID_CHUNKS[m]
                    i = n * C + m
                    pe.wait_ge(w_in, 16 * (e + 1))
                    for off, base, done in ((0, 0, a_ps), (HID, 2, b_ps)):
                        if i >= 2:
                            pe.wait_ge(hid, i - 1)
                        pe.matmul(K.ps[0:wide, base + i % 2, :], w[:, e % 2, off + at:off + at + wide],
                                  K.xnT[:, h * HALF:(h + 1) * HALF], start=True, stop=True).then_inc(done, 1)

                def down(n):
                    e, h = jobs[n]
                    if n == 0:
                        gates_tensor(pe, K, R)
                    spread_gate_tensor(pe, K, R, n, e, h)
                    pe.wait_ge(hid, C * (n + 1))
                    if n >= 2:
                        pe.wait_ge(R.used, n - 1)
                    for m, (at, wide) in enumerate(HID_CHUNKS):
                        last = pe.matmul(K.ps[:, 4 + n % 2, :], w[0:wide, e % 2, 2 * HID + m * P:2 * HID + (m + 1) * P],
                                         hidden[0:wide, n % 2, m, :], start=(m == 0), stop=(m == C - 1))
                    last.then_inc(y_ps, 1)

                for n in range(J):
                    for m in range(C):
                        up(n, m)
                        if m == 1 and n >= 1:
                            down(n - 1)
                down(J - 1)
                turn_back_tensor(pe, K, accT, (0, 1), chain, (J - 1, J), turned_back)

            @block.scalar
            def _(act):
                norm_scalar(act, K, N)
                turn_scalar(act, K, K.xnT, (4, 5), N.turned, N.xT, scale=K.col("ln2"))
                router_scalar(act, K, R, L2_E, "floor")
                for n in range(J + 1):
                    for m in range(C):
                        if n < J:
                            i = n * C + m
                            wide = HID_CHUNKS[m][1]
                            act.wait_ge(a_ps, i + 1)
                            if i >= 2:
                                act.wait_ge(hid, i - 1)
                            act.activation(a[0:wide, i % 2, :], K.ps[0:wide, i % 2, :], ACT.Silu).then_inc(silu, 1)
                        if m == 1 and n >= 1:
                            if n == 1:
                                gates_scalar(act, K, R)
                                next_rows_scalar(act, K, G)
                            spread_gate_scalar(act, K, R, n - 1)

            @block.vector
            def _(v):
                norm_vector(v, K, N, K.xn, rms, RMS_EPS, rms=True)
                router_vector(v, K, R, L2_E, None, "floor")
                link, ilink = linker(v, chain), linker(v, index_chain)
                v.memset(accT[:, :], 0.0).then_inc(R.chain, 1)

                def add(n):
                    e, h = jobs[n]
                    v.wait_ge(y_ps, n + 1)
                    v.wait_ge(R.spread_out, n + 1)
                    v.tensor_tensor(tmp[:, :], K.ps[:, 4 + n % 2, :], K.wb[:, n % 2, :], ALU.mult).then_inc(R.used, 1)
                    v.wait_ge(R.used, n + 1)
                    acc = accT[:, h * HALF:(h + 1) * HALF]
                    link(v.tensor_tensor(acc, acc, tmp[:, :], ALU.add))

                for n in range(J):
                    for m in range(C):
                        i = n * C + m
                        wide = HID_CHUNKS[m][1]
                        v.wait_ge(silu, i + 1)
                        v.wait_ge(b_ps, i + 1)
                        if m == 0 and n >= 2:
                            v.wait_ge(y_ps, n - 1)
                        v.tensor_tensor(hidden[0:wide, n % 2, m, :], a[0:wide, i % 2, :], K.ps[0:wide, 2 + i % 2, :],
                                        ALU.mult).then_inc(hid, 1)
                    if n == 0:
                        next_rows_vector(v, K, G)
                    if n >= 1:
                        add(n - 1)
                    if n % HALVES == 1:
                        next_index_vector(v, K, G, n // HALVES, ilink)
                add(J - 1)
                turn_back_vector(v, K, (0, 1), turned_back)




def layer3_gnn(nc, K, sem, g, G):
    N, A = norm_sems(sem, "gat"), attend_sems(sem, "gat")
    names = ("h_ps", "hT", "val", "src_ps", "src", "dst_w", "dst_ps", "dst", "first", "both", "pool_chain", "logit")
    S = named_sems(sem, "gat", names)
    UNITS = TILES * HEADS
    widths = [NODES] * TILES
    with ExitStack() as c:
        def sb(name, shape, dt=F32):
            return c.enter_context(nc.sbuf_tensor("gat_" + name, shape, dt))

        hT = sb("hT", [P, NODES])
        val = sb("v", [P, TILES, CH])
        dstw = sb("dstw", [P, HEADS, P])
        dst = sb("dst", [P, HEADS, NODES])
        src = sb("src", [P, UNITS])
        shifted = sb("shifted", [P, 2, NODES])
        steep = sb("steep", [P, NODES])
        flat = sb("flat", [P, NODES])
        probs = sb("probs", [P, 2, NODES])
        probsT = sb("probsT", [P, RING, NODES])
        oT = sb("oT", [P, 2, P])
        top, z, topv = sb("top", [P, UNITS]), sb("z", [P, UNITS]), sb("topv", [P, UNITS])
        b1, b2 = sb("b1", [P, UNITS]), sb("b2", [P, UNITS])
        total, rtotal = sb("total", [P, UNITS]), sb("rtotal", [P, UNITS])
        res = sb("res", [P, CH])
        with nc.Block() as block:
            @block.gpsimd
            def _(pool):
                for t in range(TILES // 2):
                    gather_pool(pool, K, G, t)

            @block.tensor
            def _(pe):
                turn_tensor(pe, K, K.xn, (0, 1), N.xn, N.turned)
                pe.wait_ge(N.xT, HALVES)
                for h in range(HALVES):
                    pe.matmul(K.ps[:, 2 + h, :], K.w("gatW"), K.xnT[:, h * HALF:(h + 1) * HALF],
                              start=True, stop=True).then_inc(S.h_ps, 1)
                for t in range(TILES):
                    last = pe.matmul(K.ps[:, 4 + t // 4, (t % 4) * P:(t % 4 + 1) * P], K.xnT[:, t * P:(t + 1) * P],
                                     K.w("gatW"), start=True, stop=True)
                last.then_inc(S.h_ps, 1)
                pe.wait_ge(S.hT, HALVES)
                for t in range(TILES):
                    last = pe.matmul(K.ps[:, 6, t * HEADS:(t + 1) * HEADS], hT[:, t * P:(t + 1) * P], K.col("a_src"),
                                     start=True, stop=True)
                last.then_inc(S.src_ps, 1)
                pe.wait_ge(S.dst_w, 1)
                for h in range(HEADS):
                    for q in range(HALVES):
                        n = HALVES * h + q
                        if n >= 4:
                            pe.wait_ge(S.dst, n - 3)
                        pe.matmul(K.ps[:, n % 4, :], dstw[:, h, :], hT[:, q * HALF:(q + 1) * HALF],
                                  start=True, stop=True).then_inc(S.dst_ps, 1)
                pe.wait_ge(S.val, 1)
                pe.wait_ge(S.src, 1)
                for n in range(2, UNITS + 5):
                    attend_tensor(pe, K, A, n, probs, probsT, oT, lambda j, h: val[:, j, h * HD:(h + 1) * HD],
                                  widths)

            @block.scalar
            def _(act):
                norm_scalar(act, K, N)
                turn_scalar(act, K, K.xnT, (0, 1), N.turned, N.xT)
                for h in range(HALVES):
                    act.wait_ge(S.h_ps, h + 1)
                    act.activation(hT[:, h * HALF:(h + 1) * HALF], K.ps[:, 2 + h, :], ACT.Identity,
                                   bias=K.col("gat_b")).then_inc(S.hT, 1)
                for n in range(HALVES * HEADS):
                    act.wait_ge(S.dst_ps, n + 1)
                    act.activation(dst[:, n // 2, (n % 2) * HALF:(n % 2 + 1) * HALF], K.ps[:, n % 4, :], ACT.Copy
                                   ).then_inc(S.dst, 1)
                for n in range(UNITS + 3):
                    if n >= 6 and (n - 6) % HEADS == 0:
                        attend_out_scalar(act, K, A, (n - 6) // HEADS, oT)
                    if 2 <= n < UNITS + 2:
                        for half in range(HALVES):
                            attend_copy(act, lambda o, i: act.activation(o, i, ACT.Copy), K, A, n - 2, half, probsT,
                                        NODES, widths)
                    if n < UNITS:
                        act.wait_ge(A.top, n + 1)
                        if n >= 1:
                            act.wait_ge(A.probs, n)
                        act.activation(steep[:, :], shifted[:, n % 2, :], ACT.Exp, bias=b1[:, n:n + 1])
                        act.activation(flat[:, :], shifted[:, n % 2, :], ACT.Exp, bias=b2[:, n:n + 1], scale=0.2
                                       ).then_inc(S.both, 1)

            @block.vector
            def _(v):
                norm_vector(v, K, N, K.x, K.xn, LN_EPS)
                for h in range(HEADS):
                    last = v.tensor_scalar(dstw[:, h, :], K.ones, K.col("a_dst")[:, h:h + 1], None, ALU.mult)
                last.then_inc(S.dst_w, 1)
                v.wait_ge(S.h_ps, HALVES + 1)
                for b in range(HALVES):
                    last = v.tensor_tensor(val[:, 4 * b:4 * b + 4, :], K.ps[:, 4 + b, :].rearrange("p (t c) -> p t c", t=4),
                                           K.row("gat_brow").unsqueeze(1).to_broadcast((P, 4, CH)), ALU.add)
                last.then_inc(S.val, 1)
                v.wait_ge(S.src_ps, 1)
                v.tensor_copy(src[:, :], K.ps[:, 6, 0:UNITS]).then_inc(S.src, 1)
                v.wait_ge(S.src, 1)
                link, glink = linker(v, A.chain), linker(v, S.pool_chain)

                def finish(t):
                    attend_scale_vector(v, K, A, t, total, rtotal, res[:, :], link)
                    v.wait_ge(A.normed, t + 1)
                    link(v.tensor_tensor(K.x[:, t, :], K.x[:, t, :], res[:, :], ALU.add))

                def first(n):
                    t, h = n // HEADS, n % HEADS
                    if h == 0 and t == 0:
                        v.wait_ge(S.dst, HALVES * HEADS)
                    if n >= 2:
                        v.wait_ge(S.both, n - 1)
                    col = slice(n, n + 1)
                    v.tensor_tensor_reduce(shifted[:, n % 2, :], dst[:, h, :], K.masked[:, t, :], 1.0, MASKED * 4,
                                           ALU.add, ALU.max, top[:, col]).then_inc(A.shifted, 1)
                    v.wait_ge(A.shifted, n + 1)
                    link(v.tensor_tensor(z[:, col], top[:, col], src[:, col], ALU.add))
                    link(v.scalar_tensor_tensor(out=topv[:, col], in0=z[:, col], scalar=0.2, in1=z[:, col],
                                                op0=ALU.mult, op1=ALU.max))
                    v.tensor_tensor(b1[:, col], src[:, col], topv[:, col], ALU.subtract)
                    v.scalar_tensor_tensor(out=b2[:, col], in0=src[:, col], scalar=0.2, in1=topv[:, col],
                                           op0=ALU.mult, op1=ALU.subtract).then_inc(A.top, 1)

                first(0)
                first(1)
                for n in range(UNITS + 3):
                    if n < UNITS:
                        v.wait_ge(S.both, n + 1)
                        if n >= 2:
                            v.wait_ge(A.turned, HALVES * (n - 1))
                        v.scalar_tensor_tensor(out=probs[:, n % 2, :], in0=steep[:, :], scalar=1.0, in1=flat[:, :],
                                               op0=ALU.mult, op1=ALU.max, accum_out=total[:, n:n + 1]
                                               ).then_inc(A.probs, 1)
                    if n + 2 < UNITS:
                        first(n + 2)
                    if n >= 6 and (n - 6) % HEADS == 0:
                        t = (n - 6) // HEADS
                        finish(t)
                        if t % 2 == 1:
                            pool_max_vector(v, K, G, t // 2, glink)




def layer3_ffn(nc, K, sem, g, G):
    N, N2, R = norm_sems(sem, "gel"), norm_sems(sem, "gel_in"), router_sems(sem, "gel")
    w_in, up_ps, hid, y_ps, xe = (sem(f"gel_{n}") for n in ("w_in", "up_ps", "hid", "y_ps", "xe"))
    chain, pool_chain, turned_back, out_ready, out_done = (sem(f"gel_{n}") for n in (
        "chain", "pool", "turned_back", "out_ready", "out_done"))
    jobs = [(e, h) for e in range(L3_E) for h in range(HALVES)]
    J, C = len(jobs), L3_HID // P
    with ExitStack() as c:
        w = c.enter_context(nc.sbuf_tensor("gel_w", [P, 2, EXP3], F32))
        hidden = c.enter_context(nc.sbuf_tensor("gel_hid", [P, 2, C, HALF], F32))
        xt2 = c.enter_context(nc.sbuf_tensor("gel_xt2", [P, TILES, CH], F32))
        x2T = c.enter_context(nc.sbuf_tensor("gel_x2T", [P, NODES], F32))
        xeT = c.enter_context(nc.sbuf_tensor("gel_xeT", [P, 2, HALF], F32))
        accT = c.enter_context(nc.sbuf_tensor("gel_accT", [P, NODES], F32))
        tmp = c.enter_context(nc.sbuf_tensor("gel_tmp", [P, HALF], F32))
        with nc.Block() as block:
            @block.sync
            def _(sp):
                for e in range(L3_E):
                    if e >= 2:
                        sp.wait_ge(y_ps, HALVES * (e - 1))
                    if e >= 1:
                        sp.wait_ge(w_in, 16 * e)
                    sp.dma_start(w[:, e % 2, :], K.d_exp3[e, :, :]).then_inc(w_in, 16)
                sp.wait_ge(out_ready, 1)
                sp.dma_start(K.d_out[g, :, :].rearrange("(t p) c -> p t c", p=P), K.x[:, :, :]).then_inc(out_done, 16)
                sp.wait_ge(out_done, 16)

            @block.gpsimd
            def _(pool):
                for t in range(TILES // 2, TILES):
                    gather_pool(pool, K, G, t)

            @block.tensor
            def _(pe):
                turn_tensor(pe, K, K.xn, (4, 5), N.xn, N.turned)
                pe.wait_ge(N.xT, HALVES)
                router_tensor(pe, K, R, K.w("Wr"), L3_E)
                turn_tensor(pe, K, xt2, (0, 1), N2.xn, N2.turned)

                def up(n, m):
                    e, h = jobs[n]
                    i = n * C + m
                    if m == 0:
                        pe.wait_ge(w_in, 16 * (e + 1))
                        pe.wait_ge(xe, n + 1)
                    if i >= 4:
                        pe.wait_ge(hid, i - 3)
                    pe.matmul(K.ps[:, i % 4, :], w[:, e % 2, m * P:(m + 1) * P], xeT[:, n % 2, :],
                              start=True, stop=True).then_inc(up_ps, 1)

                def down(n):
                    e, h = jobs[n]
                    if n == 0:
                        gates_tensor(pe, K, R)
                    spread_gate_tensor(pe, K, R, n, e, h)
                    pe.wait_ge(hid, C * (n + 1))
                    if n >= 2:
                        pe.wait_ge(R.used, n - 1)
                    for m in range(C):
                        last = pe.matmul(K.ps[:, 4 + n % 2, :], w[:, e % 2, L3_HID + m * P:L3_HID + (m + 1) * P],
                                         hidden[:, n % 2, m, :], start=(m == 0), stop=(m == C - 1))
                    last.then_inc(y_ps, 1)

                for n in range(J):
                    for m in range(C):
                        up(n, m)
                        if m == 1 and n >= 1:
                            down(n - 1)
                down(J - 1)
                turn_back_tensor(pe, K, accT, (0, 1), chain, (J - 1, J), turned_back)

            @block.scalar
            def _(act):
                norm_scalar(act, K, N)
                turn_scalar(act, K, K.xnT, (4, 5), N.turned, N.xT)
                norm_scalar(act, K, N2)
                turn_scalar(act, K, x2T, (0, 1), N2.turned, N2.xT)
                router_scalar(act, K, R, L3_E, "sum")

                def scale_in(n):
                    e, h = jobs[n]
                    if n == 0:
                        act.wait_ge(N2.xT, HALVES)
                    if n >= 2:
                        act.wait_ge(up_ps, C * (n - 1))
                    act.activation(xeT[:, n % 2, :], x2T[:, h * HALF:(h + 1) * HALF], ACT.Identity,
                                   scale=K.col("ln_g")[:, e:e + 1], bias=K.col("ln_b")[:, e:e + 1]).then_inc(xe, 1)

                scale_in(0)
                for n in range(J + 1):
                    if n + 1 < J:
                        scale_in(n + 1)
                    for m in range(C):
                        if n < J:
                            e = jobs[n][0]
                            i = n * C + m
                            act.wait_ge(up_ps, i + 1)
                            if m == 0 and n >= 2:
                                act.wait_ge(y_ps, n - 1)
                            act.activation(hidden[:, n % 2, m, :], K.ps[:, i % 4, :], ACT.Gelu,
                                           bias=K.col("b1")[:, e * C + m:e * C + m + 1]).then_inc(hid, 1)
                        if m == 1 and n >= 1:
                            if n == 1:
                                gates_scalar(act, K, R)
                            spread_gate_scalar(act, K, R, n - 1)

            @block.vector
            def _(v):
                norm_vector(v, K, N, K.x, K.xn, LN_EPS)
                v.wait_ge(N.xn, TILES)
                norm_vector(v, K, N2, K.xn, xt2, LN_EPS)
                router_vector(v, K, R, L3_E, K.row("br"), "sum")
                link, glink = linker(v, chain), linker(v, pool_chain)
                v.memset(accT[:, :], 0.0).then_inc(R.chain, 1)
                for n, (e, h) in enumerate(jobs):
                    v.wait_ge(y_ps, n + 1)
                    v.wait_ge(R.spread_out, n + 1)
                    v.scalar_tensor_tensor(out=tmp[:, :], in0=K.ps[:, 4 + n % 2, :], scalar=K.col("b2")[:, e:e + 1],
                                           in1=K.wb[:, n % 2, :], op0=ALU.add, op1=ALU.mult).then_inc(R.used, 1)
                    v.wait_ge(R.used, n + 1)
                    acc = accT[:, h * HALF:(h + 1) * HALF]
                    link(v.tensor_tensor(acc, acc, tmp[:, :], ALU.add))
                    if n % 4 == 3:
                        pool_max_vector(v, K, G, TILES // 2 + n // 4, glink)
                turn_back_vector(v, K, (0, 1), turned_back)
                v.engine_nop().then_inc(out_ready, 1)




def prologue(nc, K, sem, G):
    loaded, made = sem("loaded"), sem("made")
    chain, pool_chain = sem("start_chain"), sem("start_pool")
    with nc.Block() as block:
        @block.sync
        def _(sp):
            for dst, src in ((K.w_all, K.d_weights), (K.c_all, K.d_cols), (K.consts, K.d_consts)):
                sp.dma_start(dst[:, :], src).then_inc(loaded, 16)
            sp.dma_start(K.r_all[:, :], K.d_rowvecs.to_broadcast((P, sizes(ROWS)))).then_inc(loaded, 16)
            sp.wait_ge(made, 1)
            next_rows_sync(sp, K, G, 0)
            for t in range(TILES):
                next_adj_sync(sp, K, G, 0, t)

        @block.scalar
        def _(act):
            next_rows_scalar(act, K, G)

        @block.gpsimd
        def _(pool):
            pool.wait_ge(made, 2)
            for t in range(TILES):
                gather_pool(pool, K, G, t)

        @block.vector
        def _(v):
            v.memset(K.zero_row[:, :], 0.0).then_inc(made, 1)
            v.memset(K.causal[:, 0:NODES - P], 0.0)
            v.memset(K.ones_bf[:, :], 1.0)
            v.memset(K.ones32[:, :], 1.0)
            v.wait_ge(loaded, 64)
            link = linker(v, chain)
            link(v.tensor_tensor(K.causal32[:, :], K.le, K.ident, ALU.subtract))
            link(v.tensor_scalar(K.causal[:, NODES - P:NODES], K.causal32[:, :], MASKED, None, ALU.mult))
            next_rows_vector(v, K, G)
            for t in range(TILES):
                next_index_vector(v, K, G, t, link)
            v.engine_nop().then_inc(made, 1)
            plink = linker(v, pool_chain)
            for t in range(TILES):
                pool_max_vector(v, K, G, t, plink)


@contextmanager
def neighbour_memory(nc, K, when):
    with nc.sbuf_tensor(f"{when}_neigh", [P, 2, NEIGH, CH], F32) as K.neigh:
        yield


@contextmanager
def ranking_memory(nc, K, when):
    with (nc.sbuf_tensor(f"{when}_xg", [P, TILES, CH], F32) as K.xg,
          nc.sbuf_tensor(f"{when}_adj_next", [P, NODES], I32) as K.adj_next,
          nc.sbuf_tensor(f"{when}_ranks", [P, NODES], F32) as K.ranks):
        yield


def gather_sems(sem, name):
    names = ("x_in", "norm_chain", "var", "std", "xn", "rows", "adj_in", "ranked", "pooled", "gathered")
    one = [sem(f"{name}_{n}") for n in names[:-1]]
    return namedtuple("Semaphores", names)(*one, [sem(f"{name}_gathered{i}") for i in range(2)])


def program(nc, d_x, d_adj, d_weights, d_cols, d_rowvecs, d_consts, d_trig, d_exp2, d_exp3, d_out,
            graphs=GRAPHS):
    K = Memory()
    K.d_x, K.d_adj, K.d_weights, K.d_cols, K.d_rowvecs = d_x, d_adj, d_weights, d_cols, d_rowvecs
    K.d_consts, K.d_trig, K.d_exp2, K.d_exp3, K.d_out = d_consts, d_trig, d_exp2, d_exp3, d_out
    K.d_rows = nc.dram_tensor("normalised_rows", (NODES + 1, CH), F32, kind="Internal").ap()
    with ExitStack() as c:
        def sb(name, shape, dt=F32):
            return c.enter_context(nc.sbuf_tensor(name, shape, dt))

        K.ps = c.enter_context(nc.psum_tensor("banks", [P, 8, HALF], F32))
        K.x, K.xn, K.xnT = sb("x", [P, TILES, CH]), sb("xn", [P, TILES, CH]), sb("xnT", [P, NODES])
        K.adj, K.masked = sb("adj", [P, TILES, NODES], BF16), sb("masked", [P, TILES, NODES], BF16)
        K.w_all, K.c_all = sb("weights", [P, sizes(WEIGHTS)]), sb("cols", [P, sizes(COLS)])
        K.r_all, K.consts = sb("rowvecs", [P, sizes(ROWS)]), sb("consts", [P, sizes(CONSTS)])
        K.ones32 = sb("ones32", [P, P])
        K.ones_bf = sb("ones_bf", [P, P], BF16)
        K.causal, K.causal32 = sb("causal", [P, NODES], BF16), sb("causal32", [P, P])
        K.zero_row = sb("zero_row", [1, CH])
        K.stats, K.mv = sb("stats", [P, TILES, 6]), sb("mv", [P, TILES, 2])
        K.veps, K.std, K.rstd, K.nsq = (sb(n, [P, TILES]) for n in ("veps", "std", "rstd", "nsq"))
        K.prob, K.top, K.gate, K.gate2, K.logit = (sb(n, [P, TILES, 8]) for n in ("prob", "top", "gate", "gate2",
                                                                                 "logit"))
        K.topi, K.topf = sb("topi", [P, TILES, 8], U32), sb("topf", [P, TILES, 2])
        K.r1, K.r2, K.w1, K.w2 = (sb(n, [P, TILES]) for n in ("r1", "r2", "w1", "w2"))
        K.gateT = sb("gateT", [8, NODES])
        K.wb = sb("wb", [P, 2, HALF])
        K.agg = sb("agg", [P, TILES, CH])
        K.g_stats, K.g_mv = sb("g_stats", [P, TILES, 6]), sb("g_mv", [P, TILES, 2])
        K.g_veps, K.g_std, K.g_rstd = (sb(n, [P, TILES]) for n in ("g_veps", "g_std", "g_rstd"))
        K.first, K.floor = sb("first", [P, SLOTS]), sb("floor", [P, TILES])
        K.idx, K.aggraw = sb("idx", [P, TILES, SLOTS], U32), sb("aggraw", [P, CH])

        def named(tensor, table):
            at = offsets(table)[0]
            return lambda name: tensor[:, at[name][0]:at[name][0] + at[name][1]]

        K.w, K.col, K.row = named(K.w_all, WEIGHTS), named(K.c_all, COLS), named(K.r_all, ROWS)
        const = named(K.consts, CONSTS)
        K.ident, K.le, K.gt = const("ident"), const("le"), const("gt")
        K.onehot = const("onehot")[0:8, :]
        K.ones = K.ones32[:, :]

        with semaphores(nc, gathers=True) as sem, neighbour_memory(nc, K, "start"), \
                ranking_memory(nc, K, "start"):
            prologue(nc, K, sem, gather_sems(sem, "start"))
        with nc.Fori(0, graphs) as g:
            g_next = (g + 1) % graphs
            with semaphores(nc) as sem:
                layer0_gnn(nc, K, sem, g)
                layer0_ffn(nc, K, sem, g)
                layer1_gnn(nc, K, sem, g)
                layer1_ffn(nc, K, sem, g)
                layer2_gnn(nc, K, sem, g)
            with semaphores(nc, gathers=True) as sem:
                G = gather_sems(sem, "next")
                layer2_att(nc, K, sem, g)
                with neighbour_memory(nc, K, "next"):
                    with ranking_memory(nc, K, "next"):
                        layer2_moe(nc, K, sem, g, g_next, G)
                    layer3_gnn(nc, K, sem, g, G)
                    layer3_ffn(nc, K, sem, g, G)




def laid_out(i):
    f = np.float32

    def pack(table, parts, rows):
        cols = []
        for name, n in table:
            a = parts[name]
            a = a.reshape(a.shape[0], -1)
            out = np.zeros((rows, n), f)
            out[:a.shape[0]] = a
            cols.append(out)
        return np.concatenate(cols, 1)

    w_in = i["L1_ffn_W_in"]
    zx = [0, M_INNER, 2 * M_INNER, 2 * M_INNER + M_STATE, 2 * M_INNER + 2 * M_STATE, w_in.shape[1]]
    half = HD // 2

    def rotated(w):
        h = w.reshape(-1, 2, half, CH)
        return np.concatenate([h[:, 1:], h[:, :1]], 1).reshape(w.shape)

    wk = np.repeat(i["L2_ffn_wk"].reshape(2, 1, HD, CH), 2, 1).reshape(CH, CH)
    parts = {
        "l0_top": i["L0_gnn_W"][:CH], "l0_bot": i["L0_gnn_W"][CH:],
        "sW1": i["L0_ffn_sW1"], "sW2": i["L0_ffn_sW2"], "sW3": i["L0_ffn_sW3"],
        "eW1": i["L0_ffn_eW1"].transpose(1, 0, 2), "eW2": i["L0_ffn_eW2"].transpose(1, 0, 2),
        "eW3": i["L0_ffn_eW3"].transpose(1, 0, 2), "gW": i["L0_ffn_gW"],
        "msg": i["L1_gnn_W_msg"], "upd": i["L1_gnn_W_upd"],
        "W_z": w_in[:, zx[0]:zx[1]], "W_xh": w_in[:, zx[1]:zx[2]], "W_B": w_in[:, zx[2]:zx[3]],
        "W_C": w_in[:, zx[3]:zx[4]], "W_dt": w_in[:, zx[4]:zx[5]],
        "W_out": i["L1_ffn_W_out"].reshape(2, CH, CH).transpose(1, 0, 2), "W_lin": i["L1_ffn_W_lin"],
        "Wq": i["L2_gnn_Wq"].T, "Wk": i["L2_gnn_Wk"].T, "Wv": i["L2_gnn_Wv"].T, "Wo": i["L2_gnn_Wo"].T,
        "wq": i["L2_ffn_wq"].T, "wq_rot": rotated(i["L2_ffn_wq"]).T, "wk": wk.T, "wk_rot": rotated(wk).T,
        "wv": i["L2_ffn_wv"].T, "wo": i["L2_ffn_wo"].T, "router": i["L2_ffn_router_w"].T,
        "gatW": i["L3_gnn_W"].T, "Wr": i["L3_ffn_Wr"],
    }
    weights = pack(WEIGHTS, parts, P)

    conv_w, conv_b = i["L1_ffn_conv_w"], i["L1_ffn_conv_b"]
    a = i["L3_gnn_a"]
    a_src, a_dst = np.zeros((CH, HEADS), f), np.zeros((CH, HEADS), f)
    for h in range(HEADS):
        a_src[h * HD:(h + 1) * HD, h] = a[h, :HD]
        a_dst[h * HD:(h + 1) * HD, h] = a[h, HD:]
    one = lambda v: v.reshape(-1, 1)
    cols = pack(COLS, {
        "sb1": one(i["L0_ffn_sb1"]), "sb2": one(i["L0_ffn_sb2"]), "sb3": one(i["L0_ffn_sb3"]),
        "eb1": i["L0_ffn_eb1"].T, "eb2": i["L0_ffn_eb2"].T, "eb3": i["L0_ffn_eb3"].T, "gnn_bias": one(i["L1_gnn_bias"]),
        "conv_xh": conv_w[:M_INNER].reshape(2, CH, M_CONV).transpose(1, 0, 2),
        "conv_B": conv_w[M_INNER:M_INNER + M_STATE], "conv_C": conv_w[M_INNER + M_STATE:],
        "convb_xh": conv_b[:M_INNER].reshape(2, CH).T, "convb_B": one(conv_b[M_INNER:M_INNER + M_STATE]),
        "convb_C": one(conv_b[M_INNER + M_STATE:]), "norm_w": i["L1_ffn_norm_w"].reshape(2, CH).T,
        "bq": one(i["L2_gnn_bq"]), "bk": one(i["L2_gnn_bk"]), "ln1": one(i["L2_ffn_ln1_w"]),
        "ln2": one(i["L2_ffn_ln2_w"]), "gat_b": one(i["L3_gnn_b"]), "a_src": a_src, "a_dst": a_dst,
        "ln_g": i["L3_ffn_ln_g"].T, "ln_b": i["L3_ffn_ln_b"].T,
        "b1": i["L3_ffn_b1"].reshape(L3_E, 4, CH).transpose(2, 0, 1), "b2": i["L3_ffn_b2"].T,
    }, P)

    row = lambda v: v.reshape(1, -1)
    rows = pack(ROWS, {
        "l0_b": row(i["L0_gnn_b"]), "gb": row(i["L0_ffn_gb"]), "dt_bias": row(i["L1_ffn_dt_bias"]),
        "A_log": row(i["L1_ffn_A_log"]), "D": row(np.repeat(i["L1_ffn_D"], M_HD)), "b_lin": row(i["L1_ffn_b_lin"]),
        "bv": row(i["L2_gnn_bv"]), "bo": row(i["L2_gnn_bo"]), "gamma": row(i["L2_gnn_gamma"]),
        "beta": row(i["L2_gnn_beta"]), "gat_brow": row(i["L3_gnn_b"]), "br": row(i["L3_ffn_br"]),
        "iota8": row(np.arange(8, dtype=f)), "rank": row(np.arange(NODES, 0, -1, dtype=f)),
    }, 1)

    k = np.arange(P)
    onehot = np.zeros((8, 8, P), f)
    onehot[np.arange(8), np.arange(8)] = 1.0
    consts = pack(CONSTS, {"ident": np.eye(P, dtype=f), "le": (k[:, None] <= k).astype(f),
                           "gt": (k[:, None] > k).astype(f), "onehot": onehot}, P)
    inv = 1.0 / 10000.0 ** (np.arange(0, HD, 2, dtype=f) / HD)
    angle = np.outer(np.arange(NODES, dtype=f), inv)
    angle = np.concatenate([angle, angle], -1).T
    sign = np.where(np.arange(HD) < half, -1.0, 1.0).astype(f)[:, None]
    trig = np.concatenate([np.tile(np.cos(angle), (HEADS, 1)), np.tile(np.sin(angle) * sign, (HEADS, 1))], 1)
    trig = trig.astype(f)

    w2 = np.zeros((L2_E, 3 * P, CH), f)
    w2[:, :HID] = i["L2_ffn_w2"].transpose(0, 2, 1)
    exp2 = np.concatenate([i["L2_ffn_w1"].transpose(0, 2, 1), i["L2_ffn_w3"].transpose(0, 2, 1),
                           w2.reshape(L2_E, 3, P, CH).transpose(0, 2, 1, 3).reshape(L2_E, P, 3 * CH)], 2)
    exp3 = np.concatenate([i["L3_ffn_W1"],
                           i["L3_ffn_W2"].reshape(L3_E, 4, P, CH).transpose(0, 2, 1, 3).reshape(L3_E, P, 4 * CH)], 2)
    return {"x": i["x"], "adj": i["adj"], "weights": weights, "cols": cols, "rowvecs": rows, "consts": consts,
            "trig": trig, "exp2": exp2, "exp3": exp3}


def declare(nc, arrays):
    args = [nc.dram_tensor(f"in_{name}", a.shape, mybir.dt.from_np(a.dtype), kind="ExternalInput").ap()
            for name, a in arrays.items()]
    out = nc.dram_tensor("out", (GRAPHS, NODES, CH), F32, kind="ExternalOutput").ap()
    program(nc, *args, out)


def kernel(**inputs):
    import concourse.bacc as bacc
    from concourse.bass_utils import run_bass_kernel_spmd

    arrays = {n: np.ascontiguousarray(a) for n, a in laid_out({k: np.asarray(v) for k, v in inputs.items()}).items()}
    nc = bacc.Bacc("TRN2", target_bir_lowering=False, num_devices=1)
    declare(nc, arrays)
    result = run_bass_kernel_spmd(nc, [{f"in_{n}": a for n, a in arrays.items()}], core_ids=[0])
    return result.results[0]["out"]
```

```python
from collections import namedtuple
from contextlib import ExitStack, contextmanager

import numpy as np

import concourse.bass as bass
from concourse import mybir

F32 = mybir.dt.float32
BF16 = mybir.dt.bfloat16
I32 = mybir.dt.int32
U32 = mybir.dt.uint32
ALU = mybir.AluOpType
ACT = mybir.ActivationFunctionType
AX_X = mybir.AxisListType.X

P = 128
GRAPHS, NODES, CH = 8, 1024, 128
TILES = NODES // P
HALVES, HALF = 2, 512
NEIGH = 25
SLOTS = 32
HEADS, HD = 4, 32
MASKED = -(2.0 ** 100)
LN_EPS, RMS_EPS = 1e-5, 1e-6

L0_E, L2_E, L3_E = 4, 8, 8
EH2 = 64
HID = 341
HID_CHUNKS = [(0, 128), (128, 128), (256, HID - 256)]
L3_HID = 512
M_HEADS, M_HD, M_STATE, M_CONV = 4, 64, 64, 4
M_INNER = M_HEADS * M_HD

WEIGHTS = [
    ("l0_top", 128), ("l0_bot", 128), ("sW1", 128), ("sW2", 128), ("sW3", 128), ("eW1", L0_E * 128),
    ("eW2", L0_E * EH2), ("eW3", L0_E * 128), ("gW", L0_E), ("msg", 128), ("upd", 128),
    ("W_z", M_INNER), ("W_xh", M_INNER), ("W_BC", 2 * M_STATE), ("W_dt", M_HEADS),
    ("W_out", 2 * 128), ("W_lin", 128), ("Wq", 128), ("Wk", 128), ("Wv", 128), ("Wo", 128),
    ("wq", 128), ("wq_rot", 128), ("wk", 128), ("wk_rot", 128), ("wv", 64), ("wo", 128), ("router", L2_E),
    ("gatW", 128), ("Wr", L3_E),
]
COLS = [
    ("sb1", 1), ("sb2", 1), ("sb3", 1), ("eb1", L0_E), ("eb2", L0_E), ("eb3", L0_E), ("gnn_bias", 1),
    ("conv_xh", 2 * M_CONV), ("conv_BC", M_CONV), ("convb_xh", 2), ("convb_BC", 1),
    ("norm_w", 2), ("bq", 1), ("bk", 1), ("ln1", 1), ("ln2", 1), ("gat_b", 1),
    ("a_src", HEADS), ("a_dst", HEADS), ("ln_g", L3_E), ("ln_b", L3_E), ("b1", L3_E * 4), ("b2", L3_E),
]
ROWS = [
    ("l0_b", 128), ("gb", L0_E), ("dt_bias", M_HEADS), ("A_log", M_HEADS), ("D", M_INNER), ("b_lin", 128),
    ("bv", 128), ("bo", 128), ("gamma", 128), ("beta", 128), ("gat_brow", 128), ("br", L3_E),
    ("iota8", 8), ("rank", NODES),
]
CONSTS = [("ident", 128), ("le", 128), ("gt", 128)]
EXP2 = 2 * HID + 3 * 128
EXP3 = 2 * L3_HID


class Memory:
    pass


def named_sems(sem, layer, names):
    return namedtuple("Semaphores", names)(*[sem(f"{layer}_{n}") for n in names])


def offsets(table):
    at, out = 0, {}
    for name, n in table:
        out[name] = (at, n)
        at += n
    return out, at


def sizes(table):
    return offsets(table)[1]


@contextmanager
def semaphores(nc, gathers=False):
    with ExitStack() as c:
        used = []

        def sem(name):
            used.append(c.enter_context(nc.semaphore(name)))
            return used[-1]

        yield sem
        numbers = sorted(s.num for s in used)
        starts = [n for n in numbers if n - 1 not in numbers]
        ends = [n + 1 for n in numbers if n + 1 not in numbers]
        runs = [range(first, end) for first, end in zip(starts, ends)]
        if gathers:
            for run in runs:
                nc.gpsimd.dma_reset(run)
        for run in runs:
            nc.gpsimd.sem_clear(run)
        nc.all_engine_barrier()




def linker(engine, semaphore):
    count = [0]

    def link(instruction):
        count[0] += 1
        instruction.then_inc(semaphore, 1)
        engine.wait_ge(semaphore, count[0])

    return link


def count_vector(v, K, src, link):
    for t in range(TILES):
        last = v.bn_stats(K.stats[:, t, :], src[:, t, :])
    link(last)
    for t in range(TILES):
        last = v.bn_aggr(K.mv[:, t, :], K.stats[:, t, :])
    link(last)


def norm_vector(v, K, N, src, dst, eps, rms=False):
    link = linker(v, N.chain)
    count_vector(v, K, src, link)
    spread = K.mv[:, :, 1]
    if rms:
        link(v.tensor_tensor(K.nsq[:, :], K.mv[:, :, 0], K.mv[:, :, 0], ALU.mult))
        link(v.tensor_tensor(K.nsq[:, :], K.nsq[:, :], K.mv[:, :, 1], ALU.add))
        spread = K.nsq[:, :]
    v.tensor_scalar(K.veps[:, :], spread, eps, None, ALU.add).then_inc(N.var, 1)
    v.wait_ge(N.std, 1)
    link(v.reciprocal(K.rstd[:, :], K.std[:, :]))
    for t in range(TILES):
        if rms:
            v.tensor_scalar(dst[:, t, :], src[:, t, :], K.rstd[:, t:t + 1], None, ALU.mult).then_inc(N.xn, 1)
        else:
            v.tensor_scalar(dst[:, t, :], src[:, t, :], K.mv[:, t, 0:1], K.rstd[:, t:t + 1],
                            ALU.subtract, ALU.mult).then_inc(N.xn, 1)


def rms_vector(v, K, N, src, dst, eps):
    link = linker(v, N.chain)
    v.wait_ge(N.squared, TILES)
    v.tensor_scalar(K.veps[:, :], K.nsq[:, :], 1.0 / CH, eps, ALU.mult, ALU.add).then_inc(N.var, 1)
    v.wait_ge(N.std, 1)
    link(v.reciprocal(K.rstd[:, :], K.std[:, :]))
    for t in range(TILES):
        v.tensor_scalar(dst[:, t, :], src[:, t, :], K.rstd[:, t:t + 1], None, ALU.mult).then_inc(N.xn, 1)


def rms_scalar(act, K, N, src, squares, ready):
    for t in range(TILES):
        act.wait_ge(ready, t + 1)
        if t >= 1:
            act.wait_ge(N.squared, t)
        act.activation(squares, src[:, t, :], ACT.Square, accum_out=K.nsq[:, t:t + 1]).then_inc(N.squared, 1)
    norm_scalar(act, K, N)


def norm_scalar(act, K, N):
    act.wait_ge(N.var, 1)
    act.activation(K.std[:, :], K.veps[:, :], ACT.Sqrt).then_inc(N.std, 1)


def turn_tensor(pe, K, src, banks, ready, done):
    for t in range(TILES):
        if ready is not None:
            pe.wait_ge(ready, t + 1)
        last = pe.transpose(K.ps[:, banks[t // 4], (t % 4) * P:(t % 4 + 1) * P], src[:, t, :], K.ident)
        if t % 4 == 3:
            last.then_inc(done, 1)


def turn_scalar(act, K, dst, banks, turned, done, scale=None):
    for h in range(HALVES):
        act.wait_ge(turned, h + 1)
        out = dst[:, h * HALF:(h + 1) * HALF]
        if scale is None:
            act.activation(out, K.ps[:, banks[h], :], ACT.Copy).then_inc(done, 1)
        else:
            act.activation(out, K.ps[:, banks[h], :], ACT.Copy, scale=scale).then_inc(done, 1)


def turn_back_tensor(pe, K, accT, banks, ready, need, done):
    for h in range(HALVES):
        pe.wait_ge(ready, need[h])
        for q in range(4):
            t = 4 * h + q
            last = pe.transpose(K.ps[:, banks[h], q * P:(q + 1) * P], accT[:, t * P:(t + 1) * P], K.ident)
        last.then_inc(done, 1)


def turn_back_vector(v, K, banks, done):
    for h in range(HALVES):
        v.wait_ge(done, h + 1)
        xh = K.x[:, 4 * h:4 * h + 4, :]
        v.tensor_tensor(xh, xh, K.ps[:, banks[h], :].rearrange("p (t c) -> p t c", t=4), ALU.add)


def router_tensor(pe, K, R, w, experts):
    for t in range(TILES):
        last = pe.matmul(K.ps[:, 6, t * 8:t * 8 + experts], K.xnT[:, t * P:(t + 1) * P], w, start=True, stop=True)
    last.then_inc(R.logits, 1)


def router_vector(v, K, R, experts, bias, mode):
    link = linker(v, R.chain)

    def over(ap):
        return ap.unsqueeze(2).to_broadcast((P, TILES, experts))

    link(v.memset(K.prob[:, :, :], -1.0))
    lg = K.logit[:, :, 0:experts]
    v.wait_ge(R.logits, 1)
    got = K.ps[:, 6, 0:8 * TILES].rearrange("p (t e) -> p t e", e=8)[:, :, 0:experts]
    if bias is None:
        link(v.tensor_copy(lg, got))
    else:
        link(v.tensor_tensor(lg, got, bias.unsqueeze(1).to_broadcast((P, TILES, experts)), ALU.add))
    link(v.tensor_reduce(K.r1[:, :], lg, AX_X, ALU.max))
    v.tensor_tensor(lg, lg, over(K.r1[:, :]), ALU.subtract).then_inc(R.shifted, 1)
    v.wait_ge(R.exps, 1)
    link(v.tensor_reduce(K.r1[:, :], lg, AX_X, ALU.add))
    link(v.reciprocal(K.r2[:, :], K.r1[:, :]))
    link(v.tensor_tensor(K.prob[:, :, 0:experts], lg, over(K.r2[:, :]), ALU.mult))
    for t in range(TILES):
        last = v.max(K.top[:, t, :], K.prob[:, t, :])
    link(last)
    for t in range(TILES):
        last = v.max_index(K.topi[:, t, :], K.top[:, t, :], K.prob[:, t, :])
    link(last)
    link(v.tensor_copy(K.topf[:, :, :], K.topi[:, :, 0:2]))
    first, second = K.top[:, :, 0], K.top[:, :, 1]
    if mode == "softmax":
        v.tensor_tensor(K.r1[:, :], second, first, ALU.subtract).then_inc(R.shifted, 1)
        v.wait_ge(R.exps, 2)
        link(v.tensor_scalar(K.r2[:, :], K.r1[:, :], 1.0, None, ALU.add))
        link(v.reciprocal(K.w1[:, :], K.r2[:, :]))
        link(v.tensor_tensor(K.w2[:, :], K.r1[:, :], K.w1[:, :], ALU.mult))
    else:
        link(v.tensor_tensor(K.r1[:, :], first, second, ALU.add))
        if mode == "floor":
            link(v.tensor_scalar(K.r1[:, :], K.r1[:, :], 1e-9, None, ALU.add))
        link(v.reciprocal(K.r2[:, :], K.r1[:, :]))
        link(v.tensor_tensor(K.w1[:, :], first, K.r2[:, :], ALU.mult))
        link(v.tensor_tensor(K.w2[:, :], second, K.r2[:, :], ALU.mult))
    iota = K.row("iota8").unsqueeze(1).to_broadcast((P, TILES, 8))

    def all8(ap):
        return ap.unsqueeze(2).to_broadcast((P, TILES, 8))

    link(v.tensor_tensor(K.gate[:, :, :], iota, all8(K.topf[:, :, 0]), ALU.is_equal))
    link(v.tensor_tensor(K.gate2[:, :, :], iota, all8(K.topf[:, :, 1]), ALU.is_equal))
    link(v.tensor_tensor(K.gate[:, :, :], K.gate[:, :, :], all8(K.w1[:, :]), ALU.mult))
    link(v.tensor_tensor(K.gate2[:, :, :], K.gate2[:, :, :], all8(K.w2[:, :]), ALU.mult))
    v.tensor_tensor(K.gate[:, :, :], K.gate[:, :, :], K.gate2[:, :, :], ALU.add).then_inc(R.gate, 1)


def router_scalar(act, K, R, experts, mode):
    act.wait_ge(R.shifted, 1)
    lg = K.logit[:, :, 0:experts]
    act.activation(lg, lg, ACT.Exp).then_inc(R.exps, 1)
    if mode == "softmax":
        act.wait_ge(R.shifted, 2)
        act.activation(K.r1[:, :], K.r1[:, :], ACT.Exp).then_inc(R.exps, 1)


def gates_tensor(pe, K, R):
    pe.wait_ge(R.gate, 1)
    for t in range(TILES):
        last = pe.transpose(K.ps[0:8, 6 + t // 4, (t % 4) * P:(t % 4 + 1) * P], K.gate[:, t, :], K.ident)
    last.then_inc(R.turned, 1)


def gates_scalar(act, K, R):
    act.wait_ge(R.turned, 1)
    for h in range(HALVES):
        act.activation(K.gateT[:, h * HALF:(h + 1) * HALF], K.ps[0:8, 6 + h, :], ACT.Copy).then_inc(R.gateT, 1)


def gates_out(sp, K, R):
    sp.wait_ge(R.gateT, HALVES)
    sp.dma_start(K.d_gates, K.gateT[:, :]).then_inc(R.stored, 16)
    sp.wait_ge(R.stored, 16)


def gate_in(sp, K, R, e):
    if e >= 2:
        sp.wait_ge(R.used, HALVES * (e - 1))
    sp.dma_start(K.wb[:, e % 2, :], K.d_gates[e:e + 1, :].to_broadcast((P, NODES))).then_inc(R.spread[e % 2], 16)


def gate_vector(v, K, R, e, h):
    v.wait_ge(R.spread[e % 2], 16 * (e // 2 + 1))
    return K.wb[:, e % 2, h * HALF:(h + 1) * HALF]


@contextmanager
def gate_memory(nc, K, layer):
    with (nc.sbuf_tensor(f"{layer}_gateT", [8, NODES], F32) as K.gateT,
          nc.sbuf_tensor(f"{layer}_gate_all", [P, 2, NODES], F32) as K.wb):
        yield


def norm_sems(sem, layer):
    return named_sems(sem, f"{layer}_norm", ("chain", "var", "std", "xn", "turned", "xT", "squared"))


def router_sems(sem, layer):
    names = ("chain", "logits", "shifted", "exps", "gate", "turned", "gateT", "stored", "used", "spread")
    one = [sem(f"{layer}_route_{n}") for n in names[:-1]]
    return namedtuple("Semaphores", names)(*one, [sem(f"{layer}_route_spread{i}") for i in range(2)])




def next_rows_vector(v, K, G):
    v.wait_ge(G.x_in, 16)
    link = linker(v, G.norm_chain)
    for t in range(TILES):
        last = v.bn_stats(K.g_stats[:, t, :], K.xg[:, t, :])
    link(last)
    for t in range(TILES):
        last = v.bn_aggr(K.g_mv[:, t, :], K.g_stats[:, t, :])
    link(last)
    v.tensor_scalar(K.g_veps[:, :], K.g_mv[:, :, 1], LN_EPS, None, ALU.add).then_inc(G.var, 1)
    v.wait_ge(G.std, 1)
    link(v.reciprocal(K.g_rstd[:, :], K.g_std[:, :]))
    for t in range(TILES):
        v.tensor_scalar(K.xg[:, t, :], K.xg[:, t, :], K.g_mv[:, t, 0:1], K.g_rstd[:, t:t + 1],
                        ALU.subtract, ALU.mult).then_inc(G.xn, 1)


def next_rows_scalar(act, K, G):
    act.wait_ge(G.var, 1)
    act.activation(K.g_std[:, :], K.g_veps[:, :], ACT.Sqrt).then_inc(G.std, 1)


def next_rows_in(engine, K, G, g):
    engine.dma_start(K.xg[:, :, :], K.d_x[g, :, :].rearrange("(t p) c -> p t c", p=P)).then_inc(G.x_in, 16)


def next_rows_out(engine, K, G):
    engine.wait_ge(G.xn, TILES)
    engine.dma_start(K.d_rows[0:NODES, :].rearrange("(t p) c -> p t c", p=P), K.xg[:, :, :]).then_inc(G.rows, 16)
    engine.dma_start(K.d_rows[NODES:NODES + 1, :], K.zero_row[:, :]).then_inc(G.rows, 16)
    engine.wait_ge(G.rows, 32)


def next_adj_in(engine, K, G, g, t):
    if t >= 1:
        engine.wait_ge(G.ranked, t)
    engine.dma_start(K.adj_next[:, :], K.d_adj[g, t * P:(t + 1) * P, :]).then_inc(G.adj_in, 16)


INDEX_STEPS = 1 + 2 * (SLOTS // 8)


def next_index_vector(v, K, G, t, step, link):
    q = (step - 1) // 2
    if step == 0:
        v.wait_ge(G.adj_in, 16 * (t + 1))
        v.tensor_tensor(K.ranks[:, :], K.adj_next[:, :], K.row("rank"), ALU.mult).then_inc(G.ranked, 1)
        v.wait_ge(G.ranked, t + 1)
    elif step % 2 == 1:
        link(v.max(K.first[:, 8 * q:8 * q + 8], K.ranks[:, :]))
    elif q < SLOTS // 8 - 1:
        link(v.match_replace(K.ranks[:, :], K.first[:, 8 * q:8 * q + 8], K.ranks[:, :], 0.0))
    else:
        v.tensor_scalar(K.floor[:, t:t + 1], K.first[:, NEIGH:NEIGH + 1], 0.0, -3.0e38, ALU.is_gt, ALU.mult)
        v.tensor_scalar(K.idx[:, t, :], K.first[:, :], -1.0, float(NODES), ALU.mult, ALU.add).then_inc(G.indexed, 1)
        v.wait_ge(G.indexed, t + 1)


def gather_pool(pool, K, G, t):
    pool.wait_ge(G.indexed, t + 1)
    if t >= 2:
        pool.wait_ge(G.pooled, t - 1)
    for s in range(NEIGH):
        pool.indirect_dma_start(out=K.neigh[:, t % 2, s, :], out_offset=None, in_=K.d_rows,
                                in_offset=bass.IndirectOffsetOnAxis(ap=K.idx[:, t, s:s + 1], axis=0)
                                ).then_inc(G.gathered[t % 2], 16)


def pool_max_vector(v, K, G, t, link):
    v.wait_ge(G.gathered[t % 2], 16 * NEIGH * (t // 2 + 1))
    v.tensor_reduce(K.aggraw[:, :], K.neigh[:, t % 2, :, :].rearrange("p s c -> p c s"), AX_X, ALU.max
                    ).then_inc(G.pooled, 1)
    v.wait_ge(G.pooled, t + 1)
    link(v.tensor_scalar(K.agg[:, t, :], K.aggraw[:, :], K.floor[:, t:t + 1], None, ALU.max))


RANKED = (range(0, 5), range(5, TILES))
GATHERS = (range(0, 4), range(4, 5), range(5, TILES))


def ranking(slot, slots, tiles):
    if slot not in slots:
        return []
    at, steps = slot - slots[0], INDEX_STEPS * len(tiles)
    return [(tiles[k // INDEX_STEPS], k % INDEX_STEPS)
            for k in range(at * steps // len(slots), (at + 1) * steps // len(slots))]




def layer0_gnn(nc, K, sem, g):
    xn_in, turned, xT = sem("xn_in"), sem("pool_turned"), sem("pool_xT")
    x_in, agg_turned, aggT_ready = sem("x_in"), sem("agg_turned"), sem("aggT_ready")
    mixed, chain = sem("pool_mixed"), sem("pool_chain")
    with ExitStack() as c:
        aggT = c.enter_context(nc.sbuf_tensor("aggT", [P, NODES], F32))
        tmp = c.enter_context(nc.sbuf_tensor("pool_tmp", [P, HALVES, HALF], F32))
        with nc.Block() as block:
            @block.sync
            def _(sp):
                sp.dma_start(K.xn[:, :, :], K.d_rows[0:NODES, :].rearrange("(t p) c -> p t c", p=P)
                             ).then_inc(xn_in, 16)
                sp.dma_start(K.x[:, :, :], K.d_x[g, :, :].rearrange("(t p) c -> p t c", p=P)).then_inc(x_in, 16)

            @block.vector
            def _(v):
                v.wait_ge(x_in, 16)
                link = linker(v, chain)
                for h in range(HALVES):
                    v.wait_ge(mixed, h + 1)
                    th = tmp[:, h, :].rearrange("p (t c) -> p t c", t=4)
                    xh = K.x[:, 4 * h:4 * h + 4, :]
                    link(v.tensor_tensor(th, K.ps[:, 4 + h, :].rearrange("p (t c) -> p t c", t=4),
                                         K.row("l0_b").unsqueeze(1).to_broadcast((P, 4, CH)), ALU.add))
                    v.scalar_tensor_tensor(out=xh, in0=th, scalar=0.0, in1=xh, op0=ALU.max, op1=ALU.add)

            @block.scalar
            def _(act):
                turn_scalar(act, K, aggT, (2, 3), agg_turned, aggT_ready)
                turn_scalar(act, K, K.xnT, (0, 1), turned, xT)

            @block.tensor
            def _(pe):
                turn_tensor(pe, K, K.agg, (2, 3), None, agg_turned)
                pe.wait_ge(xn_in, 16)
                turn_tensor(pe, K, K.xn, (0, 1), None, turned)
                for h in range(HALVES):
                    pe.wait_ge(aggT_ready, h + 1)
                    pe.wait_ge(xT, h + 1)
                    for q in range(4):
                        t = 4 * h + q
                        out = K.ps[:, 4 + h, q * P:(q + 1) * P]
                        pe.matmul(out, K.xnT[:, t * P:(t + 1) * P], K.w("l0_top"), start=True, stop=False)
                        last = pe.matmul(out, aggT[:, t * P:(t + 1) * P], K.w("l0_bot"), start=False, stop=True)
                    last.then_inc(mixed, 1)




def layer0_ffn(nc, K, sem, g):
    N, R = norm_sems(sem, "mlp"), router_sems(sem, "mlp")
    l1, l2, l3 = sem("mlp_l1"), sem("mlp_l2"), sem("mlp_l3")
    h1_ready, h2_ready, y_used = sem("mlp_h1"), sem("mlp_h2"), sem("mlp_y_used")
    chain, turned_back = sem("mlp_chain"), sem("mlp_turned_back")
    adj_in, adj_done, adj_chain = [sem("adj_in0"), sem("adj_in1")], sem("adj_done"), sem("adj_chain")
    jobs = [(m, h) for m in range(1 + L0_E) for h in range(HALVES)]
    J = len(jobs)
    with ExitStack() as c:
        c.enter_context(gate_memory(nc, K, "mlp"))
        h1 = c.enter_context(nc.sbuf_tensor("h1", [P, 2, HALF], F32))
        h2 = c.enter_context(nc.sbuf_tensor("h2", [P, 2, HALF], F32))
        accT = c.enter_context(nc.sbuf_tensor("accT", [P, NODES], F32))
        tmp = c.enter_context(nc.sbuf_tensor("mlp_tmp", [P, HALF], F32))
        raw = c.enter_context(nc.sbuf_tensor("adj_raw", [P, 2, NODES], I32))
        with nc.Block() as block:
            @block.sync
            def _(sp):
                for t in range(TILES):
                    if t >= 2:
                        sp.wait_ge(adj_done, t - 1)
                    sp.dma_start(raw[:, t % 2, :], K.d_adj[g, t * P:(t + 1) * P, :]).then_inc(adj_in[t % 2], 16)
                    if t == TILES // 2:
                        gates_out(sp, K, R)
                        gate_in(sp, K, R, 0)
                        gate_in(sp, K, R, 1)
                for e in range(2, L0_E):
                    gate_in(sp, K, R, e)

            @block.gpsimd
            def _(pool):
                for t in range(TILES):
                    pool.wait_ge(adj_in[t % 2], 16 * (t // 2 + 1))
                    pool.tensor_copy(K.adj[:, t, :], raw[:, t % 2, :]).then_inc(adj_done, 1)
                    pool.wait_ge(adj_done, t + 1)
                    pool.tensor_scalar(K.masked[:, t, :], K.adj[:, t, :], -MASKED, MASKED, ALU.mult, ALU.add
                                       ).then_inc(adj_chain, 1)

            @block.tensor
            def _(pe):
                turn_tensor(pe, K, K.xn, (4, 5), N.xn, N.turned)
                pe.wait_ge(N.xT, HALVES)
                router_tensor(pe, K, R, K.w("gW"), L0_E)
                for k in range(J + 2):
                    if k < J:
                        m, h = jobs[k]
                        w = K.w("sW1") if m == 0 else K.w("eW1")[:, (m - 1) * P:m * P]
                        if k >= 2:
                            pe.wait_ge(h1_ready, k - 1)
                        pe.matmul(K.ps[:, k % 2, :], w, K.xnT[:, h * HALF:(h + 1) * HALF], start=True, stop=True
                                  ).then_inc(l1, 1)
                    if 1 <= k <= J:
                        m, h = jobs[k - 1]
                        wide = P if m == 0 else EH2
                        w = K.w("sW2") if m == 0 else K.w("eW2")[:, (m - 1) * EH2:m * EH2]
                        pe.wait_ge(h1_ready, k)
                        if k - 1 >= 2:
                            pe.wait_ge(h2_ready, k - 2)
                        pe.matmul(K.ps[0:wide, 2 + (k - 1) % 2, :], w, h1[:, (k - 1) % 2, :], start=True, stop=True
                                  ).then_inc(l2, 1)
                    if k == 3:
                        gates_tensor(pe, K, R)
                    if k >= 2:
                        n = k - 2
                        m, h = jobs[n]
                        wide = P if m == 0 else EH2
                        w = K.w("sW3") if m == 0 else K.w("eW3")[0:EH2, (m - 1) * P:m * P]
                        pe.wait_ge(h2_ready, n + 1)
                        if n >= 2 * HALVES:
                            pe.wait_ge(R.used, n - 1 - HALVES)
                        elif n >= 2:
                            pe.wait_ge(y_used, n - 1)
                        pe.matmul(K.ps[:, 4 + n % 2, :], w, h2[0:wide, n % 2, :], start=True, stop=True
                                  ).then_inc(l3, 1)
                turn_back_tensor(pe, K, accT, (0, 1), chain, (J - HALVES - 1, J - HALVES), turned_back)

            @block.scalar
            def _(act):
                norm_scalar(act, K, N)
                turn_scalar(act, K, K.xnT, (4, 5), N.turned, N.xT)
                router_scalar(act, K, R, L0_E, "softmax")
                for k in range(J + 2):
                    if k == 3:
                        gates_scalar(act, K, R)
                    if k < J:
                        m = jobs[k][0]
                        act.wait_ge(l1, k + 1)
                        if k >= 2:
                            act.wait_ge(l2, k - 1)
                        bias = K.col("sb1") if m == 0 else K.col("eb1")[:, m - 1:m]
                        act.activation(h1[:, k % 2, :], K.ps[:, k % 2, :], ACT.Relu, bias=bias).then_inc(h1_ready, 1)
                    if 1 <= k <= J:
                        n = k - 1
                        m = jobs[n][0]
                        wide = P if m == 0 else EH2
                        act.wait_ge(l2, n + 1)
                        if n >= 2:
                            act.wait_ge(l3, n - 1)
                        bias = K.col("sb2") if m == 0 else K.col("eb2")[0:EH2, m - 1:m]
                        act.activation(h2[0:wide, n % 2, :], K.ps[0:wide, 2 + n % 2, :], ACT.Relu, bias=bias
                                       ).then_inc(h2_ready, 1)

            @block.vector
            def _(v):
                norm_vector(v, K, N, K.x, K.xn, LN_EPS)
                router_vector(v, K, R, L0_E, K.row("gb"), "softmax")
                link = linker(v, chain)
                for n, (m, h) in enumerate(jobs):
                    v.wait_ge(l3, n + 1)
                    acc = accT[:, h * HALF:(h + 1) * HALF]
                    if m == 0:
                        v.tensor_scalar(acc, K.ps[:, 4 + n % 2, :], K.col("sb3"), None, ALU.add).then_inc(y_used, 1)
                        v.wait_ge(y_used, n + 1)
                        continue
                    v.scalar_tensor_tensor(out=tmp[:, :], in0=K.ps[:, 4 + n % 2, :],
                                           scalar=K.col("eb3")[:, m - 1:m], in1=gate_vector(v, K, R, m - 1, h),
                                           op0=ALU.add, op1=ALU.mult).then_inc(R.used, 1)
                    v.wait_ge(R.used, n - HALVES + 1)
                    link(v.tensor_tensor(acc, acc, tmp[:, :], ALU.add))
                turn_back_vector(v, K, (0, 1), turned_back)




def layer1_gnn(nc, K, sem, g):
    N = norm_sems(sem, "mean")
    h_ps, split, split_done, msg_ps, upd_ps = (sem(n) for n in ("mean_h", "mean_split", "mean_split_done",
                                                              "mean_msg", "mean_upd"))
    chain, summed, act_done, turned_back = (sem(n) for n in ("mean_chain", "mean_summed", "mean_act",
                                                             "mean_turned_back"))
    with ExitStack() as c:
        parts = [c.enter_context(nc.sbuf_tensor(f"mean_part{i}", [P, TILES * CH], BF16)) for i in range(3)]
        rest = c.enter_context(nc.sbuf_tensor("mean_rest", [P, NODES], F32))
        rdeg = c.enter_context(nc.sbuf_tensor("mean_rdeg", [P, NODES], F32))
        accT = c.enter_context(nc.sbuf_tensor("mean_accT", [P, NODES], F32))
        with nc.Block() as block:
            @block.tensor
            def _(pe):
                turn_tensor(pe, K, K.xn, (0, 1), N.xn, N.turned)
                for h in range(HALVES):
                    for t in range(TILES):
                        last = pe.matmul(K.ps[:, 2 + h, :], K.ones_bf[:, :], K.adj[:, t, h * HALF:(h + 1) * HALF],
                                         start=(t == 0), stop=(t == TILES - 1))
                    last.then_inc(upd_ps, 1)
                pe.wait_ge(N.xT, HALVES)
                for t in range(TILES):
                    last = pe.matmul(K.ps[:, 4 + t // 4, (t % 4) * P:(t % 4 + 1) * P], K.xnT[:, t * P:(t + 1) * P],
                                     K.w("msg"), start=True, stop=True)
                    if t % 4 == 3:
                        last.then_inc(h_ps, 1)
                for h in range(HALVES):
                    last = pe.matmul(K.ps[:, 0 + h, :], K.w("upd"), K.xnT[:, h * HALF:(h + 1) * HALF],
                                     start=True, stop=True)
                    last.then_inc(upd_ps, 1)
                for h in range(HALVES):
                    for i in range(3):
                        if h == 0:
                            pe.wait_ge(split_done, i + 1)
                        for t in range(TILES):
                            last = pe.matmul(K.ps[:, 6 + h, :], parts[i][:, t * CH:(t + 1) * CH],
                                             K.adj[:, t, h * HALF:(h + 1) * HALF],
                                             start=(i == 0 and t == 0), stop=(i == 2 and t == TILES - 1))
                    last.then_inc(msg_ps, 1)
                turn_back_tensor(pe, K, accT, (2, 3), act_done, (1, 2), turned_back)

            @block.scalar
            def _(act):
                norm_scalar(act, K, N)
                turn_scalar(act, K, K.xnT, (0, 1), N.turned, N.xT)
                for h in range(HALVES):
                    act.wait_ge(summed, h + 1)
                    out = accT[:, h * HALF:(h + 1) * HALF]
                    act.activation(out, out, ACT.Relu, bias=K.col("gnn_bias")).then_inc(act_done, 1)

            @block.vector
            def _(v):
                norm_vector(v, K, N, K.x, K.xn, LN_EPS)
                link = linker(v, chain)
                v.wait_ge(h_ps, HALVES)
                both = K.ps[:, 4:6, :].rearrange("p b n -> p (b n)")
                v.tensor_copy(parts[0][:, :], both).then_inc(split_done, 1)
                v.wait_ge(split_done, 1)
                link(v.tensor_tensor(rest[:, :], both, parts[0][:, :], ALU.subtract))
                v.tensor_copy(parts[1][:, :], rest[:, :]).then_inc(split_done, 1)
                v.wait_ge(split_done, 2)
                link(v.tensor_tensor(rest[:, :], rest[:, :], parts[1][:, :], ALU.subtract))
                v.tensor_copy(parts[2][:, :], rest[:, :]).then_inc(split_done, 1)
                v.wait_ge(upd_ps, 2 * HALVES)
                for h in range(HALVES):
                    last = v.tensor_scalar(rdeg[:, h * HALF:(h + 1) * HALF], K.ps[:, 2 + h, :], 1.0, None, ALU.max)
                link(last)
                link(v.reciprocal(rdeg[:, :], rdeg[:, :]))
                for h in range(HALVES):
                    v.wait_ge(msg_ps, h + 1)
                    out = accT[:, h * HALF:(h + 1) * HALF]
                    link(v.tensor_tensor(out, K.ps[:, 6 + h, :], rdeg[:, h * HALF:(h + 1) * HALF], ALU.mult))
                    v.tensor_tensor(out, out, K.ps[:, 0 + h, :], ALU.add).then_inc(summed, 1)
                turn_back_vector(v, K, (2, 3), turned_back)




def layer1_ffn(nc, K, sem, g):
    N = norm_sems(sem, "ssm")
    names = ("conv_ps", "conv_in", "conv_chain", "conv_done", "silu", "dt_ps", "dt_chain", "dt_exp", "dA", "sums_ps",
             "decays", "z_ps", "z_done", "seg_w", "tok_ps", "tok", "seg_ps", "seg", "cb_ps", "cbm", "mix", "xdd",
             "y_ps", "state_ps", "state", "y_chain", "y", "off", "xD", "ss_std_in", "ss_std", "yn", "yT_ps", "yT",
             "out_ps", "outT", "lin_ps", "padded", "decayed", "xdt", "squared")
    S = named_sems(sem, "ssm", names)
    CONVS = [("BC", 0), ("xh", 0), ("xh", 1)]
    with ExitStack() as c:
        def sb(name, shape, dt=F32):
            return c.enter_context(nc.sbuf_tensor("ssm_" + name, shape, dt))

        pre = [sb(f"pre{i}", [P, NODES + M_CONV - 1]) for i in range(3)]
        cv = [sb(f"cv{i}", [P, NODES]) for i in range(3)]
        conv_out = [cv[2], cv[0], cv[1]]
        CT = sb("CT", [M_STATE, NODES])
        sz = sb("sz", [P, TILES, M_INNER])
        yall = sb("y", [P, TILES, M_INNER])
        dt = sb("dt", [P, TILES * M_HEADS])
        dA = sb("dA", [P, TILES * M_HEADS])
        sp_t = [sb(f"sp{i}", [P, TILES * M_HEADS]) for i in range(4)]
        A = sb("A", [P, M_HEADS])
        decays = sb("decays", [P, 3, TILES * M_HEADS])
        segw = sb("segw", [P, 2, M_HEADS, P])
        L = sb("L", [P, M_HEADS, P])
        cbm = sb("cbm", [P, P])
        mix = sb("mix", [P, 2, M_HEADS, P])
        xtok = sb("xtok", [P, 2, M_INNER])
        xdt = sb("xdt", [P, 2, M_INNER])
        xdd = sb("xdd", [P, 2, M_INNER])
        xD = sb("xD", [P, 2, M_INNER])
        btok = sb("btok", [P, 2, M_STATE])
        state = sb("state", [M_STATE, 2, M_INNER])
        ya = sb("ya", [P, M_INNER])
        ysq = sb("ysq", [P, M_INNER])
        ss = sb("ss", [P, TILES])
        std = sb("std", [P, TILES])
        rstd = sb("rstd", [P, TILES])
        outT = sb("outT", [P, NODES])

        def heads(ap, d):
            return ap.rearrange("p (h d) -> p h d", d=d)

        def per_head(ap, d, n=P):
            return ap.unsqueeze(2).to_broadcast((n, M_HEADS, d))

        with nc.Block() as block:
            @block.tensor
            def _(pe):
                turn_tensor(pe, K, K.xn, (0, 1), N.xn, N.turned)
                pe.wait_ge(N.xT, HALVES)
                for t in range(TILES):
                    last = pe.matmul(K.ps[:, 6, t * M_HEADS:(t + 1) * M_HEADS], K.xnT[:, t * P:(t + 1) * P],
                                     K.w("W_dt"), start=True, stop=True)
                last.then_inc(S.dt_ps, 1)
                for i, (name, part) in enumerate(CONVS):
                    for h in range(HALVES):
                        n = HALVES * i + h
                        if n >= 4:
                            pe.wait_ge(S.conv_in, n - 3)
                        pe.matmul(K.ps[:, 2 + n % 4, :], K.w("W_" + name)[:, part * P:(part + 1) * P],
                                  K.xnT[:, h * HALF:(h + 1) * HALF], start=True, stop=True).then_inc(S.conv_ps, 1)
                for q in range(4):
                    if q >= 2:
                        pe.wait_ge(S.z_done, q - 1)
                    for t in (2 * q, 2 * q + 1):
                        last = pe.matmul(K.ps[:, q % 2, (t % 2) * M_INNER:(t % 2 + 1) * M_INNER],
                                         K.xnT[:, t * P:(t + 1) * P], K.w("W_z"), start=True, stop=True)
                    last.then_inc(S.z_ps, 1)
                pe.wait_ge(S.dA, 1)
                for i, tri in enumerate((K.le, K.gt, K.ones)):
                    last = pe.matmul(K.ps[:, 7, 32 * i:32 * i + 32], tri, dA[:, :], start=True, stop=True)
                last.then_inc(S.sums_ps, 1)
                pe.wait_ge(S.z_done, 4)
                pe.wait_ge(S.silu, 4)
                pe.wait_ge(S.decays, 1)

                def front(t):
                    cols = slice(t * P, (t + 1) * P)
                    if t >= 1:
                        pe.wait_ge(S.tok, 2 * t)
                        pe.wait_ge(S.cbm, t)
                    for i in range(2):
                        pe.transpose(K.ps[:, 2, i * P:(i + 1) * P], cv[i][:, cols], K.ident)
                    pe.transpose(K.ps[:, 3, 0:M_STATE], cv[2][0:M_STATE, cols], K.ident[0:M_STATE, 0:M_STATE]
                                 ).then_inc(S.tok_ps, 1)
                    pe.matmul(K.ps[:, 0, 0:P], cv[2][0:M_STATE, cols], CT[:, cols], start=True, stop=True
                              ).then_inc(S.cb_ps, 1)
                    pe.wait_ge(S.seg_w, t + 1)
                    if t >= 1:
                        pe.wait_ge(S.seg, t)
                    for h in range(M_HEADS):
                        last = pe.matmul(K.ps[:, 4, h * P:(h + 1) * P], segw[:, t % 2, h, :], K.le,
                                         start=True, stop=True)
                    last.then_inc(S.seg_ps, 1)

                def back(t):
                    b = t % 2
                    pe.wait_ge(S.xdd, t + 1)
                    if t >= 1:
                        pe.wait_ge(S.state, t)
                    if t < TILES - 1:
                        pe.matmul(K.ps[0:M_STATE, 5, 0:M_INNER], btok[:, b, :], xdd[:, b, :], start=True, stop=True
                                  ).then_inc(S.state_ps, 1)
                    if t >= 2:
                        pe.wait_ge(S.off, t - 1)
                    if t >= 1:
                        pe.matmul(K.ps[:, 6, 0:M_INNER], CT[:, t * P:(t + 1) * P], state[:, (t - 1) % 2, :],
                                  start=True, stop=True)
                        pe.wait_ge(S.y, t)
                    pe.wait_ge(S.xD, t + 1)
                    pe.matmul(K.ps[:, 7, 0:M_INNER], K.ident, xD[:, b, :], start=True, stop=False)
                    pe.wait_ge(S.mix, t + 1)
                    for h in range(M_HEADS):
                        last = pe.matmul(K.ps[:, 7, h * M_HD:(h + 1) * M_HD], mix[:, b, h, :],
                                         xdt[:, b, h * M_HD:(h + 1) * M_HD], start=False, stop=(h == M_HEADS - 1))
                    last.then_inc(S.y_ps, 1)

                front(0)
                for t in range(TILES):
                    if t + 1 < TILES:
                        front(t + 1)
                    back(t)
                for i in range(2):
                    for h in range(HALVES):
                        for q in range(4):
                            t = 4 * h + q
                            pe.wait_ge(S.yn, t + 1)
                            last = pe.transpose(K.ps[:, 2 * i + h, q * P:(q + 1) * P],
                                                yall[:, t, i * P:(i + 1) * P], K.ident)
                        last.then_inc(S.yT_ps, 1)
                for h in range(HALVES):
                    pe.wait_ge(S.yT, 4)
                    for i in range(2):
                        last = pe.matmul(K.ps[:, 4 + h, :], K.w("W_out")[:, i * P:(i + 1) * P],
                                         cv[i][:, h * HALF:(h + 1) * HALF], start=(i == 0), stop=(i == 1))
                    last.then_inc(S.out_ps, 1)
                for h in range(HALVES):
                    pe.wait_ge(S.outT, h + 1)
                    for q in range(4):
                        t = 4 * h + q
                        last = pe.matmul(K.ps[:, h, q * P:(q + 1) * P], outT[:, t * P:(t + 1) * P], K.w("W_lin"),
                                         start=True, stop=True)
                    last.then_inc(S.lin_ps, 1)

            @block.scalar
            def _(act):
                norm_scalar(act, K, N)
                act.activation(A[:, :], K.row("A_log"), ACT.Exp).then_inc(S.dt_exp, 1)
                turn_scalar(act, K, K.xnT, (0, 1), N.turned, N.xT)
                act.wait_ge(S.dt_chain, 2)
                act.activation(sp_t[1][:, :], sp_t[1][:, :], ACT.Exp, scale=-1.0).then_inc(S.dt_exp, 1)

                def conv_in(i):
                    for h in range(HALVES):
                        n = HALVES * i + h
                        act.wait_ge(S.conv_ps, n + 1)
                        at = M_CONV - 1 + h * HALF
                        act.activation(pre[i][:, at:at + HALF], K.ps[:, 2 + n % 4, :], ACT.Copy)
                        name, part = CONVS[i]
                        tap = (part + 1) * M_CONV - 1
                        act.activation(conv_out[i][:, h * HALF:(h + 1) * HALF], K.ps[:, 2 + n % 4, :], ACT.Identity,
                                       scale=K.col("conv_" + name)[:, tap:tap + 1],
                                       bias=K.col("convb_" + name)[:, part:part + 1]).then_inc(S.conv_in, 1)

                act.wait_ge(S.padded, 1)
                conv_in(0)
                conv_in(1)
                conv_in(2)
                for q in range(4):
                    act.wait_ge(S.z_ps, q + 1)
                    act.activation(sz[:, 2 * q:2 * q + 2, :].rearrange("p t n -> p (t n)"), K.ps[:, q % 2, :],
                                   ACT.Silu).then_inc(S.z_done, 1)
                act.wait_ge(S.conv_done, 1)
                act.activation(CT[:, :], cv[2][M_STATE:P, :], ACT.Silu).then_inc(S.silu, 1)
                act.activation(cv[2][0:M_STATE, :], cv[2][0:M_STATE, :], ACT.Silu).then_inc(S.silu, 1)
                for i in range(2):
                    act.wait_ge(S.conv_done, i + 2)
                    act.activation(cv[i][:, :], cv[i][:, :], ACT.Silu).then_inc(S.silu, 1)

                def square(t):
                    act.wait_ge(S.y, t + 1)
                    act.activation(ysq[:, :], yall[:, t, :], ACT.Square, accum_out=ss[:, t:t + 1]
                                   ).then_inc(S.squared, 1)
                    act.wait_ge(S.squared, t + 1)

                act.wait_ge(S.sums_ps, 1)
                act.activation(decays[:, :, :], K.ps[:, 7, 0:96].rearrange("p (i n) -> p i n", i=3), ACT.Exp
                               ).then_inc(S.decays, 1)
                for t in range(TILES):
                    b = t % 2
                    if t >= 2:
                        square(t - 2)
                    act.wait_ge(S.tok_ps, t + 1)
                    if t >= 2:
                        act.wait_ge(S.xD, t - 1)
                        act.wait_ge(S.xdt, t - 1)
                        act.wait_ge(S.state_ps, t - 1)
                    act.activation(xtok[:, b, :], K.ps[:, 2, 0:M_INNER], ACT.Copy).then_inc(S.tok, 1)
                    act.activation(btok[:, b, :], K.ps[:, 3, 0:M_STATE], ACT.Copy).then_inc(S.tok, 1)
                    act.wait_ge(S.seg_ps, t + 1)
                    if t >= 1:
                        act.wait_ge(S.mix, t)
                    act.activation(L[:, :, :], K.ps[:, 4, :].rearrange("p (h n) -> p h n", h=M_HEADS), ACT.Exp
                                   ).then_inc(S.seg, 1)
                act.activation(std[:, 0:1], A[:, 0:1], ACT.Sqrt)
                square(TILES - 2)
                square(TILES - 1)
                act.wait_ge(S.ss_std_in, 1)
                act.activation(std[:, :], ss[:, :], ACT.Sqrt).then_inc(S.ss_std, 1)
                for i in range(2):
                    for h in range(HALVES):
                        act.wait_ge(S.yT_ps, 2 * i + h + 1)
                        act.activation(cv[i][:, h * HALF:(h + 1) * HALF], K.ps[:, 2 * i + h, :], ACT.Copy,
                                       scale=K.col("norm_w")[:, i:i + 1]).then_inc(S.yT, 1)
                for h in range(HALVES):
                    act.wait_ge(S.out_ps, h + 1)
                    act.activation(outT[:, h * HALF:(h + 1) * HALF], K.ps[:, 4 + h, :], ACT.Copy
                                   ).then_inc(S.outT, 1)

            @block.gpsimd
            def _(pool):
                for i in range(3):
                    last = pool.memset(pre[i][:, 0:M_CONV - 1], 0.0)
                last.then_inc(S.padded, 1)
                pool.wait_ge(S.dA, 1)

                def seg_weights(t):
                    if t >= 2:
                        pool.wait_ge(S.seg_ps, t - 1)
                    pool.tensor_tensor(segw[:, t % 2, :, :], K.gt.unsqueeze(1).to_broadcast((P, M_HEADS, P)),
                                       per_head(dA[:, t * M_HEADS:(t + 1) * M_HEADS], P), ALU.mult
                                       ).then_inc(S.seg_w, 1)

                seg_weights(0)
                pool.wait_ge(S.decays, 1)
                for t in range(TILES):
                    b = t % 2
                    hs = slice(t * M_HEADS, (t + 1) * M_HEADS)
                    if t + 1 < TILES:
                        seg_weights(t + 1)
                    pool.wait_ge(S.xdt, t + 1)
                    if t >= 2:
                        pool.wait_ge(S.state_ps, t - 1)
                    pool.tensor_tensor(heads(xdd[:, b, :], M_HD), heads(xdt[:, b, :], M_HD),
                                       per_head(decays[:, 1, hs], M_HD), ALU.mult).then_inc(S.xdd, 1)
                    if t >= 2:
                        pool.wait_ge(S.y_ps, t - 1)
                    pool.tensor_tensor(xD[:, b, :], xtok[:, b, :], K.row("D"), ALU.mult).then_inc(S.xD, 1)
                    if 1 <= t < TILES - 1:
                        pool.wait_ge(S.state, t)
                        pool.wait_ge(S.y_ps, t)
                        pool.tensor_tensor(heads(state[:, b, :], M_HD), heads(state[:, 1 - b, :], M_HD),
                                           per_head(decays[0:M_STATE, 2, hs], M_HD, M_STATE), ALU.mult
                                           ).then_inc(S.decayed, 1)

            @block.vector
            def _(v):
                norm_vector(v, K, N, K.x, K.xn, LN_EPS)
                dlink = linker(v, S.dt_chain)
                a, u, s, w = (sp_t[i][:, :] for i in range(4))
                v.wait_ge(S.dt_ps, 1)
                dlink(v.tensor_tensor(heads(a, M_HEADS), heads(K.ps[:, 6, 0:32], M_HEADS),
                                      K.row("dt_bias").unsqueeze(1).to_broadcast((P, TILES, M_HEADS)), ALU.add))
                v.scalar_tensor_tensor(out=u, in0=a, scalar=-1.0, in1=a, op0=ALU.mult, op1=ALU.max
                                       ).then_inc(S.dt_chain, 1)
                v.wait_ge(S.dt_exp, 2)
                dlink2 = linker(v, S.y_chain)
                dlink2(v.tensor_scalar(s, u, 2.0, None, ALU.add))
                dlink2(v.reciprocal(w, s))
                dlink2(v.tensor_tensor(s, u, w, ALU.mult))
                dlink2(v.tensor_tensor(w, s, s, ALU.mult))
                dlink2(v.tensor_scalar(u, w, 1.0 / 17.0, None, ALU.mult))
                for odd in (15, 13, 11, 9, 7, 5, 3):
                    dlink2(v.scalar_tensor_tensor(out=u, in0=u, scalar=1.0 / odd, in1=w, op0=ALU.add, op1=ALU.mult))
                dlink2(v.scalar_tensor_tensor(out=u, in0=u, scalar=1.0, in1=s, op0=ALU.add, op1=ALU.mult))
                dlink2(v.tensor_scalar(u, u, 2.0, None, ALU.mult))
                dlink2(v.scalar_tensor_tensor(out=dt[:, :], in0=a, scalar=0.0, in1=u, op0=ALU.max, op1=ALU.add))
                v.scalar_tensor_tensor(out=heads(dA[:, :], M_HEADS), in0=heads(dt[:, :], M_HEADS), scalar=-1.0,
                                       in1=A[:, :].unsqueeze(1).to_broadcast((P, TILES, M_HEADS)),
                                       op0=ALU.mult, op1=ALU.mult).then_inc(S.dA, 1)
                clink = linker(v, S.conv_chain)
                for i, (name, part) in enumerate(CONVS):
                    taps = K.col("conv_" + name)[:, part * M_CONV:(part + 1) * M_CONV]
                    out = conv_out[i][:, :]
                    v.wait_ge(S.conv_in, HALVES * (i + 1))
                    for k in range(M_CONV - 1):
                        last = v.scalar_tensor_tensor(out=out, in0=pre[i][:, k:k + NODES],
                                                      scalar=taps[:, k:k + 1], in1=out, op0=ALU.mult, op1=ALU.add)
                        if k < M_CONV - 2:
                            clink(last)
                    last.then_inc(S.conv_done, 1)

                def front(t):
                    b = t % 2
                    v.wait_ge(S.tok, 2 * t + 2)
                    if t >= 2:
                        v.wait_ge(S.y_ps, t - 1)
                        v.wait_ge(S.xdd, t - 1)
                    v.tensor_tensor(heads(xdt[:, b, :], M_HD), heads(xtok[:, b, :], M_HD),
                                    per_head(dt[:, t * M_HEADS:(t + 1) * M_HEADS], M_HD), ALU.mult).then_inc(S.xdt, 1)
                    v.wait_ge(S.cb_ps, t + 1)
                    if t >= 1:
                        v.wait_ge(S.mix, t)
                    v.tensor_tensor(cbm[:, :], K.ps[:, 0, 0:P], K.le, ALU.mult).then_inc(S.cbm, 1)
                    v.wait_ge(S.cbm, t + 1)
                    v.wait_ge(S.seg, t + 1)
                    v.tensor_tensor(mix[:, b, :, :], L[:, :, :], cbm[:, :].unsqueeze(1).to_broadcast((P, M_HEADS, P)),
                                    ALU.mult).then_inc(S.mix, 1)

                ylink = linker(v, S.off)
                front(0)
                for t in range(TILES):
                    b = t % 2
                    hs = slice(t * M_HEADS, (t + 1) * M_HEADS)
                    if t + 1 < TILES:
                        front(t + 1)
                        v.wait_ge(S.state_ps, t + 1)
                        if t == 0:
                            v.tensor_copy(state[:, 0, :], K.ps[0:M_STATE, 5, 0:M_INNER]).then_inc(S.state, 1)
                        else:
                            v.wait_ge(S.decayed, t)
                            v.tensor_tensor(state[:, b, :], state[:, b, :], K.ps[0:M_STATE, 5, 0:M_INNER], ALU.add
                                            ).then_inc(S.state, 1)
                    v.wait_ge(S.y_ps, t + 1)
                    if t == 0:
                        v.tensor_tensor(yall[:, 0, :], K.ps[:, 7, 0:M_INNER], sz[:, 0, :], ALU.mult).then_inc(S.y, 1)
                        continue
                    ylink(v.tensor_tensor(heads(ya[:, :], M_HD), heads(K.ps[:, 6, 0:M_INNER], M_HD),
                                          per_head(decays[:, 0, hs], M_HD), ALU.mult))
                    dlink2(v.tensor_tensor(ya[:, :], ya[:, :], K.ps[:, 7, 0:M_INNER], ALU.add))
                    v.tensor_tensor(yall[:, t, :], ya[:, :], sz[:, t, :], ALU.mult).then_inc(S.y, 1)
                v.wait_ge(S.squared, TILES)
                v.tensor_scalar(ss[:, :], ss[:, :], 1.0 / M_INNER, LN_EPS, ALU.mult, ALU.add).then_inc(S.ss_std_in, 1)
                v.wait_ge(S.ss_std, 1)
                dlink2(v.reciprocal(rstd[:, :], std[:, :]))
                for t in range(TILES):
                    v.tensor_scalar(yall[:, t, :], yall[:, t, :], rstd[:, t:t + 1], None, ALU.mult
                                    ).then_inc(S.yn, 1)
                dlink2(v.tensor_tensor(K.x[:, :, :], K.x[:, :, :],
                                       K.row("b_lin").unsqueeze(1).to_broadcast((P, TILES, CH)), ALU.add))
                for h in range(HALVES):
                    v.wait_ge(S.lin_ps, h + 1)
                    xh = K.x[:, 4 * h:4 * h + 4, :]
                    v.tensor_tensor(xh, xh, K.ps[:, h, :].rearrange("p (t c) -> p t c", t=4), ALU.add)




def attend_sems(sem, layer):
    names = ("scores", "shifted", "top", "probs", "turned", "copied0", "copied1", "out", "outT", "back", "normed", "chain")
    return named_sems(sem, f"{layer}_att", names)



RING = 8


def attend_scores_tensor(pe, K, A, n, qT, kT, width):
    t, h = n // HEADS, n % HEADS
    if n >= 2:
        pe.wait_ge(A.shifted, n - 1)
    for at in range(0, width, HALF):
        n_cols = min(HALF, width - at)
        last = pe.matmul(K.ps[:, 2 * (n % 2) + at // HALF, 0:n_cols], qT[:, h, t * P:(t + 1) * P],
                         kT[:, at:at + n_cols], start=True, stop=True)
    last.then_inc(A.scores, 1)


def attend_turn_tensor(pe, K, A, n, probs, width, pairs, kept):
    pe.wait_ge(A.probs, n + 1)
    bank = pairs[n % len(pairs)]
    if n >= len(pairs):
        pe.wait_ge(A.copied0, n - len(pairs) + 1)
        pe.wait_ge(A.copied1, n - len(pairs) + 1)
    for at in range(0, width, HALF):
        for j in range(at // P, min(at + HALF, width) // P):
            last = pe.transpose(K.ps[:, bank + at // HALF, (j % 4) * P:(j % 4 + 1) * P],
                                probs[:, n % kept, j * P:(j + 1) * P], K.ident)
        last.then_inc(A.turned, 1)


def attend_values_tensor(pe, K, A, t, probsT, values, width):
    pe.wait_ge(A.copied0, HEADS * (t + 1))
    pe.wait_ge(A.copied1, HEADS * (t + 1))
    if t >= 1:
        pe.wait_ge(A.outT, t)
    blocks = width // P
    for j in range(blocks):
        for h in range(HEADS):
            last = pe.matmul(K.ps[h * HD:(h + 1) * HD, 6, 0:P], values(j, h),
                             probsT[:, (HEADS * t + h) % RING, j * P:(j + 1) * P],
                             start=(j == 0), stop=(j == blocks - 1))
    last.then_inc(A.out, 1)


def attend_out_scalar(act, K, A, t, oT):
    act.wait_ge(A.out, t + 1)
    if t >= 2:
        act.wait_ge(A.back, t - 1)
    act.activation(oT[:, t % 2, :], K.ps[:, 6, 0:P], ACT.Copy).then_inc(A.outT, 1)


def attend_back_tensor(pe, K, A, t, oT):
    pe.wait_ge(A.outT, t + 1)
    if t >= 1:
        pe.wait_ge(A.normed, t)
    pe.transpose(K.ps[:, 7, 0:P], oT[:, t % 2, :], K.ident).then_inc(A.back, 1)


def attend_tensor(pe, K, A, n, probs, probsT, oT, values, widths, pairs=(4,), kept=2, lag=6):
    units = HEADS * TILES
    if 2 <= n < units + 2:
        attend_turn_tensor(pe, K, A, n - 2, probs, widths[(n - 2) // HEADS], pairs, kept)
    if n >= lag and (n - lag) % HEADS == 0:
        t = (n - lag) // HEADS
        if t < TILES:
            attend_values_tensor(pe, K, A, t, probsT, values, widths[t])
    if n >= lag + 2 and (n - lag - 2) % HEADS == 0:
        attend_back_tensor(pe, K, A, (n - lag - 2) // HEADS, oT)


def attend_scale_vector(v, K, A, t, total, rtotal, out, link):
    v.wait_ge(A.back, t + 1)
    cols = slice(HEADS * t, HEADS * (t + 1))
    link(v.reciprocal(rtotal[:, cols], total[:, cols]))
    v.tensor_tensor(out.rearrange("p (h d) -> p h d", d=HD), K.ps[:, 7, 0:CH].rearrange("p (h d) -> p h d", d=HD),
                    rtotal[:, cols].unsqueeze(2).to_broadcast((P, HEADS, HD)), ALU.mult).then_inc(A.normed, 1)


def turned_count(widths, n, half):
    each = [min(HALVES, -(-widths[m // HEADS] // HALF)) for m in range(n + 1)]
    return sum(each[:n]) + min(half + 1, each[n])


def attend_copy(engine, copy, K, A, n, half, probsT, width, widths, pairs=(4,)):
    engine.wait_ge(A.turned, turned_count(widths, n, half))
    if n >= RING:
        engine.wait_ge(A.out, n // HEADS - 1)
    cols = min(HALF, width - half * HALF)
    copy(probsT[:, n % RING, half * HALF:half * HALF + cols], K.ps[:, pairs[n % len(pairs)] + half, 0:cols]
         ).then_inc((A.copied0, A.copied1)[half], 1)




def layer2_gnn(nc, K, sem, g):
    N, A, N2 = norm_sems(sem, "att"), attend_sems(sem, "att"), norm_sems(sem, "att_out")
    qkv_ps, qk_ready, v_ready = sem("att_qkv_ps"), sem("att_qk"), sem("att_v")
    zeroed = sem("att_zeroed")
    o_turned, oT_ready, mixed, chain = sem("att_o_turned"), sem("att_oT"), sem("att_mixed"), sem("att_chain2")
    UNITS = TILES * HEADS
    widths = [NODES] * TILES
    scale = float(np.float32(HD) ** np.float32(-0.5))
    with ExitStack() as c:
        def sb(name, shape, dt=F32):
            return c.enter_context(nc.sbuf_tensor("att_" + name, shape, dt))

        qT, kT = sb("qT", [P, HEADS, NODES]), sb("kT", [P, NODES])
        val = sb("v", [P, TILES, CH])
        shifted = sb("shifted", [P, 2, NODES])
        probs = sb("probs", [P, 2, NODES])
        probsT = sb("probsT", [P, RING, NODES])
        oT = sb("oT", [P, 2, P])
        top, ntop, total = sb("top", [P, UNITS]), sb("ntop", [P, UNITS]), sb("total", [P, UNITS])
        rtotal = sb("rtotal", [P, UNITS])
        out = sb("out", [P, TILES, CH])
        outT = sb("outT", [P, NODES])
        with nc.Block() as block:
            @block.gpsimd
            def _(pool):
                pool.memset(qT[:, :, :], 0.0).then_inc(zeroed, 1)

            @block.tensor
            def _(pe):
                turn_tensor(pe, K, K.xn, (0, 1), N.xn, N.turned)
                pe.wait_ge(N.xT, HALVES)
                for i, name in enumerate(("Wq", "Wk")):
                    for h in range(HALVES):
                        pe.matmul(K.ps[:, 2 + 2 * i + h, :], K.w(name), K.xnT[:, h * HALF:(h + 1) * HALF],
                                  start=True, stop=True).then_inc(qkv_ps, 1)
                for t in range(TILES):
                    last = pe.matmul(K.ps[:, 6 + t // 4, (t % 4) * P:(t % 4 + 1) * P], K.xnT[:, t * P:(t + 1) * P],
                                     K.w("Wv"), start=True, stop=True)
                last.then_inc(qkv_ps, 1)
                pe.wait_ge(qk_ready, 2 * HALVES)
                pe.wait_ge(v_ready, 1)
                for n in range(UNITS + 5):
                    if n < UNITS:
                        attend_scores_tensor(pe, K, A, n, qT, kT, NODES)
                    attend_tensor(pe, K, A, n, probs, probsT, oT, lambda j, h: val[:, j, h * HD:(h + 1) * HD],
                                  widths)
                turn_tensor(pe, K, out, (0, 1), A.normed, o_turned)
                for h in range(HALVES):
                    pe.wait_ge(oT_ready, h + 1)
                    for q in range(4):
                        t = 4 * h + q
                        last = pe.matmul(K.ps[:, 2 + h, q * P:(q + 1) * P], outT[:, t * P:(t + 1) * P], K.w("Wo"),
                                         start=True, stop=True)
                    last.then_inc(mixed, 1)

            @block.scalar
            def _(act):
                norm_scalar(act, K, N)
                turn_scalar(act, K, K.xnT, (0, 1), N.turned, N.xT)
                act.wait_ge(zeroed, 1)
                for h in range(HALVES):
                    act.wait_ge(qkv_ps, h + 1)
                    for head in range(HEADS):
                        rows = slice(head * HD, (head + 1) * HD)
                        last = act.activation(qT[rows, head, h * HALF:(h + 1) * HALF], K.ps[rows, 2 + h, :],
                                              ACT.Identity, bias=K.col("bq")[rows, :])
                    last.then_inc(qk_ready, 1)
                for h in range(HALVES):
                    act.wait_ge(qkv_ps, 2 + h + 1)
                    act.activation(kT[:, h * HALF:(h + 1) * HALF], K.ps[:, 4 + h, :], ACT.Identity,
                                   bias=K.col("bk")).then_inc(qk_ready, 1)
                for n in range(UNITS + 2):
                    if n < UNITS:
                        act.wait_ge(A.top, n + 1)
                        if n >= 2:
                            act.wait_ge(A.turned, HALVES * (n - 1))
                        act.activation(probs[:, n % 2, :], shifted[:, n % 2, :], ACT.Exp, bias=ntop[:, n:n + 1],
                                       scale=scale, accum_out=total[:, n:n + 1]).then_inc(A.probs, 1)
                    if 1 <= n <= UNITS:
                        attend_copy(act, lambda o, i: act.activation(o, i, ACT.Copy), K, A, n - 1, 0, probsT,
                                    NODES, widths)
                    if n >= 5 and (n - 5) % HEADS == 0:
                        attend_out_scalar(act, K, A, (n - 5) // HEADS, oT)
                turn_scalar(act, K, outT, (0, 1), o_turned, oT_ready)
                norm_scalar(act, K, N2)

            @block.vector
            def _(v):
                norm_vector(v, K, N, K.x, K.xn, LN_EPS)
                v.wait_ge(qkv_ps, 5)
                v.tensor_tensor(val[:, :, :], K.ps[:, 6:8, :].rearrange("p b (t c) -> p (b t) c", c=CH),
                                K.row("bv").unsqueeze(1).to_broadcast((P, TILES, CH)), ALU.add).then_inc(v_ready, 1)
                link = linker(v, A.chain)

                for n in range(UNITS + 5):
                    if n < UNITS:
                        t, h = n // HEADS, n % HEADS
                        v.wait_ge(A.scores, n + 1)
                        if n >= 2:
                            v.wait_ge(A.probs, n - 1)
                        b = 2 * (n % 2)
                        v.tensor_tensor_reduce(shifted[:, n % 2, :], K.ps[:, b:b + 2, :].rearrange("p b n -> p (b n)"),
                                               K.masked[:, t, :], 1.0, MASKED * 4, ALU.add, ALU.max,
                                               top[:, n:n + 1]).then_inc(A.shifted, 1)
                        v.wait_ge(A.shifted, n + 1)
                        v.tensor_scalar(ntop[:, n:n + 1], top[:, n:n + 1], -scale, None, ALU.mult).then_inc(A.top, 1)
                    if 2 <= n < UNITS + 2:
                        attend_copy(v, v.tensor_copy, K, A, n - 2, 1, probsT, NODES, widths)
                    if n >= 8 and (n - 8) % HEADS == 0:
                        t = (n - 8) // HEADS
                        attend_scale_vector(v, K, A, t, total, rtotal, out[:, t, :], link)
                link2 = linker(v, chain)
                link2(v.tensor_tensor(K.x[:, :, :], K.x[:, :, :],
                                      K.row("beta").unsqueeze(1).to_broadcast((P, TILES, CH)), ALU.add))
                for h in range(HALVES):
                    v.wait_ge(mixed, h + 1)
                    link2(v.tensor_tensor(K.xn[:, 4 * h:4 * h + 4, :],
                                          K.ps[:, 2 + h, :].rearrange("p (t c) -> p t c", t=4),
                                          K.row("bo").unsqueeze(1).to_broadcast((P, 4, CH)), ALU.add))
                count_vector(v, K, K.xn, link2)
                v.tensor_scalar(K.veps[:, :], K.mv[:, :, 1], LN_EPS, None, ALU.add).then_inc(N2.var, 1)
                for t in range(TILES):
                    last = v.scalar_tensor_tensor(out=out[:, t, :], in0=K.xn[:, t, :], scalar=K.mv[:, t, 0:1],
                                                  in1=K.row("gamma"), op0=ALU.subtract, op1=ALU.mult)
                link2(last)
                v.wait_ge(N2.std, 1)
                link2(v.reciprocal(K.rstd[:, :], K.std[:, :]))
                for t in range(TILES):
                    v.scalar_tensor_tensor(out=K.x[:, t, :], in0=out[:, t, :], scalar=K.rstd[:, t:t + 1],
                                           in1=K.x[:, t, :], op0=ALU.mult, op1=ALU.add)




def layer2_att(nc, K, sem, g):
    N, A, N2 = norm_sems(sem, "rot"), attend_sems(sem, "rot"), norm_sems(sem, "rot_rms")
    qkv_ps, rotated, v_ready, trig_in = sem("rot_qkv_ps"), sem("rot_qk"), sem("rot_v"), sem("rot_trig")
    zeroed, q_spread = sem("rot_zeroed"), sem("rot_q_spread")
    o_turned, oT_ready, mixed, chain = sem("rot_o_turned"), sem("rot_oT"), sem("rot_mixed"), sem("rot_chain2")
    rope_chain = sem("rot_rope")
    UNITS = TILES * HEADS
    widths = [(t + 1) * P for t in range(TILES)]
    scale = float(1.0 / np.sqrt(np.float32(HD)))
    with ExitStack() as c:
        def sb(name, shape, dt=F32):
            return c.enter_context(nc.sbuf_tensor("rot_" + name, shape, dt))

        q = sb("q", [P, NODES])
        qT, kT, hT = sb("qT", [P, HEADS, NODES]), sb("kT", [P, NODES]), sb("hT", [P, NODES])
        trig = sb("trig", [P, 2, NODES])
        tmp = sb("tmp", [P, 2, HALF])
        squares = sb("squares", [P, CH])
        val = sb("v", [P, TILES, 64])
        shifted = sb("shifted", [P, 2, NODES])
        probs = sb("probs", [P, 2, NODES])
        probsT = sb("probsT", [P, RING, NODES])
        oT = sb("oT", [P, 2, P])
        top, ntop, total = sb("top", [P, UNITS]), sb("ntop", [P, UNITS]), sb("total", [P, UNITS])
        rtotal = sb("rtotal", [P, UNITS])
        out = sb("out", [P, TILES, CH])
        outT = sb("outT", [P, NODES])
        with nc.Block() as block:
            @block.sync
            def _(sp):
                sp.dma_start(trig[:, :, :], K.d_trig.rearrange("p (i n) -> p i n", i=2)).then_inc(trig_in, 16)

            @block.gpsimd
            def _(pool):
                pool.memset(qT[:, :, :], 0.0).then_inc(zeroed, 1)

            @block.tensor
            def _(pe):
                turn_tensor(pe, K, out, (0, 1), N2.xn, N2.turned)
                pe.wait_ge(N2.xT, HALVES)
                for h in range(HALVES):
                    for i, name in enumerate(("wq", "wq_rot", "wk", "wk_rot")):
                        if h == 1:
                            pe.wait_ge(rotated, 1 + i // 2)
                        pe.matmul(K.ps[:, 2 + i, :], K.w(name), hT[:, h * HALF:(h + 1) * HALF],
                                  start=True, stop=True).then_inc(qkv_ps, 1)
                for t in range(TILES):
                    last = pe.matmul(K.ps[:, 6, t * 64:(t + 1) * 64], hT[:, t * P:(t + 1) * P], K.w("wv"),
                                     start=True, stop=True)
                last.then_inc(qkv_ps, 1)
                pe.wait_ge(rotated, 2 * HALVES)
                pe.wait_ge(q_spread, HALVES)
                pe.wait_ge(v_ready, 1)
                for n in range(UNITS + 5):
                    if n < UNITS:
                        attend_scores_tensor(pe, K, A, n, qT, kT, widths[n // HEADS])
                    attend_tensor(pe, K, A, n, probs, probsT, oT,
                                  lambda j, h: val[:, j, (h // 2) * HD:(h // 2 + 1) * HD], widths)
                turn_tensor(pe, K, out, (0, 1), A.normed, o_turned)
                for h in range(HALVES):
                    pe.wait_ge(oT_ready, h + 1)
                    for q in range(4):
                        t = 4 * h + q
                        last = pe.matmul(K.ps[:, 2 + h, q * P:(q + 1) * P], outT[:, t * P:(t + 1) * P], K.w("wo"),
                                         start=True, stop=True)
                    last.then_inc(mixed, 1)

            @block.scalar
            def _(act):
                norm_scalar(act, K, N)
                rms_scalar(act, K, N2, K.xn, squares[:, :], N.xn)
                turn_scalar(act, K, hT, (0, 1), N2.turned, N2.xT, scale=K.col("ln1"))
                act.wait_ge(zeroed, 1)
                for h in range(HALVES):
                    act.wait_ge(rotated, 2 * h + 1)
                    for head in range(HEADS):
                        rows, cols = slice(head * HD, (head + 1) * HD), slice(h * HALF, (h + 1) * HALF)
                        last = act.activation(qT[rows, head, cols], q[rows, cols], ACT.Copy)
                    last.then_inc(q_spread, 1)
                act.wait_ge(qkv_ps, 4 * HALVES + 1)
                act.activation(val[:, :, :], K.ps[:, 6, :].rearrange("p (t c) -> p t c", c=64), ACT.Copy
                               ).then_inc(v_ready, 1)
                for n in range(UNITS + 2):
                    if n < UNITS:
                        width = widths[n // HEADS]
                        act.wait_ge(A.top, n + 1)
                        if n >= 2:
                            act.wait_ge(A.turned, turned_count(widths, n - 2, 1))
                        act.activation(probs[:, n % 2, 0:width], shifted[:, n % 2, 0:width], ACT.Exp,
                                       bias=ntop[:, n:n + 1], scale=scale, accum_out=total[:, n:n + 1]
                                       ).then_inc(A.probs, 1)
                    if 1 <= n <= UNITS:
                        attend_copy(act, lambda o, i: act.activation(o, i, ACT.Copy), K, A, n - 1, 0, probsT,
                                    widths[(n - 1) // HEADS], widths)
                    if n >= 5 and (n - 5) % HEADS == 0:
                        attend_out_scalar(act, K, A, (n - 5) // HEADS, oT)
                turn_scalar(act, K, outT, (0, 1), o_turned, oT_ready)

            @block.vector
            def _(v):
                norm_vector(v, K, N, K.x, K.xn, LN_EPS)
                rms_vector(v, K, N2, K.xn, out, RMS_EPS)
                v.wait_ge(trig_in, 16)
                rlink = linker(v, rope_chain)
                for h in range(HALVES):
                    cols = slice(h * HALF, (h + 1) * HALF)
                    for i in range(2):
                        v.wait_ge(qkv_ps, 4 * h + 2 * i + 2)
                        v.tensor_tensor(tmp[:, 0, :], K.ps[:, 3 + 2 * i, :], trig[:, 1, cols], ALU.mult)
                        rlink(v.tensor_tensor(tmp[:, 1, :], K.ps[:, 2 + 2 * i, :], trig[:, 0, cols], ALU.mult))
                        v.tensor_tensor((q[:, cols], kT[:, cols])[i], tmp[:, 0, :], tmp[:, 1, :], ALU.add
                                        ).then_inc(rotated, 1)
                        v.wait_ge(rotated, 2 * h + i + 1)
                link = linker(v, A.chain)

                for n in range(UNITS + 5):
                    if n < UNITS:
                        t, h = n // HEADS, n % HEADS
                        width = widths[t]
                        v.wait_ge(A.scores, n + 1)
                        if n >= 2:
                            v.wait_ge(A.probs, n - 1)
                        b = 2 * (n % 2)
                        v.tensor_tensor_reduce(shifted[:, n % 2, 0:width],
                                               K.ps[:, b:b + 2, :].rearrange("p b n -> p (b n)")[:, 0:width],
                                               K.causal[:, NODES - width:NODES], 1.0, MASKED * 4, ALU.add, ALU.max,
                                               top[:, n:n + 1]).then_inc(A.shifted, 1)
                        v.wait_ge(A.shifted, n + 1)
                        v.tensor_scalar(ntop[:, n:n + 1], top[:, n:n + 1], -scale, None, ALU.mult).then_inc(A.top, 1)
                    if 2 <= n < UNITS + 2:
                        m = n - 2
                        if widths[m // HEADS] > HALF:
                            attend_copy(v, v.tensor_copy, K, A, m, 1, probsT, widths[m // HEADS], widths)
                        else:
                            v.engine_nop().then_inc(A.copied1, 1)
                    if n >= 8 and (n - 8) % HEADS == 0:
                        t = (n - 8) // HEADS
                        attend_scale_vector(v, K, A, t, total, rtotal, out[:, t, :], link)
                link2 = linker(v, chain)
                for h in range(HALVES):
                    v.wait_ge(mixed, h + 1)
                    xh = K.xn[:, 4 * h:4 * h + 4, :]
                    link2(v.tensor_tensor(xh, xh, K.ps[:, 2 + h, :].rearrange("p (t c) -> p t c", t=4), ALU.add))
                v.tensor_tensor(K.x[:, :, :], K.x[:, :, :], K.xn[:, :, :], ALU.add)




def layer2_moe(nc, K, sem, g, g_next, G):
    N, R = norm_sems(sem, "glu"), router_sems(sem, "glu")
    w_in, a_ps, b_ps, silu, hid, y_ps = (sem(f"glu_{n}") for n in ("w_in", "a_ps", "b_ps", "silu", "hid", "y_ps"))
    chain, index_chain, turned_back = sem("glu_chain"), sem("glu_index"), sem("glu_turned_back")
    pool_chain = sem("glu_pool")
    jobs = [(e, h) for e in range(L2_E) for h in range(HALVES)]
    J, C = len(jobs), len(HID_CHUNKS)
    rank_slots = range(C, J * C)
    with ExitStack() as c:
        c.enter_context(gate_memory(nc, K, "glu"))
        w = c.enter_context(nc.sbuf_tensor("glu_w", [P, 2, EXP2], F32))
        a = c.enter_context(nc.sbuf_tensor("glu_a", [P, 2, HALF], F32))
        hidden = c.enter_context(nc.sbuf_tensor("glu_hid", [P, 2, C, HALF], F32))
        rms = c.enter_context(nc.sbuf_tensor("glu_rms", [P, TILES, CH], F32))
        accT = c.enter_context(nc.sbuf_tensor("glu_accT", [P, NODES], F32))
        tmp = c.enter_context(nc.sbuf_tensor("glu_tmp", [P, HALF], F32))
        with nc.Block() as block:
            @block.sync
            def _(sp):
                next_rows_in(sp, K, G, g_next)
                next_adj_in(sp, K, G, g_next, 0)
                for e in range(L2_E):
                    if e == 2:
                        gates_out(sp, K, R)
                        gate_in(sp, K, R, 0)
                        gate_in(sp, K, R, 1)
                        next_rows_out(sp, K, G)
                    if e >= 2:
                        sp.wait_ge(y_ps, HALVES * (e - 1))
                    if e >= 1:
                        sp.wait_ge(w_in, 16 * e)
                    sp.dma_start(w[:, e % 2, :], K.d_exp2[e, :, :]).then_inc(w_in, 16)
                    if e >= 2:
                        gate_in(sp, K, R, e)

            @block.gpsimd
            def _(pool):
                pool.wait_ge(G.rows, 32)
                for t in GATHERS[0]:
                    gather_pool(pool, K, G, t)

            @block.tensor
            def _(pe):
                turn_tensor(pe, K, rms, (4, 5), N.xn, N.turned)
                pe.wait_ge(N.xT, HALVES)
                router_tensor(pe, K, R, K.w("router"), L2_E)

                def up(n, m):
                    e, h = jobs[n]
                    at, wide = HID_CHUNKS[m]
                    i = n * C + m
                    pe.wait_ge(w_in, 16 * (e + 1))
                    for off, base, done in ((0, 0, a_ps), (HID, 2, b_ps)):
                        if i >= 2:
                            pe.wait_ge(hid, i - 1)
                        pe.matmul(K.ps[0:wide, base + i % 2, :], w[:, e % 2, off + at:off + at + wide],
                                  K.xnT[:, h * HALF:(h + 1) * HALF], start=True, stop=True).then_inc(done, 1)

                def down(n):
                    e, h = jobs[n]
                    if n == 0:
                        gates_tensor(pe, K, R)
                    pe.wait_ge(hid, C * (n + 1))
                    if n >= 2:
                        pe.wait_ge(R.used, n - 1)
                    for m, (at, wide) in enumerate(HID_CHUNKS):
                        last = pe.matmul(K.ps[:, 4 + n % 2, :], w[0:wide, e % 2, 2 * HID + m * P:2 * HID + (m + 1) * P],
                                         hidden[0:wide, n % 2, m, :], start=(m == 0), stop=(m == C - 1))
                    last.then_inc(y_ps, 1)

                for n in range(J):
                    for m in range(C):
                        up(n, m)
                        if m == 1 and n >= 1:
                            down(n - 1)
                down(J - 1)
                turn_back_tensor(pe, K, accT, (0, 1), chain, (J - 1, J), turned_back)

            @block.scalar
            def _(act):
                norm_scalar(act, K, N)
                turn_scalar(act, K, K.xnT, (4, 5), N.turned, N.xT, scale=K.col("ln2"))
                router_scalar(act, K, R, L2_E, "floor")
                for n in range(J):
                    for m in range(C):
                        i = n * C + m
                        wide = HID_CHUNKS[m][1]
                        act.wait_ge(a_ps, i + 1)
                        if i >= 2:
                            act.wait_ge(hid, i - 1)
                        act.activation(a[0:wide, i % 2, :], K.ps[0:wide, i % 2, :], ACT.Silu).then_inc(silu, 1)
                        if m == 1 and n == 1:
                            gates_scalar(act, K, R)
                            next_rows_scalar(act, K, G)
                        for t, step in ranking(i - 1, rank_slots, RANKED[0]):
                            if step == 0 and t + 1 in RANKED[0]:
                                next_adj_in(act, K, G, g_next, t + 1)

            @block.vector
            def _(v):
                norm_vector(v, K, N, K.xn, rms, RMS_EPS, rms=True)
                router_vector(v, K, R, L2_E, None, "floor")
                link, ilink, glink = linker(v, chain), linker(v, index_chain), linker(v, pool_chain)
                v.memset(accT[:, :], 0.0).then_inc(R.chain, 1)

                def add(n):
                    e, h = jobs[n]
                    v.wait_ge(y_ps, n + 1)
                    v.tensor_tensor(tmp[:, :], K.ps[:, 4 + n % 2, :], gate_vector(v, K, R, e, h), ALU.mult).then_inc(R.used, 1)
                    v.wait_ge(R.used, n + 1)
                    acc = accT[:, h * HALF:(h + 1) * HALF]
                    link(v.tensor_tensor(acc, acc, tmp[:, :], ALU.add))

                for n in range(J):
                    for m in range(C):
                        i = n * C + m
                        wide = HID_CHUNKS[m][1]
                        v.wait_ge(silu, i + 1)
                        v.wait_ge(b_ps, i + 1)
                        if m == 0 and n >= 2:
                            v.wait_ge(y_ps, n - 1)
                        v.tensor_tensor(hidden[0:wide, n % 2, m, :], a[0:wide, i % 2, :], K.ps[0:wide, 2 + i % 2, :],
                                        ALU.mult).then_inc(hid, 1)
                        for t, step in ranking(i, rank_slots, RANKED[0]):
                            next_index_vector(v, K, G, t, step, ilink)
                    if n == 0:
                        next_rows_vector(v, K, G)
                    if n >= 1:
                        add(n - 1)
                    if n in (7, 11):
                        pool_max_vector(v, K, G, (n - 7) // 4, glink)
                add(J - 1)
                turn_back_vector(v, K, (0, 1), turned_back)




def layer3_gnn(nc, K, sem, g, G):
    N, A = norm_sems(sem, "gat"), attend_sems(sem, "gat")
    names = ("h_ps", "hT", "val", "src_ps", "src", "dst_w", "dst_ps", "dst", "first", "both", "pool_chain", "logit")
    S = named_sems(sem, "gat", names)
    UNITS = TILES * HEADS
    widths = [NODES] * TILES
    PAIRS = (4, 2, 0)
    KEPT = 4
    with ExitStack() as c:
        def sb(name, shape, dt=F32):
            return c.enter_context(nc.sbuf_tensor("gat_" + name, shape, dt))

        hT = K.xn[:, :, :].rearrange("p t c -> p (t c)")
        val = sb("v", [P, TILES, CH])
        dstw = sb("dstw", [P, HEADS, P])
        dst = sb("dst", [P, HEADS, NODES])
        src8 = sb("src8", [P, UNITS])
        shifted = sb("shifted", [P, 4, NODES])
        flat = sb("flat", [P, 2, NODES])
        probs = sb("probs", [P, KEPT, NODES])
        probsT = sb("probsT", [P, RING, NODES])
        oT = sb("oT", [P, 2, P])
        top, bend = sb("top", [P, UNITS]), sb("bend", [P, UNITS])
        b1, b2 = sb("b1", [P, UNITS]), sb("b2", [P, UNITS])
        total, rtotal = sb("total", [P, UNITS]), sb("rtotal", [P, UNITS])
        res = sb("res", [P, CH])
        with nc.Block() as block:
            @block.gpsimd
            def _(pool):
                for t in GATHERS[1]:
                    gather_pool(pool, K, G, t)

            @block.tensor
            def _(pe):
                turn_tensor(pe, K, K.xn, (0, 1), N.xn, N.turned)
                pe.wait_ge(N.xT, HALVES)
                for h in range(HALVES):
                    pe.matmul(K.ps[:, 2 + h, :], K.w("gatW"), K.xnT[:, h * HALF:(h + 1) * HALF],
                              start=True, stop=True).then_inc(S.h_ps, 1)
                pe.wait_ge(S.hT, HALVES)
                pe.wait_ge(S.dst_w, 1)
                for h in range(HEADS):
                    if h == 2:
                        for t in range(TILES):
                            last = pe.matmul(K.ps[:, 6, t * HEADS:(t + 1) * HEADS], hT[:, t * P:(t + 1) * P],
                                             K.col("a_src"), start=True, stop=True)
                        last.then_inc(S.src_ps, 1)
                    for q in range(HALVES):
                        n = HALVES * h + q
                        if n >= 4:
                            pe.wait_ge(S.dst, n - 3)
                        pe.matmul(K.ps[:, n % 4, :], dstw[:, h, :], hT[:, q * HALF:(q + 1) * HALF],
                                  start=True, stop=True).then_inc(S.dst_ps, 1)
                for t in range(TILES):
                    last = pe.matmul(K.ps[:, 4 + t // 4, (t % 4) * P:(t % 4 + 1) * P], K.xnT[:, t * P:(t + 1) * P],
                                     K.w("gatW"), start=True, stop=True)
                last.then_inc(S.h_ps, 1)
                pe.wait_ge(S.val, 1)
                pe.wait_ge(S.src, 1)
                for n in range(2, UNITS + 6):
                    attend_tensor(pe, K, A, n, probs, probsT, oT, lambda j, h: val[:, j, h * HD:(h + 1) * HD],
                                  widths, pairs=PAIRS, kept=KEPT, lag=7)

            @block.scalar
            def _(act):
                norm_scalar(act, K, N)
                turn_scalar(act, K, K.xnT, (0, 1), N.turned, N.xT)
                for h in range(HALVES):
                    act.wait_ge(S.h_ps, h + 1)
                    act.activation(hT[:, h * HALF:(h + 1) * HALF], K.ps[:, 2 + h, :], ACT.Identity,
                                   bias=K.col("gat_b")).then_inc(S.hT, 1)
                for n in range(HALVES * HEADS):
                    act.wait_ge(S.dst_ps, n + 1)
                    act.activation(dst[:, n // 2, (n % 2) * HALF:(n % 2 + 1) * HALF], K.ps[:, n % 4, :], ACT.Copy
                                   ).then_inc(S.dst, 1)
                for n in range(UNITS + 5):
                    if n >= 8 and (n - 8) % HEADS == 0:
                        attend_out_scalar(act, K, A, (n - 8) // HEADS, oT)
                    if 3 <= n < UNITS + 3:
                        for half in range(HALVES):
                            attend_copy(act, lambda o, i: act.activation(o, i, ACT.Copy), K, A, n - 3, half, probsT,
                                        NODES, widths, PAIRS)
                    if n < UNITS:
                        act.wait_ge(A.top, n // 2 + 1)
                        if n >= 2:
                            act.wait_ge(A.probs, n - 1)
                        if n >= KEPT:
                            act.wait_ge(A.turned, HALVES * (n - KEPT + 1))
                        act.activation(probs[:, n % KEPT, :], shifted[:, n % 4, :], ACT.Exp, bias=b1[:, n:n + 1])
                        act.activation(flat[:, n % 2, :], shifted[:, n % 4, :], ACT.Exp, bias=b2[:, n:n + 1],
                                       scale=0.2).then_inc(S.both, 1)

            @block.vector
            def _(v):
                norm_vector(v, K, N, K.x, K.xn, LN_EPS)
                for h in range(HEADS):
                    last = v.tensor_scalar(dstw[:, h, :], K.ones, K.col("a_dst")[:, h:h + 1], None, ALU.mult)
                last.then_inc(S.dst_w, 1)
                glink = linker(v, S.pool_chain)
                for t in (2, 3):
                    pool_max_vector(v, K, G, t, glink)
                link = linker(v, A.chain)

                def finish(t):
                    attend_scale_vector(v, K, A, t, total, rtotal, res[:, :], link)
                    v.wait_ge(A.normed, t + 1)
                    link(v.tensor_tensor(K.x[:, t, :], K.x[:, t, :], res[:, :], ALU.add))

                def first(p):
                    if p < 2:
                        v.wait_ge(S.dst, 2 * HALVES * (p + 1))
                    if p >= 2:
                        v.wait_ge(S.both, 2 * p - 2)
                    for n in (2 * p, 2 * p + 1):
                        v.tensor_tensor_reduce(shifted[:, n % 4, :], dst[:, n % HEADS, :], K.masked[:, n // HEADS, :],
                                               1.0, MASKED * 4, ALU.add, ALU.max, top[:, n:n + 1]
                                               ).then_inc(A.shifted, 1)
                    if p == 0:
                        v.wait_ge(S.src_ps, 1)
                        v.tensor_scalar(src8[:, :], K.ps[:, 6, 0:UNITS], 0.8, None, ALU.mult).then_inc(S.src, 1)
                        v.wait_ge(S.src, 1)
                    v.wait_ge(A.shifted, 2 * p + 2)
                    cols = slice(2 * p, 2 * p + 2)
                    link(v.scalar_tensor_tensor(out=bend[:, cols], in0=top[:, cols], scalar=-0.2, in1=src8[:, cols],
                                                op0=ALU.mult, op1=ALU.add))
                    link(v.scalar_tensor_tensor(out=b1[:, cols], in0=top[:, cols], scalar=-1.0, in1=bend[:, cols],
                                                op0=ALU.mult, op1=ALU.min))
                    v.tensor_tensor(b2[:, cols], b1[:, cols], src8[:, cols], ALU.subtract).then_inc(A.top, 1)

                first(0)
                v.wait_ge(S.h_ps, HALVES + 1)
                for b in range(HALVES):
                    last = v.tensor_tensor(val[:, 4 * b:4 * b + 4, :],
                                           K.ps[:, 4 + b, :].rearrange("p (t c) -> p t c", t=4),
                                           K.row("gat_brow").unsqueeze(1).to_broadcast((P, 4, CH)), ALU.add)
                last.then_inc(S.val, 1)
                for n in range(UNITS + 6):
                    if n < UNITS:
                        v.wait_ge(S.both, n + 1)
                        v.scalar_tensor_tensor(out=probs[:, n % KEPT, :], in0=probs[:, n % KEPT, :], scalar=1.0,
                                               in1=flat[:, n % 2, :],
                                               op0=ALU.mult, op1=ALU.max, accum_out=total[:, n:n + 1]
                                               ).then_inc(A.probs, 1)
                    if n == 0:
                        first(1)
                    if n % 2 == 1 and n + 3 < UNITS:
                        first((n + 3) // 2)
                    if n >= 9 and (n - 9) % HEADS == 0:
                        finish((n - 9) // HEADS)




def layer3_ffn(nc, K, sem, g, g_next, G):
    N, N2, R = norm_sems(sem, "gel"), norm_sems(sem, "gel_in"), router_sems(sem, "gel")
    w_in, up_ps, hid, y_ps, xe = (sem(f"gel_{n}") for n in ("w_in", "up_ps", "hid", "y_ps", "xe"))
    chain, index_chain, pool_chain, turned_back, out_ready, out_done = (sem(f"gel_{n}") for n in (
        "chain", "index", "pool", "turned_back", "out_ready", "out_done"))
    jobs = [(e, h) for e in range(L3_E) for h in range(HALVES)]
    J, C = len(jobs), L3_HID // P
    rank_slots = range(0, 7)
    with ExitStack() as c:
        c.enter_context(gate_memory(nc, K, "gel"))
        c.enter_context(ranking_memory(nc, K, "late"))
        w = c.enter_context(nc.sbuf_tensor("gel_w", [P, 2, EXP3], F32))
        hidden = c.enter_context(nc.sbuf_tensor("gel_hid", [P, 2, C, HALF], F32))
        xt2 = c.enter_context(nc.sbuf_tensor("gel_xt2", [P, TILES, CH], F32))
        x2T = c.enter_context(nc.sbuf_tensor("gel_x2T", [P, NODES], F32))
        xeT = c.enter_context(nc.sbuf_tensor("gel_xeT", [P, 2, HALF], F32))
        accT = c.enter_context(nc.sbuf_tensor("gel_accT", [P, NODES], F32))
        tmp = c.enter_context(nc.sbuf_tensor("gel_tmp", [P, HALF], F32))
        with nc.Block() as block:
            @block.sync
            def _(sp):
                next_adj_in(sp, K, G, g_next, RANKED[1][0])
                for e in range(L3_E):
                    if e >= 2:
                        sp.wait_ge(y_ps, HALVES * (e - 1))
                    if e >= 1:
                        sp.wait_ge(w_in, 16 * e)
                    sp.dma_start(w[:, e % 2, :], K.d_exp3[e, :, :]).then_inc(w_in, 16)
                    if e == 1:
                        gates_out(sp, K, R)
                        gate_in(sp, K, R, 0)
                    if e >= 1:
                        gate_in(sp, K, R, e)
                sp.wait_ge(out_ready, 1)
                sp.dma_start(K.d_out[g, :, :].rearrange("(t p) c -> p t c", p=P), K.x[:, :, :]).then_inc(out_done, 16)
                sp.wait_ge(out_done, 16)

            @block.gpsimd
            def _(pool):
                for t in GATHERS[2]:
                    gather_pool(pool, K, G, t)

            @block.tensor
            def _(pe):
                turn_tensor(pe, K, K.xn, (4, 5), N.xn, N.turned)
                pe.wait_ge(N.xT, HALVES)
                router_tensor(pe, K, R, K.w("Wr"), L3_E)
                turn_tensor(pe, K, xt2, (0, 1), N2.xn, N2.turned)

                def up(n, m):
                    e, h = jobs[n]
                    i = n * C + m
                    if m == 0:
                        pe.wait_ge(w_in, 16 * (e + 1))
                        pe.wait_ge(xe, n + 1)
                    if i >= 4:
                        pe.wait_ge(hid, i - 3)
                    pe.matmul(K.ps[:, i % 4, :], w[:, e % 2, m * P:(m + 1) * P], xeT[:, n % 2, :],
                              start=True, stop=True).then_inc(up_ps, 1)

                def down(n):
                    e, h = jobs[n]
                    if n == 0:
                        gates_tensor(pe, K, R)
                    pe.wait_ge(hid, C * (n + 1))
                    if n >= 2:
                        pe.wait_ge(R.used, n - 1)
                    for m in range(C):
                        last = pe.matmul(K.ps[:, 4 + n % 2, :], w[:, e % 2, L3_HID + m * P:L3_HID + (m + 1) * P],
                                         hidden[:, n % 2, m, :], start=(m == 0), stop=(m == C - 1))
                    last.then_inc(y_ps, 1)

                for n in range(J):
                    for m in range(C):
                        up(n, m)
                        if m == 1 and n >= 1:
                            down(n - 1)
                down(J - 1)
                turn_back_tensor(pe, K, accT, (0, 1), chain, (J - 1, J), turned_back)

            @block.scalar
            def _(act):
                norm_scalar(act, K, N)
                turn_scalar(act, K, K.xnT, (4, 5), N.turned, N.xT)
                norm_scalar(act, K, N2)
                turn_scalar(act, K, x2T, (0, 1), N2.turned, N2.xT)
                router_scalar(act, K, R, L3_E, "sum")

                def scale_in(n):
                    e, h = jobs[n]
                    if n == 0:
                        act.wait_ge(N2.xT, HALVES)
                    if n >= 2:
                        act.wait_ge(up_ps, C * (n - 1))
                    act.activation(xeT[:, n % 2, :], x2T[:, h * HALF:(h + 1) * HALF], ACT.Identity,
                                   scale=K.col("ln_g")[:, e:e + 1], bias=K.col("ln_b")[:, e:e + 1]).then_inc(xe, 1)

                scale_in(0)
                for n in range(J + 1):
                    if n + 1 < J:
                        scale_in(n + 1)
                    for m in range(C):
                        if n < J:
                            e = jobs[n][0]
                            i = n * C + m
                            act.wait_ge(up_ps, i + 1)
                            if m == 0 and n >= 2:
                                act.wait_ge(y_ps, n - 1)
                            act.activation(hidden[:, n % 2, m, :], K.ps[:, i % 4, :], ACT.Gelu,
                                           bias=K.col("b1")[:, e * C + m:e * C + m + 1]).then_inc(hid, 1)
                        if m == 1 and n == 1:
                            gates_scalar(act, K, R)
                    for t, step in ranking(n - 1, rank_slots, RANKED[1]):
                        if step == 0 and t + 1 < TILES:
                            next_adj_in(act, K, G, g_next, t + 1)

            @block.vector
            def _(v):
                norm_vector(v, K, N, K.x, K.xn, LN_EPS)
                v.wait_ge(N.xn, TILES)
                norm_vector(v, K, N2, K.xn, xt2, LN_EPS)
                router_vector(v, K, R, L3_E, K.row("br"), "sum")
                link, ilink, glink = linker(v, chain), linker(v, index_chain), linker(v, pool_chain)
                v.memset(accT[:, :], 0.0).then_inc(R.chain, 1)
                pool_max_vector(v, K, G, 4, glink)
                for n, (e, h) in enumerate(jobs):
                    v.wait_ge(y_ps, n + 1)
                    v.scalar_tensor_tensor(out=tmp[:, :], in0=K.ps[:, 4 + n % 2, :], scalar=K.col("b2")[:, e:e + 1],
                                           in1=gate_vector(v, K, R, e, h), op0=ALU.add, op1=ALU.mult).then_inc(R.used, 1)
                    v.wait_ge(R.used, n + 1)
                    acc = accT[:, h * HALF:(h + 1) * HALF]
                    link(v.tensor_tensor(acc, acc, tmp[:, :], ALU.add))
                    for t, step in ranking(n, rank_slots, RANKED[1]):
                        next_index_vector(v, K, G, t, step, ilink)
                    if n in (7, 10, 13):
                        pool_max_vector(v, K, G, 5 + (n - 7) // 3, glink)
                turn_back_vector(v, K, (0, 1), turned_back)
                v.engine_nop().then_inc(out_ready, 1)




def prologue(nc, K, sem, G):
    loaded, made = sem("loaded"), sem("made")
    chain, pool_chain = sem("start_chain"), sem("start_pool")
    with nc.Block() as block:
        @block.sync
        def _(sp):
            for dst, src in ((K.w_all, K.d_weights), (K.c_all, K.d_cols), (K.consts, K.d_consts)):
                sp.dma_start(dst[:, :], src).then_inc(loaded, 16)
            sp.dma_start(K.r_all[:, :], K.d_rowvecs.to_broadcast((P, sizes(ROWS)))).then_inc(loaded, 16)
            sp.wait_ge(made, 1)
            next_rows_in(sp, K, G, 0)
            next_rows_out(sp, K, G)
            for t in range(TILES):
                next_adj_in(sp, K, G, 0, t)

        @block.scalar
        def _(act):
            next_rows_scalar(act, K, G)

        @block.gpsimd
        def _(pool):
            for t in range(TILES):
                gather_pool(pool, K, G, t)

        @block.vector
        def _(v):
            v.memset(K.zero_row[:, :], 0.0).then_inc(made, 1)
            v.memset(K.causal[:, 0:NODES - P], 0.0)
            v.memset(K.ones_bf[:, :], 1.0)
            v.memset(K.ones32[:, :], 1.0)
            v.wait_ge(loaded, 64)
            link = linker(v, chain)
            link(v.tensor_tensor(K.causal32[:, :], K.le, K.ident, ALU.subtract))
            link(v.tensor_scalar(K.causal[:, NODES - P:NODES], K.causal32[:, :], MASKED, None, ALU.mult))
            next_rows_vector(v, K, G)
            plink = linker(v, pool_chain)
            for t in range(TILES + 1):
                if t < TILES:
                    for step in range(INDEX_STEPS):
                        next_index_vector(v, K, G, t, step, link)
                if t >= 1:
                    pool_max_vector(v, K, G, t - 1, plink)


@contextmanager
def neighbour_memory(nc, K, when):
    with nc.sbuf_tensor(f"{when}_neigh", [P, 2, NEIGH, CH], F32) as K.neigh:
        yield


@contextmanager
def ranking_memory(nc, K, when):
    with (nc.sbuf_tensor(f"{when}_adj_next", [P, NODES], I32) as K.adj_next,
          nc.sbuf_tensor(f"{when}_ranks", [P, NODES], F32) as K.ranks):
        yield


def gather_sems(sem, name):
    names = ("x_in", "norm_chain", "var", "std", "xn", "rows", "adj_in", "ranked", "indexed",
             "pooled", "gathered")
    one = [sem(f"{name}_{n}") for n in names[:-1]]
    return namedtuple("Semaphores", names)(*one, [sem(f"{name}_gathered{i}") for i in range(2)])


def program(nc, d_x, d_adj, d_weights, d_cols, d_rowvecs, d_consts, d_trig, d_exp2, d_exp3, d_out,
            graphs=GRAPHS):
    K = Memory()
    K.d_x, K.d_adj, K.d_weights, K.d_cols, K.d_rowvecs = d_x, d_adj, d_weights, d_cols, d_rowvecs
    K.d_consts, K.d_trig, K.d_exp2, K.d_exp3, K.d_out = d_consts, d_trig, d_exp2, d_exp3, d_out
    K.d_gates = nc.dram_tensor("gates", (8, NODES), F32, kind="Internal").ap()
    K.d_rows = nc.dram_tensor("normalised_rows", (NODES + 1, CH), F32, kind="Internal").ap()
    with ExitStack() as c:
        def sb(name, shape, dt=F32):
            return c.enter_context(nc.sbuf_tensor(name, shape, dt))

        K.ps = c.enter_context(nc.psum_tensor("banks", [P, 8, HALF], F32))
        K.x, K.xn, K.xnT = sb("x", [P, TILES, CH]), sb("xn", [P, TILES, CH]), sb("xnT", [P, NODES])
        K.adj, K.masked = sb("adj", [P, TILES, NODES], BF16), sb("masked", [P, TILES, NODES], BF16)
        K.w_all, K.c_all = sb("weights", [P, sizes(WEIGHTS)]), sb("cols", [P, sizes(COLS)])
        K.r_all, K.consts = sb("rowvecs", [P, sizes(ROWS)]), sb("consts", [P, sizes(CONSTS)])
        K.ones32 = sb("ones32", [P, P])
        K.ones_bf = sb("ones_bf", [P, P], BF16)
        K.causal, K.causal32 = sb("causal", [P, NODES], BF16), sb("causal32", [P, P])
        K.zero_row = sb("zero_row", [1, CH])
        K.stats, K.mv = sb("stats", [P, TILES, 6]), sb("mv", [P, TILES, 2])
        K.veps, K.std, K.rstd, K.nsq = (sb(n, [P, TILES]) for n in ("veps", "std", "rstd", "nsq"))
        K.prob, K.top, K.gate, K.gate2, K.logit = (sb(n, [P, TILES, 8]) for n in ("prob", "top", "gate", "gate2",
                                                                                 "logit"))
        K.topi, K.topf = sb("topi", [P, TILES, 8], U32), sb("topf", [P, TILES, 2])
        K.r1, K.r2, K.w1, K.w2 = (sb(n, [P, TILES]) for n in ("r1", "r2", "w1", "w2"))
        K.agg = sb("agg", [P, TILES, CH])
        K.g_stats, K.g_mv = sb("g_stats", [P, TILES, 6]), sb("g_mv", [P, TILES, 2])
        K.g_veps, K.g_std, K.g_rstd = (sb(n, [P, TILES]) for n in ("g_veps", "g_std", "g_rstd"))
        K.first, K.floor = sb("first", [P, SLOTS]), sb("floor", [P, TILES])
        K.idx, K.aggraw = sb("idx", [P, TILES, SLOTS], U32), sb("aggraw", [P, CH])

        def named(tensor, table):
            at = offsets(table)[0]
            return lambda name: tensor[:, at[name][0]:at[name][0] + at[name][1]]

        K.w, K.col, K.row = named(K.w_all, WEIGHTS), named(K.c_all, COLS), named(K.r_all, ROWS)
        const = named(K.consts, CONSTS)
        K.ident, K.le, K.gt = const("ident"), const("le"), const("gt")
        K.ones = K.ones32[:, :]

        with semaphores(nc, gathers=True) as sem, neighbour_memory(nc, K, "start"), \
                ranking_memory(nc, K, "start"), nc.sbuf_tensor("start_xg", [P, TILES, CH], F32) as K.xg:
            prologue(nc, K, sem, gather_sems(sem, "start"))
        with nc.Fori(0, graphs) as g:
            g_next = (g + 1) % graphs
            with semaphores(nc) as sem:
                layer0_gnn(nc, K, sem, g)
                layer0_ffn(nc, K, sem, g)
                layer1_gnn(nc, K, sem, g)
                layer1_ffn(nc, K, sem, g)
                layer2_gnn(nc, K, sem, g)
            with semaphores(nc, gathers=True) as sem:
                G = gather_sems(sem, "next")
                layer2_att(nc, K, sem, g)
                with neighbour_memory(nc, K, "next"):
                    with ranking_memory(nc, K, "next"), \
                            nc.sbuf_tensor("next_xg", [P, TILES, CH], F32) as K.xg:
                        layer2_moe(nc, K, sem, g, g_next, G)
                    layer3_gnn(nc, K, sem, g, G)
                    layer3_ffn(nc, K, sem, g, g_next, G)




def laid_out(i):
    f = np.float32

    def pack(table, parts, rows):
        cols = []
        for name, n in table:
            a = parts[name]
            a = a.reshape(a.shape[0], -1)
            out = np.zeros((rows, n), f)
            out[:a.shape[0]] = a
            cols.append(out)
        return np.concatenate(cols, 1)

    w_in = i["L1_ffn_W_in"]
    zx = [0, M_INNER, 2 * M_INNER, 2 * M_INNER + M_STATE, 2 * M_INNER + 2 * M_STATE, w_in.shape[1]]
    half = HD // 2

    def rotated(w):
        h = w.reshape(-1, 2, half, CH)
        return np.concatenate([h[:, 1:], h[:, :1]], 1).reshape(w.shape)

    wk = np.repeat(i["L2_ffn_wk"].reshape(2, 1, HD, CH), 2, 1).reshape(CH, CH)
    parts = {
        "l0_top": i["L0_gnn_W"][:CH], "l0_bot": i["L0_gnn_W"][CH:],
        "sW1": i["L0_ffn_sW1"], "sW2": i["L0_ffn_sW2"], "sW3": i["L0_ffn_sW3"],
        "eW1": i["L0_ffn_eW1"].transpose(1, 0, 2), "eW2": i["L0_ffn_eW2"].transpose(1, 0, 2),
        "eW3": i["L0_ffn_eW3"].transpose(1, 0, 2), "gW": i["L0_ffn_gW"],
        "msg": i["L1_gnn_W_msg"], "upd": i["L1_gnn_W_upd"],
        "W_z": w_in[:, zx[0]:zx[1]], "W_xh": w_in[:, zx[1]:zx[2]], "W_BC": w_in[:, zx[2]:zx[4]],
        "W_dt": w_in[:, zx[4]:zx[5]],
        "W_out": i["L1_ffn_W_out"].reshape(2, CH, CH).transpose(1, 0, 2), "W_lin": i["L1_ffn_W_lin"],
        "Wq": i["L2_gnn_Wq"].T, "Wk": i["L2_gnn_Wk"].T, "Wv": i["L2_gnn_Wv"].T, "Wo": i["L2_gnn_Wo"].T,
        "wq": i["L2_ffn_wq"].T, "wq_rot": rotated(i["L2_ffn_wq"]).T, "wk": wk.T, "wk_rot": rotated(wk).T,
        "wv": i["L2_ffn_wv"].T, "wo": i["L2_ffn_wo"].T, "router": i["L2_ffn_router_w"].T,
        "gatW": i["L3_gnn_W"].T, "Wr": i["L3_ffn_Wr"],
    }
    weights = pack(WEIGHTS, parts, P)

    conv_w, conv_b = i["L1_ffn_conv_w"], i["L1_ffn_conv_b"]
    a = i["L3_gnn_a"]
    a_src, a_dst = np.zeros((CH, HEADS), f), np.zeros((CH, HEADS), f)
    for h in range(HEADS):
        a_src[h * HD:(h + 1) * HD, h] = a[h, :HD]
        a_dst[h * HD:(h + 1) * HD, h] = a[h, HD:]
    one = lambda v: v.reshape(-1, 1)
    cols = pack(COLS, {
        "sb1": one(i["L0_ffn_sb1"]), "sb2": one(i["L0_ffn_sb2"]), "sb3": one(i["L0_ffn_sb3"]),
        "eb1": i["L0_ffn_eb1"].T, "eb2": i["L0_ffn_eb2"].T, "eb3": i["L0_ffn_eb3"].T, "gnn_bias": one(i["L1_gnn_bias"]),
        "conv_xh": conv_w[:M_INNER].reshape(2, CH, M_CONV).transpose(1, 0, 2),
        "conv_BC": conv_w[M_INNER:],
        "convb_xh": conv_b[:M_INNER].reshape(2, CH).T, "convb_BC": one(conv_b[M_INNER:]),
        "norm_w": i["L1_ffn_norm_w"].reshape(2, CH).T,
        "bq": one(i["L2_gnn_bq"]), "bk": one(i["L2_gnn_bk"]), "ln1": one(i["L2_ffn_ln1_w"]),
        "ln2": one(i["L2_ffn_ln2_w"]), "gat_b": one(i["L3_gnn_b"]), "a_src": a_src, "a_dst": a_dst,
        "ln_g": i["L3_ffn_ln_g"].T, "ln_b": i["L3_ffn_ln_b"].T,
        "b1": i["L3_ffn_b1"].reshape(L3_E, 4, CH).transpose(2, 0, 1), "b2": i["L3_ffn_b2"].T,
    }, P)

    row = lambda v: v.reshape(1, -1)
    rows = pack(ROWS, {
        "l0_b": row(i["L0_gnn_b"]), "gb": row(i["L0_ffn_gb"]), "dt_bias": row(i["L1_ffn_dt_bias"]),
        "A_log": row(i["L1_ffn_A_log"]), "D": row(np.repeat(i["L1_ffn_D"], M_HD)), "b_lin": row(i["L1_ffn_b_lin"]),
        "bv": row(i["L2_gnn_bv"]), "bo": row(i["L2_gnn_bo"]), "gamma": row(i["L2_gnn_gamma"]),
        "beta": row(i["L2_gnn_beta"]), "gat_brow": row(i["L3_gnn_b"]), "br": row(i["L3_ffn_br"]),
        "iota8": row(np.arange(8, dtype=f)), "rank": row(np.arange(NODES, 0, -1, dtype=f)),
    }, 1)

    k = np.arange(P)
    consts = pack(CONSTS, {"ident": np.eye(P, dtype=f), "le": (k[:, None] <= k).astype(f),
                           "gt": (k[:, None] > k).astype(f)}, P)
    inv = 1.0 / 10000.0 ** (np.arange(0, HD, 2, dtype=f) / HD)
    angle = np.outer(np.arange(NODES, dtype=f), inv)
    angle = np.concatenate([angle, angle], -1).T
    sign = np.where(np.arange(HD) < half, -1.0, 1.0).astype(f)[:, None]
    trig = np.concatenate([np.tile(np.cos(angle), (HEADS, 1)), np.tile(np.sin(angle) * sign, (HEADS, 1))], 1)
    trig = trig.astype(f)

    w2 = np.zeros((L2_E, 3 * P, CH), f)
    w2[:, :HID] = i["L2_ffn_w2"].transpose(0, 2, 1)
    exp2 = np.concatenate([i["L2_ffn_w1"].transpose(0, 2, 1), i["L2_ffn_w3"].transpose(0, 2, 1),
                           w2.reshape(L2_E, 3, P, CH).transpose(0, 2, 1, 3).reshape(L2_E, P, 3 * CH)], 2)
    exp3 = np.concatenate([i["L3_ffn_W1"],
                           i["L3_ffn_W2"].reshape(L3_E, 4, P, CH).transpose(0, 2, 1, 3).reshape(L3_E, P, 4 * CH)], 2)
    return {"x": i["x"], "adj": i["adj"], "weights": weights, "cols": cols, "rowvecs": rows, "consts": consts,
            "trig": trig, "exp2": exp2, "exp3": exp3}


def declare(nc, arrays):
    args = [nc.dram_tensor(f"in_{name}", a.shape, mybir.dt.from_np(a.dtype), kind="ExternalInput").ap()
            for name, a in arrays.items()]
    out = nc.dram_tensor("out", (GRAPHS, NODES, CH), F32, kind="ExternalOutput").ap()
    program(nc, *args, out)


def kernel(**inputs):
    import concourse.bacc as bacc
    from concourse.bass_utils import run_bass_kernel_spmd

    arrays = {n: np.ascontiguousarray(a) for n, a in laid_out({k: np.asarray(v) for k, v in inputs.items()}).items()}
    nc = bacc.Bacc("TRN2", target_bir_lowering=False, num_devices=1)
    declare(nc, arrays)
    result = run_bass_kernel_spmd(nc, [{f"in_{n}": a for n, a in arrays.items()}], core_ids=[0])
    return result.results[0]["out"]
```
